# Optimizing a Trainium2 kernel written in Bass

```python
import numpy as np
import jax
import jax.numpy as jnp

def _softmax(x, axis=-1):
    return jax.nn.softmax(x, axis=axis)

def _gelu(x):
    return jax.nn.gelu(x, approximate=True)

def _silu(x):
    return jax.nn.silu(x)

def _sigmoid(x):
    return jax.nn.sigmoid(x)

def _layernorm(x, axis=-1, eps=1e-05):
    m = jnp.mean(x, axis=axis, keepdims=True)
    v = jnp.var(x, axis=axis, keepdims=True)
    return (x - m) / jnp.sqrt(v + eps)

def _scatter_add(tgt, idx, src, axis=0):
    return tgt.at[idx].add(src)

def _segment_sum(src, seg, n):
    return jax.ops.segment_sum(src, seg, n)
kernel_name = 'mk_early_fusion_embed_d1_tok_img256_r4_3d9cda'

def setup_inputs(seed: int=0):
    np.random.seed(seed)
    _w = jnp.asarray

    def _rec_inputs():
        import jax
        import jax.numpy as jnp
        _rk = jax.random.key(seed)
        x = -0.00040386 + 0.999972 * jax.random.normal(jax.random.fold_in(_rk, 1), (8, 3, 224, 224), jnp.float32)
        x_txt = jax.random.randint(jax.random.fold_in(_rk, 51), (8, 77), 0, 14, jnp.int32)
        return (x, x_txt)
    x, x_txt = _rec_inputs()

    def _L0_tok_setup():
        import jax, jax.numpy as jnp
        import numpy as np
        EPS = 1e-05
        P = 8
        DIM = 64
        NUM_TOKENS = 64
        PATCH_DIM = 3 * P * P

        def layernorm(x, g, b):
            mu = jnp.mean(x, axis=-1, keepdims=True)
            var = jnp.mean(jnp.square(x - mu), axis=-1, keepdims=True)
            return (x - mu) * jax.lax.rsqrt(var + EPS) * g + b
        key = jax.random.key(seed)
        ks = jax.random.split(key, 8)
        b, c, h, w = (16, 3, 128, 128)
        x = jax.random.normal(ks[0], (b, c, h, w), dtype=jnp.float32)
        ln1_g = jnp.ones((PATCH_DIM,), jnp.float32)
        ln1_b = jnp.zeros((PATCH_DIM,), jnp.float32)
        W1 = jax.random.normal(ks[1], (PATCH_DIM, DIM), jnp.float32) * 0.02
        b1 = jnp.zeros((DIM,), jnp.float32)
        ln2_g = jnp.ones((DIM,), jnp.float32)
        ln2_b = jnp.zeros((DIM,), jnp.float32)
        Wp1 = jax.random.normal(ks[2], (DIM, DIM), jnp.float32) * 0.02
        bp1 = jnp.zeros((DIM,), jnp.float32)
        lnp_g = jnp.ones((DIM,), jnp.float32)
        lnp_b = jnp.zeros((DIM,), jnp.float32)
        Wp2 = jax.random.normal(ks[3], (DIM, NUM_TOKENS), jnp.float32) * 0.02
        bp2 = jnp.zeros((NUM_TOKENS,), jnp.float32)
        return {'x': x, 'ln1_g': ln1_g, 'ln1_b': ln1_b, 'W1': W1, 'b1': b1, 'ln2_g': ln2_g, 'ln2_b': ln2_b, 'Wp1': Wp1, 'bp1': bp1, 'lnp_g': lnp_g, 'lnp_b': lnp_b, 'Wp2': Wp2, 'bp2': bp2}
    _L0_tok_all = _L0_tok_setup()
    _L0_tok_in = {k: v for k, v in _L0_tok_all.items() if k in ('ln1_g', 'ln1_b', 'W1', 'b1', 'ln2_g', 'ln2_b', 'Wp1', 'bp1', 'lnp_g', 'lnp_b', 'Wp2', 'bp2')}
    del _L0_tok_all

    def _L0_txt_setup():
        import jax, jax.numpy as jnp
        import numpy as np
        _PRIME = 31
        SIZES = tuple(range(3, 21))
        TBL = 1024
        MIXED = TBL
        NUM_SIZES_P1 = len(SIZES) + 1
        B, L, D = (8, 2048, 64)

        def _ngram_ids(byte_ids):
            dna_map = jnp.full((14,), -1, dtype=jnp.int32)
            dna_map = dna_map.at[jnp.array([1, 2, 3, 4])].set(jnp.array([0, 1, 2, 3], dtype=jnp.int32))
            dna_idx = dna_map[byte_ids]
            safe = jnp.maximum(dna_idx, 0)
            bad1 = dna_idx == -1
            h = safe
            bad = bad1
            ids = []
            for k in range(2, max(SIZES) + 1):
                h = (jnp.pad(h[:, :-1], ((0, 0), (1, 0))) * _PRIME + safe) % TBL
                bad = jnp.pad(bad[:, :-1], ((0, 0), (1, 0)), constant_values=True) | bad1
                if k in SIZES:
                    ids.append(jnp.where(bad, MIXED, h))
            return ids
        key = jax.random.key(seed)
        k1, k2 = jax.random.split(key)
        byte_ids = jax.random.randint(k1, (B, L), 0, 14, dtype=jnp.int32)
        tables = jax.random.normal(k2, (len(SIZES), TBL + 1, D), dtype=jnp.float32) * 0.02
        return {'byte_ids': byte_ids, 'tables': tables}
    _L0_txt_all = _L0_txt_setup()
    _L0_txt_in = {k: v for k, v in _L0_txt_all.items() if k in ('tables',)}
    del _L0_txt_all

    def _L0_attn_setup():
        import jax, jax.numpy as jnp
        import numpy as np
        H, D = (8, 32)
        EPS = 1e-05
        key = jax.random.key(seed)
        ks = jax.random.split(key, 4)
        B, N, C = (2, 512, 64)
        inner = H * D
        return {'node_features': jax.random.normal(ks[0], (B, N, C), jnp.float32), 'ln_gamma': jnp.ones((C,), jnp.float32), 'ln_beta': jnp.zeros((C,), jnp.float32), 'W_qkv': jax.random.normal(ks[1], (3 * inner, C), jnp.float32) * 0.02, 'W_gate': jax.random.normal(ks[2], (inner, C), jnp.float32) * 0.02, 'b_gate': jnp.ones((inner,), jnp.float32), 'W_final': jax.random.normal(ks[3], (C, inner), jnp.float32) * 0.02, 'b_final': jnp.zeros((C,), jnp.float32)}
    _L0_attn_all = _L0_attn_setup()
    _L0_attn_in = {k: v for k, v in _L0_attn_all.items() if k in ('ln_gamma', 'ln_beta', 'W_qkv', 'W_gate', 'b_gate', 'W_final', 'b_final')}
    del _L0_attn_all

    def _L0_ffn_setup():
        import jax, jax.numpy as jnp
        import numpy as np
        B, S, D = (8, 1024, 64)
        H = 4 * D
        CAPACITY = 0.5
        key = jax.random.key(seed)
        ks = jax.random.split(key, 6)
        x = jax.random.normal(ks[0], (B, S, D), dtype=jnp.float32)
        attention_mask = jnp.zeros((B, 1, 1, S), dtype=jnp.float32)
        wr = jax.random.normal(ks[1], (D, 1), dtype=jnp.float32) * 0.02
        br = jnp.zeros((1,), dtype=jnp.float32)
        w1 = jax.random.normal(ks[2], (D, H), dtype=jnp.float32) * 0.02
        b1 = jnp.zeros((H,), dtype=jnp.float32)
        w2 = jax.random.normal(ks[3], (H, D), dtype=jnp.float32) * 0.02
        b2 = jnp.zeros((D,), dtype=jnp.float32)
        return {'x': x, 'attention_mask': attention_mask, 'wr': wr, 'br': br, 'w1': w1, 'b1': b1, 'w2': w2, 'b2': b2}
    _L0_ffn_all = _L0_ffn_setup()
    _L0_ffn_in = {k: v for k, v in _L0_ffn_all.items() if k in ('attention_mask', 'wr', 'br', 'w1', 'b1', 'w2', 'b2')}
    del _L0_ffn_all
    return {'x': x, 'x_txt': x_txt, 'L0_tok_ln1_g': _L0_tok_in['ln1_g'], 'L0_tok_ln1_b': _L0_tok_in['ln1_b'], 'L0_tok_W1': _L0_tok_in['W1'], 'L0_tok_b1': _L0_tok_in['b1'], 'L0_tok_ln2_g': _L0_tok_in['ln2_g'], 'L0_tok_ln2_b': _L0_tok_in['ln2_b'], 'L0_tok_Wp1': _L0_tok_in['Wp1'], 'L0_tok_bp1': _L0_tok_in['bp1'], 'L0_tok_lnp_g': _L0_tok_in['lnp_g'], 'L0_tok_lnp_b': _L0_tok_in['lnp_b'], 'L0_tok_Wp2': _L0_tok_in['Wp2'], 'L0_tok_bp2': _L0_tok_in['bp2'], 'L0_txt_tables': _L0_txt_in['tables'], 'L0_attn_ln_gamma': _L0_attn_in['ln_gamma'], 'L0_attn_ln_beta': _L0_attn_in['ln_beta'], 'L0_attn_W_qkv': _L0_attn_in['W_qkv'], 'L0_attn_W_gate': _L0_attn_in['W_gate'], 'L0_attn_b_gate': _L0_attn_in['b_gate'], 'L0_attn_W_final': _L0_attn_in['W_final'], 'L0_attn_b_final': _L0_attn_in['b_final'], 'L0_ffn_attention_mask': _L0_ffn_in['attention_mask'], 'L0_ffn_wr': _L0_ffn_in['wr'], 'L0_ffn_br': _L0_ffn_in['br'], 'L0_ffn_w1': _L0_ffn_in['w1'], 'L0_ffn_b1': _L0_ffn_in['b1'], 'L0_ffn_w2': _L0_ffn_in['w2'], 'L0_ffn_b2': _L0_ffn_in['b2']}

def reference(x, x_txt, L0_tok_ln1_g, L0_tok_ln1_b, L0_tok_W1, L0_tok_b1, L0_tok_ln2_g, L0_tok_ln2_b, L0_tok_Wp1, L0_tok_bp1, L0_tok_lnp_g, L0_tok_lnp_b, L0_tok_Wp2, L0_tok_bp2, L0_txt_tables, L0_attn_ln_gamma, L0_attn_ln_beta, L0_attn_W_qkv, L0_attn_W_gate, L0_attn_b_gate, L0_attn_W_final, L0_attn_b_final, L0_ffn_attention_mask, L0_ffn_wr, L0_ffn_br, L0_ffn_w1, L0_ffn_b1, L0_ffn_w2, L0_ffn_b2):
    import jax
    import jax.numpy as jnp

    def _L0_tok_ref(x, ln1_g, ln1_b, W1, b1, ln2_g, ln2_b, Wp1, bp1, lnp_g, lnp_b, Wp2, bp2):
        import jax, jax.numpy as jnp
        import numpy as np
        EPS = 1e-05
        P = 8
        DIM = 64
        NUM_TOKENS = 64
        PATCH_DIM = 3 * P * P

        def layernorm(x, g, b):
            mu = jnp.mean(x, axis=-1, keepdims=True)
            var = jnp.mean(jnp.square(x - mu), axis=-1, keepdims=True)
            return (x - mu) * jax.lax.rsqrt(var + EPS) * g + b
        b, c, H, W = x.shape
        hp, wp = (H // P, W // P)
        patches = x.reshape(b, c, hp, P, wp, P)
        patches = jnp.transpose(patches, (0, 2, 4, 3, 5, 1))
        patches = patches.reshape(b, hp * wp, P * P * c)
        tokens = layernorm(patches, ln1_g, ln1_b)
        tokens = tokens @ W1 + b1
        tokens = layernorm(tokens, ln2_g, ln2_b)
        q = tokens
        k = tokens
        tokens = jnp.concatenate([q, k, tokens], axis=1)
        h1 = layernorm(tokens @ Wp1 + bp1, lnp_g, lnp_b)
        h1 = jax.nn.silu(h1)
        return h1 @ Wp2 + bp2

    def _L0_txt_ref(byte_ids, tables):
        import jax, jax.numpy as jnp
        import numpy as np
        _PRIME = 31
        SIZES = tuple(range(3, 21))
        TBL = 1024
        MIXED = TBL
        NUM_SIZES_P1 = len(SIZES) + 1
        B, L, D = (8, 2048, 64)

        def _ngram_ids(byte_ids):
            dna_map = jnp.full((14,), -1, dtype=jnp.int32)
            dna_map = dna_map.at[jnp.array([1, 2, 3, 4])].set(jnp.array([0, 1, 2, 3], dtype=jnp.int32))
            dna_idx = dna_map[byte_ids]
            safe = jnp.maximum(dna_idx, 0)
            bad1 = dna_idx == -1
            h = safe
            bad = bad1
            ids = []
            for k in range(2, max(SIZES) + 1):
                h = (jnp.pad(h[:, :-1], ((0, 0), (1, 0))) * _PRIME + safe) % TBL
                bad = jnp.pad(bad[:, :-1], ((0, 0), (1, 0)), constant_values=True) | bad1
                if k in SIZES:
                    ids.append(jnp.where(bad, MIXED, h))
            return ids
        ids = _ngram_ids(byte_ids)
        total = jnp.zeros(byte_ids.shape + (tables.shape[-1],), dtype=tables.dtype)
        for t, id_n in enumerate(ids):
            total = total + tables[t][id_n]
        return total / NUM_SIZES_P1

    def _L0_attn_ref(node_features, ln_gamma, ln_beta, W_qkv, W_gate, b_gate, W_final, b_final):
        import jax, jax.numpy as jnp
        import numpy as np
        H, D = (8, 32)
        EPS = 1e-05
        x = node_features
        B, N, _ = x.shape
        mu = jnp.mean(x, axis=-1, keepdims=True)
        var = jnp.mean(jnp.square(x - mu), axis=-1, keepdims=True)
        normed = (x - mu) / jnp.sqrt(var + EPS) * ln_gamma + ln_beta
        qkv = normed @ W_qkv.T
        q, k, v = jnp.split(qkv, 3, axis=-1)

        def to_heads(t):
            return t.reshape(B, N, H, D).transpose(0, 2, 1, 3)
        q, k, v = (to_heads(q), to_heads(k), to_heads(v))
        gate = jax.nn.sigmoid(to_heads(x @ W_gate.T + b_gate))
        scores = jnp.einsum('bhid,bhjd->bhij', q, k) * D ** (-0.5)
        attn = jax.nn.softmax(scores, axis=-1)
        out = jnp.einsum('bhij,bhid->bhjd', attn, v) * gate
        out = out.transpose(0, 2, 1, 3).reshape(B, N, H * D)
        return x + out @ W_final.T + b_final

    def _L0_ffn_ref(x, attention_mask, wr, br, w1, b1, w2, b2):
        import jax, jax.numpy as jnp
        import numpy as np
        B, S, D = (8, 1024, 64)
        H = 4 * D
        CAPACITY = 0.5
        b, s, d = x.shape
        weights = (jnp.einsum('bsd,do->bso', x, wr) + br)[..., 0]
        k = max(1, int(CAPACITY * s))
        kk = k - 1 if k > 1 else 1
        _, idx = jax.lax.top_k(weights, k)
        sel_idx = idx[:, :kk]
        sel = jnp.take_along_axis(x, sel_idx[:, :, None], axis=1)
        h = jax.nn.gelu(jnp.einsum('bkd,dh->bkh', sel, w1) + b1)
        y = jnp.einsum('bkh,hd->bkd', h, w2) + b2
        w_sel = jnp.take_along_axis(weights, sel_idx, axis=1)
        y = y * w_sel[..., None]
        batch_idx = jnp.arange(b)[:, None]
        processed = jnp.zeros_like(x).at[batch_idx, sel_idx].set(y)
        return processed + x
    h = _L0_tok_ref(x, L0_tok_ln1_g, L0_tok_ln1_b, L0_tok_W1, L0_tok_b1, L0_tok_ln2_g, L0_tok_ln2_b, L0_tok_Wp1, L0_tok_bp1, L0_tok_lnp_g, L0_tok_lnp_b, L0_tok_Wp2, L0_tok_bp2)
    h = jnp.concatenate([h, _L0_txt_ref(x_txt, L0_txt_tables)], axis=1)
    h = h + _L0_attn_ref(_layernorm(h, axis=-1), L0_attn_ln_gamma, L0_attn_ln_beta, L0_attn_W_qkv, L0_attn_W_gate, L0_attn_b_gate, L0_attn_W_final, L0_attn_b_final)
    h = h + _L0_ffn_ref(_layernorm(h, axis=-1), L0_ffn_attention_mask, L0_ffn_wr, L0_ffn_br, L0_ffn_w1, L0_ffn_b1, L0_ffn_w2, L0_ffn_b2)
    return h

_drawn_inputs = setup_inputs


def setup_inputs(seed=0):
    import zlib

    import numpy as np

    out = dict(_drawn_inputs(seed))
    spreads = {'L0_tok_ln1_g': (1.0, 0.2),
     'L0_tok_ln1_b': (0.0, 0.1),
     'L0_tok_b1': (0.0, 0.1),
     'L0_tok_ln2_g': (1.0, 0.2),
     'L0_tok_ln2_b': (0.0, 0.1),
     'L0_tok_bp1': (0.0, 0.1),
     'L0_tok_lnp_g': (1.0, 0.2),
     'L0_tok_lnp_b': (0.0, 0.1),
     'L0_tok_bp2': (0.0, 0.1),
     'L0_attn_ln_gamma': (1.0, 0.6),
     'L0_attn_ln_beta': (0.0, 0.8),
     'L0_attn_b_gate': (1.0, 0.6),
     'L0_attn_b_final': (0.0, 0.1),
     'L0_ffn_b1': (0.0, 0.8),
     'L0_ffn_b2': (0.0, 0.8)}
    factors = {'L0_attn_W_gate': 8.0, 'L0_ffn_wr': 5.043, 'L0_ffn_w1': 8.0, 'L0_ffn_w2': 8.0}
    for name, (base, spread) in spreads.items():
        noise = np.random.default_rng([zlib.crc32(name.encode()), seed]).standard_normal(out[name].shape)
        drawn = base * np.exp(spread * noise) if base else spread * noise
        out[name] = jnp.asarray(drawn.astype(out[name].dtype))
    for name, factor in factors.items():
        out[name] = (out[name] * factor).astype(out[name].dtype)
    return out
```

```python
from contextlib import ExitStack

import numpy as np

import concourse.bass as bass
from concourse import mybir
from concourse.alu_op_type import AluOpType as ALU

F32 = mybir.dt.float32
BF16 = mybir.dt.bfloat16
I32 = mybir.dt.int32
ACT = mybir.ActivationFunctionType
AX = mybir.AxisListType
RMAX = bass.bass_isa.ReduceOp.max

B = 8
C, HW, PS = 3, 224, 8
GR = HW // PS
NI = GR * GR
L = 77
NU = NI + L
SEQ = 3 * NI + L
T = 7
PI, PT = NI // T, L // T
P = PI + PT
QW = GR // T
D = 64
FD = C * PS * PS
FC = FD // 2
H, DH = 8, 32
HQ = 4
INNER = H * DH
HID = 4 * D
EPS = 1e-5
SIZES = range(3, 21)
NS = len(SIZES)
TBL = 1024
PRIME = 31
SEL = int(0.5 * SEQ) - 1
KP = 96
BANK = 512
W4 = 4 * P
SLOTS = 3
STEPS = 2 * T
PARTS = [((0, 0), (0, 2)), ((0, 1), (1, 2)), ((1, 0), (2, 0)), ((1, 1), (2, 1))]


PATCH_JOBS = {2: ["A1", "A2"], 3: ["A3"], 4: ["A4"], 5: ["A5"], 6: ["A6"], 7: ["A7"], 9: ["A8", "A9"],
              10: ["q0", "k0"], 11: ["v0", "g0"]}
OWN_JOBS = {0: ["q1", "k1"], 2: ["v1", "g1"]}
FFN_JOBS = {2: ["F"], 4: ["C1"], 5: ["C2"], 6: ["C3", "C2b"], 7: ["C4"], 10: ["C5"], 11: ["C6"]}


def body_jobs(nxt, prev):
    names = []
    for s in range(STEPS):
        names += [f"s{s}.{h}" for h in range(HQ)]
        names += (FFN_JOBS.get(s, []) if prev else []) + OWN_JOBS.get(s, []) + (PATCH_JOBS.get(s, []) if nxt else [])
    return names


BODIES = {
    "prologue": ["W1", "W2", "W3", "W4", "W5", "W6", "W7"] + [j for s in sorted(PATCH_JOBS) for j in PATCH_JOBS[s]],
    "first": body_jobs(True, False),
    "steady": body_jobs(True, True),
    "last": body_jobs(False, True),
    "epilogue": [j for s in sorted(FFN_JOBS) for j in FFN_JOBS[s]],
}


def slots_of(body):
    at = [(n - len(BODIES[body])) % SLOTS for n in range(len(BODIES[body]))]
    return {name: (at[n], at[:n].count(at[n])) for n, name in enumerate(BODIES[body])}


def in_slot(body, slot):
    return sum(k == slot for k, _ in slots_of(body).values())


def uses_before(body, slot, b):
    n = 0
    if body == "prologue":
        return n
    n += in_slot("prologue", slot)
    if body == "first":
        return n
    n += in_slot("first", slot)
    if body == "steady":
        return (b - 1) * in_slot("steady", slot) + n
    n += (B - 2) * in_slot("steady", slot)
    if body == "last":
        return n
    return n + in_slot("last", slot)


def build(nc, x, x_txt, p, out):
    ctx = ExitStack()
    with ctx:
        def sb(name, shape, dt=F32):
            return ctx.enter_context(nc.sbuf_tensor(name, shape, dt))

        def sem(name):
            return ctx.enter_context(nc.semaphore(name))

        slot = [ctx.enter_context(nc.psum_tensor(f"slot{k}", [128, 2 * BANK], F32)) for k in range(SLOTS)]
        o_acc = ctx.enter_context(nc.psum_tensor("o_acc", [128, 2 * BANK], F32))

        ident = sb("ident", [128, 128])
        neg_half = sb("neg_half", [128, T])
        before = sb("before", [128, P])
        images = sb("images", [128, P])
        v_weight = sb("v_weight", [128, 1])
        zeros7 = sb("zeros7", [128, T])
        ln1_gb = sb("ln1_gb", [FC, 2, 2])
        w1_raw = sb("w1_raw", [FC, 2, D])
        w1 = sb("w1", [FC + 1, 2, D])
        col = sb("col", [128, 12])
        wp1_raw = sb("wp1_raw", [D, D])
        wp1 = sb("wp1", [KP, D])
        wp2 = sb("wp2", [KP, D])
        wqkv = sb("wqkv", [KP, 3 * INNER])
        wgate = sb("wgate", [KP, INNER])
        wfinal = sb("wfinal", [128, 2, D])
        wroute = sb("wroute", [KP, P])
        wh = sb("wh", [KP, HID])
        wy = sb("wy", [128, 2, D])
        bf_rep = sb("bf_rep", [128, D])
        b2_rep = sb("b2_rep", [128, D])
        row = sb("row", [1, 2 * D])
        tok_raw = sb("tok_raw", [B, L], I32)
        tokf = sb("tokf", [B, L])
        ok = sb("ok", [B, L])
        ok2 = sb("ok2", [B, L])
        safe = sb("safe", [B, L])
        bad1 = sb("bad1", [B, L])
        hash_f = sb("hash_f", [B, 2, L])
        hash_i = sb("hash_i", [B, 2, L], I32)
        bad = sb("bad", [B, 2, L])
        ids = sb("ids", [L, NS, B], I32)
        ids_now = sb("ids_now", [L, NS], I32)
        rows_flat = sb("rows_flat", [128, NS * D])
        rows = rows_flat[0:L, :].rearrange("p (n d) -> p n d", n=NS)
        text = sb("text", [L, D])
        patches = sb("patches", [PI, C, PS, T * PS])
        pn_flat = sb("pn_flat", [128, T * FD])
        pn = pn_flat[0:PI, :].rearrange("p (t f) -> p t f", t=T)
        st = {k: sb(f"st_{k}", [128, T, 6]) for k in ("p", "x", "y", "u", "n", "w")}
        mv = {k: sb(f"mv_{k}", [128, T, 2]) for k in ("p", "x", "y", "u", "n", "w")}
        ve = {k: sb(f"ve_{k}", [128, T]) for k in ("p", "x", "y", "u", "n", "w")}
        rstd = {k: sb(f"rstd_{k}", [128, T]) for k in ("p", "x", "y", "u", "n", "w")}
        pnT = sb("pnT", [FC + 1, 2, NI])
        x2 = sb("x2", [P, T, D])
        x2T = sb("x2T", [KP, NI])
        y2 = x2
        zT = sb("zT", [D, NI])
        x3T = x2T
        h_all = sb("h_all", [P, B, T, D])
        u = sb("u", [P, T, D])
        n2 = x2
        uT = sb("uT", [KP, NU])
        nT = sb("nT", [KP, NU])
        qparts = sb("qparts", [128, 3, NU], BF16)
        kparts = sb("kparts", [128, 3, NU], BF16)
        rest = {k: sb(f"rest_{k}", [128, NU]) for k in "qk"}
        qs = [sb(f"qs{g}", [128, HQ, 2, NU], BF16) for g in range(2)]
        ks = [sb(f"ks{g}", [128, HQ, 2, NU], BF16) for g in range(2)]
        v = [sb(f"v{g}", [P, T, HQ * DH]) for g in range(2)]
        gate = [sb(f"gate{g}", [128, NU]) for g in range(2)]
        e_flat = sb("e_flat", [128, 2 * HQ * NU])
        e = e_flat[0:P, :].rearrange("p (r h t q) -> p r h t q", r=2, h=HQ, t=T)
        raw_qkv = e_flat[:, 0:6 * D].rearrange("p (k n) -> p k n", k=6)
        raw_gate = e_flat[:, 6 * D:8 * D].rearrange("p (k n) -> p k n", k=2)
        raw_final = e_flat[0:D, 8 * D:8 * D + INNER]
        qkv_t = e_flat[0:D, 1024:1024 + 3 * INNER]
        ids_f = e_flat[0:B, 2048:2048 + NS * L].rearrange("p (n l) -> p n l", n=NS)
        negmax = sb("negmax", [P, 2, HQ])
        s_all = sb("s_all", [P, 2, HQ])
        s_txt = sb("s_txt", [P, 2, HQ])
        den = sb("den", [P, 2, HQ])
        rden = sb("rden", [P, 2, HQ])
        vs = sb("vs", [P, 2, HQ, DH])
        og = [sb("og0", [128, NU]), gate[1]]
        h2 = sb("h2", [P, T, D])
        w = sb("w", [P, T, D])
        wT = sb("wT", [KP, NU])
        base = sb("base", [P, T, D])
        route = sb("route", [P, NU])
        w_tok = sb("w_tok", [P, T])
        cmp = sb("cmp", [P, NU], BF16)
        cnt_all = sb("cnt_all", [P, T])
        cnt_txt = sb("cnt_txt", [P, T])
        c3 = sb("c3", [P, T])
        above_cnt = sb("above_cnt", [P, T])
        cand = sb("cand", [P, T])
        edge = sb("edge", [P, 2])
        above = sb("above", [P, T])
        tied = sb("tied", [P, T])
        tied_sum = sb("tied_sum", [P, 1])
        tie_no = sb("tie_no", [P, T])
        ties = sb("ties", [P, 2])
        limit = sb("limit", [P, 3])
        take = sb("take", [P, 3, T])
        hz = [rest[k] for k in "qk"]
        hT = [pn_flat[:, 0:NU], rows_flat[:, 0:NU]]
        ys = sb("ys", [P, T, D])
        o_c = [sb(f"o_c{c}", [P, T, D]) for c in range(3)]

        filled = [sem(f"slot{k}_filled") for k in range(SLOTS)]
        drained = [sem(f"slot{k}_drained") for k in range(SLOTS)]
        weights_in = sem("weights_in")
        text_in = sem("text_in")
        consts_ready = sem("consts_ready")
        settled = sem("settled")
        ids_f_ready = sem("ids_f_ready")
        ids_now_ready = sem("ids_now_ready")
        rows_in = sem("rows_in")
        text_ready = sem("text_ready")
        text_placed = sem("text_placed")
        patches_in = sem("patches_in")
        patches_normed = sem("patches_normed")
        var_ready = {k: sem(f"var_ready_{k}") for k in mv}
        rstd_ready = {k: sem(f"rstd_ready_{k}") for k in mv}
        silu_in_ready = sem("silu_in_ready")
        silu_ready = sem("silu_ready")
        u_ready = sem("u_ready")
        n_ready = sem("n_ready")
        hub_ready = sem("hub_ready")
        q_top_ready = sem("q_top_ready")
        k_top_ready = sem("k_top_ready")
        q_mid_ready = sem("q_mid_ready")
        k_mid_ready = sem("k_mid_ready")
        q_parts_ready = sem("q_parts_ready")
        k_parts_ready = sem("k_parts_ready")
        q_placed = sem("q_placed")
        k_placed = sem("k_placed")
        negmax_ready = sem("negmax_ready")
        vs_ready = sem("vs_ready")
        av_done = sem("av_done")
        o_drained = sem("o_drained")
        w_ready = sem("w_ready")
        base_ready = sem("base_ready")
        gelu_arg_ready = sem("gelu_arg_ready")
        gelu_tanh_ready = sem("gelu_tanh_ready")
        gelu_ready = sem("gelu_ready")
        cand_ready = sem("cand_ready")
        edge_ready = sem("edge_ready")
        tied_ready = sem("tied_ready")
        take_ready = sem("take_ready")
        out_ready = sem("out_ready")
        stored = sem("stored")

        def wait(eng, s, value):
            if not (isinstance(value, int) and value <= 0):
                eng.wait_ge(s, value)

        def settle(eng):
            eng.sem_inc(settled)

        class Job:

            def __init__(self, body, name, b):
                self.k, turn = slots_of(body)[name]
                self.n = uses_before(body, self.k, b) + turn
                self.tile = slot[self.k]

            def wait_free(self, pe):
                wait(pe, drained[self.k], self.n)

            def wait_filled(self, eng):
                eng.wait_ge(filled[self.k], self.n + 1)

            def wait_drained(self, eng):
                eng.wait_ge(drained[self.k], self.n + 1)

            def fill(self, ins):
                ins.then_inc(filled[self.k], 1)

            def drain(self, ins):
                ins.then_inc(drained[self.k], 1)

        class Chain:

            def __init__(self, eng, name):
                self.eng, self.sem, self.n = eng, sem(name), 0

            def __call__(self, ins):
                ins.then_inc(self.sem, 1)
                self.n += 1

            def sync(self):
                if self.n:
                    self.eng.wait_ge(self.sem, self.n)

            def restart(self):
                if self.n:
                    self.eng.wait_ge(self.sem, self.n)
                    self.eng.sem_clear(self.sem)
                    self.n = 0

        def run(eng, iteration, prologue, epilogue):
            prologue()
            iteration("first", 0, True, False)
            with eng.Fori(1, B - 1) as b:
                iteration("steady", b, True, True)
            iteration("last", B - 1, False, True)
            epilogue("epilogue", B - 1)

        def pieces(n):
            return [(a, min(n, a + BANK)) for a in range(0, n, BANK)]

        def tile_col(t, parts):
            return (t // 4) * BANK + (t % 4) * parts

        def fold(eng_do, dst, tile, rows_, parts):
            eng_do(dst[:, 0:4 * parts], tile[0:rows_, 0:4 * parts])
            return eng_do(dst[:, 4 * parts:T * parts], tile[0:rows_, BANK:BANK + (T - 4) * parts])

        NW = 27
        block = ctx.enter_context(nc.Block())

        @block.sync
        def _(sp):
            def load(dst, src, s, elements=False):
                sp.dma_start(dst, src, allow_slow_non_contiguous=elements).then_inc(s, 16)

            def load_patches(b):
                for q in range(QW):
                    for c in range(C):
                        load(patches[q:PI:QW, c, :, :],
                             x[b, c].rearrange("(r y) (q w) -> q r y w", y=PS, q=QW)[q], patches_in)

            load(tok_raw[:, :], x_txt, text_in)
            load_patches(0)
            count = [0]

            def load_w(dst, src, elements=False):
                count[0] += 1
                load(dst, src, weights_in, elements)

            one = lambda a: a.rearrange("(a n) -> a n", a=1)
            column = lambda a: a.rearrange("(n a) -> n a", a=1)
            w1_d = p["L0_tok_W1"].rearrange("(f c) n -> c f n", c=C)
            for src, dst in ((w1_d, lambda a, b_, k: w1_raw[a:b_, k, :]),
                             (p["L0_tok_ln1_g"].rearrange("(f c o) -> c f o", c=C, o=1), lambda a, b_, k: ln1_gb[a:b_, k, 0:1]),
                             (p["L0_tok_ln1_b"].rearrange("(f c o) -> c f o", c=C, o=1), lambda a, b_, k: ln1_gb[a:b_, k, 1:2])):
                half = PS * PS // 2
                few = src is not w1_d
                load_w(dst(0, 2 * half, 0), src[0], few)
                load_w(dst(2 * half, 3 * half, 0), src[1, 0:half], few)
                load_w(dst(0, half, 1), src[1, half:2 * half], few)
                load_w(dst(half, 3 * half, 1), src[2], few)
            load_w(raw_qkv[:, :, :], p["L0_attn_W_qkv"].rearrange("(k r) n -> r k n", r=128))
            load_w(raw_gate[:, :, :], p["L0_attn_W_gate"].rearrange("(k r) n -> r k n", r=128))
            load_w(raw_final[:, :], p["L0_attn_W_final"])
            load_w(wp1_raw[:, :], p["L0_tok_Wp1"])
            for n, name in enumerate(("L0_tok_ln2_g", "L0_tok_ln2_b", "L0_tok_lnp_g", "L0_tok_lnp_b",
                                      "L0_attn_ln_gamma", "L0_attn_ln_beta")):
                load_w(col[0:D, n:n + 1], column(p[name]), True)
            load_w(row[0:1, 0:D], one(p["L0_tok_b1"]))
            load_w(row[0:1, D:2 * D], one(p["L0_tok_bp1"]))
            load_w(wy[:, :, :], p["L0_ffn_w2"].rearrange("(k r) n -> r k n", r=128))
            load_w(bf_rep[0:P, :], one(p["L0_attn_b_final"]).to_broadcast([P, D]))
            load_w(b2_rep[0:P, :], one(p["L0_ffn_b2"]).to_broadcast([P, D]))
            assert count[0] == NW, count
            sp.wait_ge(consts_ready, 1)
            load_w(wp2[0:D, :], p["L0_tok_Wp2"])
            load_w(wp2[D:D + 1, :], one(p["L0_tok_bp2"]))
            load_w(wgate[D:D + 1, :], one(p["L0_attn_b_gate"]))
            load_w(col[0:D, 7:8], p["L0_ffn_wr"], True)
            load_w(col[D:D + 1, 7:8], one(p["L0_ffn_br"]), True)
            load_w(wh[0:D, :], p["L0_ffn_w1"])
            load_w(wh[D:D + 1, :], one(p["L0_ffn_b1"]))
            assert count[0] == NW + 7

            def place(parts, dst, side, s):
                for h in range(HQ):
                    for r, passes in enumerate(PARTS):
                        i, j = passes[0][side], passes[1][side]
                        src = parts[DH * h:DH * h + DH, i:j + 1:max(j - i, 1), :] if j > i else \
                            parts[DH * h:DH * h + DH, i:i + 1, :].to_broadcast([DH, 2, NU])
                        load(dst[DH * r:DH * r + DH, h, :, :], src, s)

            def place_quad(b, g, turn):
                sp.wait_ge(q_parts_ready, turn + 1)
                place(qparts, qs[g], 0, q_placed)
                sp.wait_ge(k_parts_ready, turn + 1)
                place(kparts, ks[g], 1, k_placed)

            def place_text(b):
                sp.wait_ge(text_ready, b + 1)
                for t in range(T):
                    load(h_all[PI:P, b, t, :], text[t:L:T, :], text_placed)

            def store(b):
                for c in range(3):
                    sp.wait_ge(out_ready, 3 * b + c + 1)
                    n = P if c == 2 else PI
                    load(out[b, c * NI:c * NI + n * T, :].rearrange("(p t) d -> p t d", t=T), o_c[c][0:n, :, :], stored)

            def prologue():
                sp.wait_ge(patches_normed, 1)
                load_patches(1)
                place_text(0)
                place_quad(0, 0, 0)

            def iteration(body, b, nxt, prev):
                place_quad(b, 1, 2 * b + 1)
                if nxt:
                    sp.wait_ge(patches_normed, b + 2)
                    load_patches((b + 2) % B)
                    place_text(b + 1)
                    place_quad(b + 1, 0, 2 * b + 2)
                if prev:
                    store(b - 1)

            def epilogue(body, b):
                store(b)
                sp.wait_ge(stored, 16 * 3 * B)
                sp.wait_ge(patches_in, 16 * QW * C * (B + 1))

            run(sp, iteration, prologue, epilogue)

        @block.gpsimd
        def _(pool):
            chain = Chain(pool, "pool_chain")

            def step(ins):
                chain(ins)
                chain.sync()

            for tile in (wp1, wp2, wqkv, wgate, wroute, wh, x2T, uT, nT, wT):
                step(pool.memset(tile[D:KP, :], 0.0))
            step(pool.memset(ident[:, :], 0.0))
            step(pool.memset(before[:, :], 1.0))
            step(pool.memset(images[:, :], 1.0))
            step(pool.memset(v_weight[:, :], 1.5))
            step(pool.memset(neg_half[:, :], -0.5))
            step(pool.memset(pnT[FC:FC + 1, 1, :], 1.0))
            step(pool.memset(zeros7[:, :], 0.0))
            step(pool.memset(bad[:, :, :], 1.0))
            step(pool.memset(hash_f[:, :, :], 0.0))
            step(pool.memset(hash_i[:, :, :], 0))
            for tile in (x2T, uT, nT, wT):
                step(pool.memset(tile[D:D + 1, :], 1.0))
            step(pool.affine_select(out=ident[:, :], in_=ident[:, :], compare_op=ALU.not_equal, fill=1.0,
                                     base=0, pattern=[[-1, 128]], channel_multiplier=1))
            step(pool.affine_select(out=before[:, :], in_=before[:, :], compare_op=ALU.is_gt, fill=0.0,
                                     base=0, pattern=[[1, P]], channel_multiplier=-1))
            step(pool.affine_select(out=images[:, :], in_=images[:, :], compare_op=ALU.is_gt, fill=0.0,
                                     base=PI, pattern=[[0, P]], channel_multiplier=-1))
            step(pool.affine_select(out=v_weight[:, :], in_=v_weight[:, :], compare_op=ALU.is_gt, fill=0.5,
                                     base=PI, pattern=[[0, 1]], channel_multiplier=-1))
            pool.memset(ys[:, :, :], 0.0).then_inc(consts_ready, 1)
            pool.wait_ge(consts_ready, 1)

            def gather(b):
                pool.wait_ge(ids_now_ready, b + 1)
                settle(pool)
                for n in range(NS):
                    pool.indirect_dma_start(
                        out=rows[:, n, :], out_offset=None,
                        in_=p["L0_txt_tables"].rearrange("n r d -> (n r) d"),
                        in_offset=bass.IndirectOffsetOnAxis(ap=ids_now[:, n:n + 1], axis=0)).then_inc(rows_in, 16)

            def finish_rstd(k, b, parts):
                pool.wait_ge(var_ready[k], b + 1)
                settle(pool)
                chain(pool.tensor_scalar(ve[k][0:parts, :], mv[k][0:parts, :, 1], EPS, None, ALU.add))
                chain.sync()
                pool.tensor_tensor(rstd[k][0:parts, :], ve[k][0:parts, :], neg_half[0:parts, :], ALU.pow)\
                    .then_inc(rstd_ready[k], 1)

            def make_hub(b):
                pool.wait_ge(u_ready, b + 1)
                chain(pool.tensor_tensor(h_all[:, b, :, :], h_all[:, b, :, :], u[:, :, :], ALU.add))
                chain.sync()
                pool.tensor_tensor(h_all[:, b, :, :], h_all[:, b, :, :],
                                   bf_rep[0:P, :].unsqueeze(1).to_broadcast([P, T, D]), ALU.add).then_inc(hub_ready, 1)

            def low_part(parts, k, mid_ready, parts_ready, turn):
                pool.wait_ge(mid_ready, turn + 1)
                pool.tensor_tensor(parts[:, 2, :], rest[k][:, :], parts[:, 1, :], ALU.subtract).then_inc(parts_ready, 1)

            def low_parts(turn):
                low_part(qparts, "q", q_mid_ready, q_parts_ready, turn)
                low_part(kparts, "k", k_mid_ready, k_parts_ready, turn)

            def make_base(b):
                pool.wait_ge(w_ready, b + 1)
                wait(pool, out_ready, 3 * b)
                pool.tensor_tensor(base[:, :, :], h2[:, :, :], w[:, :, :], ALU.add).then_inc(base_ready, 1)

            def gelu_arg(body, c, g):
                Job(body, f"C{3 + g}", c).wait_drained(pool)
                chain(pool.tensor_tensor(hT[g][:, :], hz[g][:, :], hz[g][:, :], ALU.mult))
                chain.sync()
                chain(pool.tensor_scalar(hT[g][:, :], hT[g][:, :], 0.044715, 1.0, ALU.mult, ALU.add))
                chain.sync()
                pool.tensor_tensor(hT[g][:, :], hT[g][:, :], hz[g][:, :], ALU.mult).then_inc(gelu_arg_ready, 1)

            def find_edge(b):
                pool.wait_ge(cand_ready, b + 1)
                settle(pool)
                pool.partition_all_reduce(edge[:, 1:2], edge[:, 0:1], P, RMAX).then_inc(edge_ready, 1)

            def finish(body, c, b):
                pool.wait_ge(take_ready, b + 1)
                Job(body, "C5", c).wait_drained(pool)
                wait(pool, stored, 48 * b)
                for k in range(3):
                    if k:
                        pool.wait_ge(out_ready, 3 * b + k)
                    else:
                        wait(pool, out_ready, 3 * b)
                    chain(pool.tensor_tensor(o_c[k][:, :, :], ys[:, :, :],
                                             take[:, k, :].unsqueeze(2).to_broadcast([P, T, D]), ALU.mult))
                    chain.sync()
                    pool.tensor_tensor(o_c[k][:, :, :], o_c[k][:, :, :], base[:, :, :], ALU.add).then_inc(out_ready, 1)

            def prologue():
                finish_rstd("p", 0, PI)
                gather(0)
                finish_rstd("x", 0, PI)
                finish_rstd("y", 0, PI)
                finish_rstd("u", 0, P)
                finish_rstd("n", 0, P)
                make_hub(0)
                low_parts(0)

            def iteration(body, b, nxt, prev):
                chain.restart()
                low_parts(2 * b + 1)
                if nxt:
                    gather(b + 1)
                    finish_rstd("p", b + 1, PI)
                if prev:
                    finish_rstd("w", b - 1, P)
                if nxt:
                    finish_rstd("x", b + 1, PI)
                if prev:
                    make_base(b - 1)
                if nxt:
                    finish_rstd("y", b + 1, PI)
                if prev:
                    gelu_arg(body, b, 0)
                    gelu_arg(body, b, 1)
                if nxt:
                    finish_rstd("u", b + 1, P)
                    finish_rstd("n", b + 1, P)
                if prev:
                    find_edge(b - 1)
                if nxt:
                    make_hub(b + 1)
                    low_parts(2 * b + 2)
                if prev:
                    finish(body, b, b - 1)
                chain.restart()

            def epilogue(body, b):
                finish_rstd("w", b, P)
                make_base(b)
                gelu_arg(body, b, 0)
                gelu_arg(body, b, 1)
                find_edge(b)
                finish(body, b, b)

            run(pool, iteration, prologue, epilogue)

        @block.scalar
        def _(act):
            chain = Chain(act, "act_chain")

            def copy(dst, src, **kw):
                return act.activation(dst, src, ACT.Copy, **kw)

            def evict(body, name, b, dst, rows_, parts):
                j = Job(body, name, b)
                j.wait_filled(act)
                j.drain(fold(copy, dst, j.tile, rows_, parts))

            def prepare_weights():
                act.wait_ge(consts_ready, 1)
                act.wait_ge(weights_in, 16 * (NW + 7))
                for k in range(2):
                    chain(act.activation(w1[0:FC, k, :], w1_raw[:, k, :], ACT.Copy, scale=ln1_gb[:, k, 0:1]))
                chain(act.activation(wp1[0:D, :], wp1_raw[:, :], ACT.Copy, scale=col[0:D, 0:1]))
                chain(act.activation(wp2[0:D, :], wp2[0:D, :], ACT.Copy, scale=0.5))
                chain(act.activation(wy[:, :, :], wy[:, :, :], ACT.Copy, scale=0.5))
                chain(copy(wroute[0:D + 1, :], col[0:D + 1, 7:8].to_broadcast([D + 1, P])))
                j = Job("prologue", "W1", 0)
                j.wait_filled(act)
                chain(copy(qkv_t[:, :], j.tile[0:D, 0:3 * INNER]))
                chain.sync()
                chain(act.activation(col[0:D, 6:7], col[0:D, 4:5], ACT.Copy, scale=float(DH) ** -0.5))
                chain.sync()
                chain(act.activation(wqkv[0:D, 0:INNER], qkv_t[:, 0:INNER], ACT.Copy, scale=col[0:D, 6:7]))
                j.drain(act.activation(wqkv[0:D, INNER:3 * INNER], qkv_t[:, INNER:3 * INNER], ACT.Copy,
                                       scale=col[0:D, 4:5]))
                j = Job("prologue", "W2", 0)
                j.wait_filled(act)
                j.drain(copy(wgate[0:D, :], j.tile[0:D, 0:INNER]))
                j = Job("prologue", "W3", 0)
                j.wait_filled(act)
                j.drain(act.activation(wfinal[:, :, :], j.tile[:, 0:2 * D].rearrange("p (k n) -> p k n", k=2),
                                       ACT.Copy, scale=0.5))
                j = Job("prologue", "W4", 0)
                j.wait_filled(act)
                chain(act.activation(wqkv[D:D + 1, 0:INNER], j.tile[0:1, 0:INNER], ACT.Copy,
                                     scale=float(DH) ** -0.5))
                j.drain(copy(wqkv[D:D + 1, INNER:3 * INNER], j.tile[0:1, INNER:3 * INNER]))
                j = Job("prologue", "W7", 0)
                j.wait_filled(act)
                j.drain(copy(ids[:, :, :], j.tile[0:L, 0:NS * B].rearrange("p (n b) -> p n b", n=NS)))

            def evict_patches(body, b):
                for k, name in enumerate(("A1", "A2")):
                    evict(body, name, b, pnT[0:FC, k, :], FC, PI)

            def silu(body, b):
                j = Job(body, "A6", b)
                j.wait_filled(act)
                j.drain(fold(lambda o, i: act.activation(o, i, ACT.Identity, scale=col[0:D, 2:3], bias=col[0:D, 3:4]),
                             zT[:, :], j.tile, D, PI))
                j.wait_drained(act)
                act.activation(x3T[0:D, :], zT[:, :], ACT.Tanh, scale=0.5).then_inc(silu_in_ready, 1)

            def evict_tokens(body, b, dst_b):
                j = Job(body, "A7", b)
                j.wait_filled(act)
                j.drain(copy(h_all[0:PI, dst_b, :, :], j.tile[0:PI, 0:T * D].rearrange("p (t d) -> p t d", t=T)))

            def top_parts(body, b, g, turn):
                for name, parts, placed, ready in ((f"q{g}", qparts, q_placed, q_top_ready),
                                                   (f"k{g}", kparts, k_placed, k_top_ready)):
                    j = Job(body, name, b)
                    j.wait_filled(act)
                    wait(act, placed, 16 * HQ * len(PARTS) * turn)
                    copy(parts[:, 0, :], j.tile[:, 0:NU]).then_inc(ready, 1)

            def evict_values(body, b, g):
                j = Job(body, f"v{g}", b)
                j.wait_filled(act)
                j.drain(act.activation(v[g][:, :, :], j.tile[0:P, 0:T * HQ * DH].rearrange("p (t n) -> p t n", t=T),
                                       ACT.Copy, scale=v_weight[0:P, :]))

            def gates(body, b, g):
                j = Job(body, f"g{g}", b)
                j.wait_filled(act)
                j.drain(act.activation(gate[g][:, :], j.tile[:, 0:NU], ACT.Tanh, scale=0.5))

            def exps(body, b, s):
                for h in range(HQ):
                    j = Job(body, f"s{s}.{h}", b)
                    act.wait_ge(negmax_ready, (b * STEPS + s) * HQ + h + 1)
                    j.drain(act.activation(e[:, s % 2, h, :, :], j.tile[0:P, 0:NU].rearrange("p (t q) -> p t q", t=T),
                                           ACT.Exp, bias=negmax[:, s % 2, h:h + 1], accum_out=s_all[:, s % 2, h:h + 1]))

            def gelu_z(body, c, g, turn):
                j = Job(body, f"C{3 + g}", c)
                j.wait_filled(act)
                act.wait_ge((q_parts_ready, k_parts_ready)[g], turn)
                j.drain(copy(hz[g][:, :], j.tile[:, 0:NU]))

            def gelu_tanh(b, g):
                act.wait_ge(gelu_arg_ready, 2 * b + g + 1)
                act.activation(hT[g][:, :], hT[g][:, :], ACT.Tanh, scale=0.7978845608028654).then_inc(gelu_tanh_ready, 1)

            def evict_route(body, c, b):
                j = Job(body, "C2", c)
                j.wait_filled(act)
                wait(act, cand_ready, b)
                j.drain(copy(route[:, :], j.tile[0:P, 0:NU]))

            def prologue():
                prepare_weights()
                evict_patches("prologue", 0)
                evict("prologue", "A4", 0, x2T[0:D, :], D, PI)
                silu("prologue", 0)
                evict_tokens("prologue", 0, 0)
                evict("prologue", "A8", 0, uT[0:D, :], D, P)
                evict("prologue", "A9", 0, nT[0:D, :], D, P)
                top_parts("prologue", 0, 0, 0)
                evict_values("prologue", 0, 0)
                gates("prologue", 0, 0)

            def iteration(body, b, nxt, prev):
                chain.restart()
                for s in range(STEPS):
                    exps(body, b, s)
                    if s == 0:
                        top_parts(body, b, 1, 2 * b + 1)
                    if s == 2:
                        evict_values(body, b, 1)
                        gates(body, b, 1)
                    if prev:
                        if s == 4:
                            evict(body, "C1", b, wT[0:D, :], D, P)
                        if s == 5:
                            evict_route(body, b, b - 1)
                        if s == 6:
                            gelu_z(body, b, 0, 2 * b + 2)
                        if s == 7:
                            gelu_z(body, b, 1, 2 * b + 2)
                        if s == 8:
                            gelu_tanh(b - 1, 0)
                            gelu_tanh(b - 1, 1)
                    if nxt:
                        if s == 2:
                            evict_patches(body, b)
                        if s == 4:
                            evict(body, "A4", b, x2T[0:D, :], D, PI)
                        if s == 6:
                            silu(body, b)
                        if s == 7:
                            evict_tokens(body, b, b + 1)
                        if s == 9:
                            evict(body, "A8", b, uT[0:D, :], D, P)
                            evict(body, "A9", b, nT[0:D, :], D, P)
                        if s == 10:
                            top_parts(body, b, 0, 2 * b + 2)
                        if s == 11:
                            evict_values(body, b, 0)
                            gates(body, b, 0)
                chain.restart()

            def epilogue(body, b):
                evict(body, "C1", b, wT[0:D, :], D, P)
                evict_route(body, b, b)
                gelu_z(body, b, 0, 2 * b + 2)
                gelu_z(body, b, 1, 2 * b + 2)
                gelu_tanh(b, 0)
                gelu_tanh(b, 1)

            run(act, iteration, prologue, epilogue)

        @block.vector
        def _(dve):
            chain = Chain(dve, "dve_chain")

            def stats(k, b, src, parts):
                for t in range(T):
                    chain(dve.bn_stats(st[k][0:parts, t, :], src(t)))
                chain.sync()
                for t in range(T):
                    ins = dve.bn_aggr(mv[k][0:parts, t, :], st[k][0:parts, t, :])
                    if t < T - 1:
                        chain(ins)
                ins.then_inc(var_ready[k], 1)

            def normalize(k, b, dst, src, parts):
                dve.wait_ge(rstd_ready[k], b + 1)
                for t in range(T):
                    ins = dve.tensor_scalar(dst(t), src(t), mv[k][0:parts, t, 0:1], rstd[k][0:parts, t:t + 1],
                                            ALU.subtract, ALU.mult)
                    if t < T - 1:
                        chain(ins)
                return ins

            patch_tile = lambda t: patches[:, :, :, PS * t:PS * t + PS].rearrange("p c y x -> p (c y) x")

            def patch_stats(b):
                dve.wait_ge(patches_in, 16 * QW * C * (b + 1))
                stats("p", b, patch_tile, PI)

            def patch_norm(b):
                normalize("p", b, lambda t: pn[:, t, :].rearrange("p (f x) -> p f x", x=PS), patch_tile, PI)\
                    .then_inc(patches_normed, 1)

            def psum_tile(j, parts):
                return lambda t: j.tile[0:parts, D * t:D * t + D]

            def slot_stats(body, name, c, k, b):
                j = Job(body, name, c)
                j.wait_filled(dve)
                stats(k, b, psum_tile(j, PI), PI)

            def slot_norm(body, name, c, k, b, dst):
                j = Job(body, name, c)
                j.drain(normalize(k, b, lambda t: dst[0:PI, t, :], psum_tile(j, PI), PI))

            def silu_product(b):
                dve.wait_ge(silu_in_ready, b + 1)
                dve.scalar_tensor_tensor(out=x3T[0:D, :], in0=x3T[0:D, :], scalar=1.0, in1=zT[:, :],
                                         op0=ALU.add, op1=ALU.mult).then_inc(silu_ready, 1)

            def pick_ids(b):
                wait(dve, rows_in, 16 * NS * b)
                dve.tensor_copy(ids_now[:, :], ids[:, :, b]).then_inc(ids_now_ready, 1)

            def sum_text(b):
                dve.wait_ge(rows_in, 16 * NS * (b + 1))
                wait(dve, text_placed, 16 * T * b)
                chain(dve.tensor_reduce(out=text[:, :], in_=rows[:, :, :].rearrange("p n d -> p d n"), axis=AX.X, op=ALU.add))
                chain.sync()
                dve.tensor_scalar(text[:, :], text[:, :], 1.0 / (NS + 1), None, ALU.mult).then_inc(text_ready, 1)

            def u_stats(body, c, b):
                Job(body, "A7", c).wait_drained(dve)
                dve.wait_ge(text_placed, 16 * T * (b + 1))
                stats("u", b, lambda t: h_all[:, b, t, :], P)

            def u_norm(b):
                wait(dve, hub_ready, b)
                normalize("u", b, lambda t: u[:, t, :], lambda t: h_all[:, b, t, :], P).then_inc(u_ready, 1)

            def n_stats(b):
                dve.wait_ge(u_ready, b + 1)
                stats("n", b, lambda t: u[:, t, :], P)

            def n_norm(b):
                normalize("n", b, lambda t: n2[:, t, :], lambda t: u[:, t, :], P).then_inc(n_ready, 1)

            def mid_parts(body, c, g, turn):
                for k, parts, top_ready, mid_ready in (("q", qparts, q_top_ready, q_mid_ready),
                                                       ("k", kparts, k_top_ready, k_mid_ready)):
                    j = Job(body, f"{k}{g}", c)
                    dve.wait_ge(top_ready, turn + 1)
                    j.drain(dve.tensor_tensor(rest[k][:, :], j.tile[:, 0:NU], parts[:, 0, :], ALU.subtract))
                    j.wait_drained(dve)
                    dve.tensor_copy(parts[:, 1, :], rest[k][:, :]).then_inc(mid_ready, 1)

            def maxima(body, b, s):
                for h in range(HQ):
                    j = Job(body, f"s{s}.{h}", b)
                    j.wait_filled(dve)
                    dve.tensor_reduce(out=negmax[:, s % 2, h:h + 1], in_=j.tile[0:P, 0:NU], axis=AX.X, op=ALU.max,
                                      negate=True).then_inc(negmax_ready, 1)

            def scale_values(body, b, s):
                g, t, r = s // T, s % T, s % 2
                if s == STEPS - 1:
                    dve.wait_ge(drained[SLOTS - 1], uses_before(body, SLOTS - 1, b))
                else:
                    Job(body, f"s{s}.{HQ - 1}", b).wait_drained(dve)
                chain(dve.tensor_reduce(out=s_txt[:, r, :], in_=e[:, r, :, :, PI:P], axis=AX.XY, op=ALU.add))
                chain.sync()
                chain(dve.scalar_tensor_tensor(out=den[:, r, :], in0=s_all[:, r, :], scalar=1.5, in1=s_txt[:, r, :],
                                               op0=ALU.mult, op1=ALU.subtract))
                chain.sync()
                chain(dve.reciprocal(rden[:, r, :], den[:, r, :]))
                chain.sync()
                dve.tensor_tensor(vs[:, r, :, :], v[g][:, t, :].rearrange("p (h d) -> p h d", h=HQ),
                                  rden[:, r, :].unsqueeze(2).to_broadcast([P, HQ, DH]), ALU.mult).then_inc(vs_ready, 1)

            def gate_output(b, g):
                dve.wait_ge(av_done, b * STEPS + T * (g + 1))
                dve.scalar_tensor_tensor(out=og[g][:, :], in0=gate[g][:, :], scalar=1.0, in1=o_acc[:, 0:NU],
                                         op0=ALU.add, op1=ALU.mult).then_inc(o_drained, 1)

            def add_residual(body, c, b):
                j = Job(body, "F", c)
                j.wait_filled(dve)
                dve.wait_ge(hub_ready, b + 1)
                wait(dve, base_ready, b)
                j.drain(dve.tensor_tensor(h2[:, :, :], j.tile[0:P, 0:T * D].rearrange("p (t d) -> p t d", t=T),
                                          h_all[:, b, :, :], ALU.add))

            def w_stats(body, c, b):
                Job(body, "F", c).wait_drained(dve)
                stats("w", b, lambda t: h2[:, t, :], P)

            def w_norm(b):
                normalize("w", b, lambda t: w[:, t, :], lambda t: h2[:, t, :], P).then_inc(w_ready, 1)

            def own_route(body, c):
                j = Job(body, "C2b", c)
                j.wait_filled(dve)
                j.drain(dve.tensor_copy(w_tok[:, :], j.tile[0:P, 0:T]))
                j.wait_drained(dve)

            def count_above(tiles):
                for t in tiles:
                    chain.sync()
                    chain(dve.tensor_scalar(cmp[:, :], route[:, :], w_tok[:, t:t + 1], 0.0, ALU.is_gt, ALU.add,
                                            accum_out=cnt_all[:, t:t + 1]))
                    chain.sync()
                    chain(dve.tensor_reduce(out=cnt_txt[:, t:t + 1],
                                            in_=cmp[:, :].rearrange("p (t q) -> p t q", t=T)[:, :, PI:P],
                                            axis=AX.XY, op=ALU.add))

            def candidates(b):
                chain.sync()
                chain(dve.tensor_scalar(c3[:, :], cnt_txt[:, :], -2.0, 1.0, ALU.mult, ALU.add))
                chain.sync()
                chain(dve.scalar_tensor_tensor(out=above_cnt[:, :], in0=cnt_all[:, :], scalar=3.0, in1=c3[:, :],
                                               op0=ALU.mult, op1=ALU.add))
                chain.sync()
                chain(dve.scalar_tensor_tensor(out=cand[:, :], in0=above_cnt[:, :], scalar=float(SEL), in1=above_cnt[:, :],
                                               op0=ALU.is_le, op1=ALU.mult))
                chain.sync()
                dve.tensor_reduce(out=edge[:, 0:1], in_=cand[:, :], axis=AX.X, op=ALU.max).then_inc(cand_ready, 1)

            def tied_tokens(b):
                dve.wait_ge(edge_ready, b + 1)
                chain(dve.tensor_scalar(above[:, :], above_cnt[:, :], edge[:, 1:2], None, ALU.is_lt))
                chain(dve.tensor_scalar(tied[:, :], above_cnt[:, :], edge[:, 1:2], None, ALU.is_equal))
                chain.sync()
                dve.tensor_reduce(out=tied_sum[:, :], in_=tied[:, :], axis=AX.X, op=ALU.add).then_inc(tied_ready, 1)

            def selection(body, c, b):
                j = Job(body, "C6", c)
                j.wait_filled(dve)
                j.drain(dve.tensor_copy(ties[:, :], j.tile[0:P, 0:2]))
                j.wait_drained(dve)
                chain(dve.tensor_tensor_scan(out=tie_no[:, :], data0=tied[:, :], data1=zeros7[0:P, :],
                                             initial=ties[:, 0:1], op0=ALU.add, op1=ALU.add))
                chain(dve.tensor_scalar(limit[:, 0:1], edge[:, 1:2], -1.0, float(SEL + 1), ALU.mult, ALU.add))
                chain.sync()
                chain(dve.tensor_tensor(limit[:, 1:2], limit[:, 0:1], ties[:, 1:2], ALU.subtract))
                chain(dve.tensor_tensor(tie_no[:, :], tie_no[:, :], tied[:, :], ALU.subtract))
                chain.sync()
                chain(dve.tensor_tensor(limit[:, 2:3], limit[:, 1:2], ties[:, 1:2], ALU.subtract))
                chain.sync()
                for k in range(3):
                    chain(dve.scalar_tensor_tensor(out=take[:, k, :], in0=tie_no[:, :], scalar=limit[:, k:k + 1],
                                                   in1=tied[:, :], op0=ALU.is_lt, op1=ALU.mult))
                chain.sync()
                chain(dve.tensor_tensor(take[:, :, :], take[:, :, :], above[:, :].unsqueeze(1).to_broadcast([P, 3, T]), ALU.add))
                chain.sync()
                dve.tensor_tensor(take[:, :, :], take[:, :, :], w_tok[:, :].unsqueeze(1).to_broadcast([P, 3, T]), ALU.mult)\
                    .then_inc(take_ready, 1)

            def gelu_product(b, g):
                dve.wait_ge(gelu_tanh_ready, 2 * b + g + 1)
                dve.scalar_tensor_tensor(out=hT[g][:, :], in0=hT[g][:, :], scalar=1.0, in1=hz[g][:, :],
                                         op0=ALU.add, op1=ALU.mult).then_inc(gelu_ready, 1)

            def ffn_output(body, c, b):
                j = Job(body, "C5", c)
                j.wait_filled(dve)
                wait(dve, out_ready, 3 * b)
                j.drain(dve.tensor_tensor(ys[:, :, :], j.tile[0:P, 0:T * D].rearrange("p (t d) -> p t d", t=T),
                                          b2_rep[0:P, :].unsqueeze(1).to_broadcast([P, T, D]), ALU.add))

            def hash_text():
                dve.wait_ge(text_in, 16)
                dve.wait_ge(consts_ready, 1)
                chain(dve.tensor_copy(tokf[:, :], tok_raw[:, :]))
                chain.sync()
                chain(dve.tensor_scalar(ok[:, :], tokf[:, :], 1.0, None, ALU.is_ge))
                chain(dve.tensor_scalar(ok2[:, :], tokf[:, :], 4.0, None, ALU.is_le))
                chain.sync()
                chain(dve.tensor_tensor(ok[:, :], ok[:, :], ok2[:, :], ALU.mult))
                chain.sync()
                chain(dve.scalar_tensor_tensor(out=safe[:, :], in0=tokf[:, :], scalar=-1.0, in1=ok[:, :],
                                               op0=ALU.add, op1=ALU.mult))
                chain(dve.tensor_scalar(bad1[:, :], ok[:, :], -1.0, 1.0, ALU.mult, ALU.add))
                chain.sync()
                chain(dve.tensor_copy(hash_i[:, 1, :], safe[:, :]))
                chain(dve.tensor_copy(bad[:, 1, :], bad1[:, :]))
                chain.sync()
                for k in range(2, SIZES[-1] + 1):
                    now, last = k % 2, (k + 1) % 2
                    chain(dve.scalar_tensor_tensor(out=hash_i[:, now, 1:L], in0=hash_i[:, last, 0:L - 1],
                                                   scalar=float(PRIME), in1=safe[:, 1:L], op0=ALU.mult, op1=ALU.add))
                    chain(dve.tensor_copy(hash_i[:, now, 0:1], safe[:, 0:1]))
                    chain(dve.tensor_tensor(bad[:, now, 1:L], bad[:, last, 0:L - 1], bad1[:, 1:L], ALU.max))
                    chain(dve.memset(bad[:, now, 0:1], 1.0))
                    chain.sync()
                    chain(dve.tensor_scalar(hash_i[:, now, :], hash_i[:, now, :], TBL - 1, None, ALU.bitwise_and))
                    chain.sync()
                    if k in SIZES:
                        n = k - SIZES[0]
                        chain(dve.scalar_tensor_tensor(out=ids_f[:, n, :], in0=bad[:, now, :], scalar=float(TBL),
                                                       in1=hash_i[:, now, :], op0=ALU.mult, op1=ALU.max))
                        chain.sync()
                        ins = dve.tensor_scalar(ids_f[:, n, :], ids_f[:, n, :], float(n * (TBL + 1)), None, ALU.add)
                        if n == NS - 1:
                            ins.then_inc(ids_f_ready, 1)
                        else:
                            chain(ins)

            def bias_rows():
                dve.wait_ge(weights_in, 16 * (NW + 7))
                j = Job("prologue", "W5", 0)
                j.wait_filled(dve)
                j.drain(dve.tensor_tensor(w1[FC:FC + 1, 1, :], j.tile[0:1, 0:D], row[0:1, 0:D], ALU.add))
                j = Job("prologue", "W6", 0)
                j.wait_filled(dve)
                j.drain(dve.tensor_tensor(wp1[D:D + 1, :], j.tile[0:1, 0:D], row[0:1, D:2 * D], ALU.add))

            def prologue():
                patch_stats(0)
                hash_text()
                patch_norm(0)
                bias_rows()
                Job("prologue", "W7", 0).wait_drained(dve)
                pick_ids(0)
                slot_stats("prologue", "A3", 0, "x", 0)
                slot_norm("prologue", "A3", 0, "x", 0, x2)
                slot_stats("prologue", "A5", 0, "y", 0)
                slot_norm("prologue", "A5", 0, "y", 0, y2)
                silu_product(0)
                sum_text(0)
                u_stats("prologue", 0, 0)
                u_norm(0)
                n_stats(0)
                n_norm(0)
                mid_parts("prologue", 0, 0, 0)

            def iteration(body, b, nxt, prev):
                chain.restart()
                for s in range(STEPS):
                    if nxt:
                        if s == 1:
                            patch_stats(b + 1)
                        if s == 4:
                            slot_norm(body, "A3", b, "x", b + 1, x2)
                        if s == 6:
                            slot_norm(body, "A5", b, "y", b + 1, y2)
                        if s == 7:
                            silu_product(b + 1)
                        if s == 8:
                            u_stats(body, b, b + 1)
                        if s == 9:
                            n_norm(b + 1)
                    maxima(body, b, s)
                    if s:
                        scale_values(body, b, s - 1)
                    elif prev:
                        scale_values(body, b, STEPS - 1)
                    if s == 0:
                        mid_parts(body, b, 1, 2 * b + 1)
                        if nxt:
                            pick_ids(b + 1)
                    if s == 1:
                        if prev:
                            gate_output(b - 1, 1)
                        if nxt:
                            patch_norm(b + 1)
                    if s == 7:
                        gate_output(b, 0)
                    if prev:
                        if s == 2:
                            add_residual(body, b, b - 1)
                            w_stats(body, b, b - 1)
                        if s == 3:
                            w_norm(b - 1)
                        if s == 6:
                            own_route(body, b)
                            count_above(range(0, 2))
                        if s == 7:
                            count_above(range(2, 5))
                        if s == 8:
                            count_above(range(5, 7))
                            candidates(b - 1)
                        if s == 9:
                            gelu_product(b - 1, 0)
                            gelu_product(b - 1, 1)
                        if s == 10:
                            tied_tokens(b - 1)
                            ffn_output(body, b, b - 1)
                        if s == 11:
                            selection(body, b, b - 1)
                    if nxt:
                        if s == 3:
                            slot_stats(body, "A3", b, "x", b + 1)
                        if s == 4:
                            sum_text(b + 1)
                        if s == 5:
                            slot_stats(body, "A5", b, "y", b + 1)
                        if s == 8:
                            u_norm(b + 1)
                            n_stats(b + 1)
                        if s == 10:
                            mid_parts(body, b, 0, 2 * b + 2)
                chain.restart()

            def epilogue(body, b):
                scale_values(body, b, STEPS - 1)
                gate_output(b, 1)
                add_residual(body, b, b)
                w_stats(body, b, b)
                w_norm(b)
                own_route(body, b)
                count_above(range(T))
                candidates(b)
                gelu_product(b, 0)
                gelu_product(b, 1)
                tied_tokens(b)
                ffn_output(body, b, b)
                selection(body, b, b)

            run(dve, iteration, prologue, epilogue)

        @block.tensor
        def _(pe):
            def job(body, name, c):
                j = Job(body, name, c)
                j.wait_free(pe)
                return j

            def transposes(j, src, parts, cols):
                settle(pe)
                for t in range(T):
                    a = tile_col(t, parts)
                    ins = pe.transpose(j.tile[0:cols, a:a + parts], src(t), ident[0:parts, 0:parts])
                j.fill(ins)

            def project(j, rows_, weights, xT):
                for a, z in pieces(NU):
                    ins = pe.matmul(j.tile[0:rows_, a:z], weights, xT[:, a:z], start=True, stop=True)
                j.fill(ins)

            def token_major(j, parts, pairs):
                for t in range(T):
                    for i, (xT, weights) in enumerate(pairs):
                        ins = pe.matmul(j.tile[0:parts, t * D:t * D + D], xT[:, t * parts:(t + 1) * parts], weights,
                                        start=(i == 0), stop=(i == len(pairs) - 1))
                j.fill(ins)

            def weight_jobs():
                pe.wait_ge(consts_ready, 1)
                pe.wait_ge(weights_in, 16 * (NW + 7))
                j = job("prologue", "W1", 0)
                for k in range(6):
                    ins = pe.transpose(j.tile[0:D, k * 128:(k + 1) * 128], raw_qkv[:, k, :], ident[:, :])
                j.fill(ins)
                j = job("prologue", "W2", 0)
                for k in range(2):
                    ins = pe.transpose(j.tile[0:D, k * 128:(k + 1) * 128], raw_gate[:, k, :], ident[:, :])
                j.fill(ins)
                j = job("prologue", "W3", 0)
                for k in range(2):
                    ins = pe.transpose(j.tile[:, k * D:(k + 1) * D], raw_final[:, k * 128:(k + 1) * 128], ident[0:D, 0:D])
                j.fill(ins)
                Job("prologue", "W1", 0).wait_drained(pe)
                j = job("prologue", "W4", 0)
                for a, z in pieces(3 * INNER):
                    ins = pe.matmul(j.tile[0:1, a:z], col[0:D, 5:6], qkv_t[:, a:z], start=True, stop=True)
                j.fill(ins)
                j = job("prologue", "W5", 0)
                for k in range(2):
                    ins = pe.matmul(j.tile[0:1, 0:D], ln1_gb[:, k, 1:2], w1_raw[:, k, :], start=(k == 0), stop=(k == 1))
                j.fill(ins)
                j = job("prologue", "W6", 0)
                j.fill(pe.matmul(j.tile[0:1, 0:D], col[0:D, 1:2], wp1_raw[:, :], start=True, stop=True))
                pe.wait_ge(ids_f_ready, 1)
                j = job("prologue", "W7", 0)
                for n in range(NS):
                    ins = pe.transpose(j.tile[0:L, n * B:(n + 1) * B], ids_f[:, n, :], ident[0:B, 0:B])
                j.fill(ins)
                for name in ("W4", "W5", "W6"):
                    Job("prologue", name, 0).wait_drained(pe)

            def patch_transposes(body, c, b):
                pe.wait_ge(patches_normed, b + 1)
                for k, name in enumerate(("A1", "A2")):
                    transposes(job(body, name, c), lambda t: pn[:, t, k * FC:(k + 1) * FC], PI, FC)

            def embed(body, c):
                Job(body, "A2", c).wait_drained(pe)
                token_major(job(body, "A3", c), PI, [(pnT[0:FC, 0, :], w1[0:FC, 0, :]), (pnT[:, 1, :], w1[:, 1, :])])

            def x2_transposes(body, c):
                Job(body, "A3", c).wait_drained(pe)
                transposes(job(body, "A4", c), lambda t: x2[0:PI, t, :], PI, D)

            def pool_in(body, c):
                Job(body, "A4", c).wait_drained(pe)
                token_major(job(body, "A5", c), PI, [(x2T[:, :], wp1[:, :])])

            def y2_transposes(body, c):
                Job(body, "A5", c).wait_drained(pe)
                transposes(job(body, "A6", c), lambda t: y2[0:PI, t, :], PI, D)

            def pool_out(body, c, b):
                pe.wait_ge(silu_ready, b + 1)
                token_major(job(body, "A7", c), PI, [(x3T[:, :], wp2[:, :])])

            def token_transposes(body, c, b):
                pe.wait_ge(u_ready, b + 1)
                transposes(job(body, "A8", c), lambda t: u[:, t, :], P, D)
                pe.wait_ge(n_ready, b + 1)
                transposes(job(body, "A9", c), lambda t: n2[:, t, :], P, D)

            def queries_keys(body, c, g):
                if g == 0:
                    Job(body, "A9", c).wait_drained(pe)
                for i, name in enumerate("qk"):
                    a = i * INNER + g * 128
                    project(job(body, f"{name}{g}", c), 128, wqkv[:, a:a + 128], nT)

            def values_gates(body, c, g):
                j = job(body, f"v{g}", c)
                a = 2 * INNER + g * 128
                for t in range(T):
                    ins = pe.matmul(j.tile[0:P, t * 128:(t + 1) * 128], nT[:, t * P:(t + 1) * P], wqkv[:, a:a + 128],
                                    start=True, stop=True)
                j.fill(ins)
                project(job(body, f"g{g}", c), 128, wgate[:, g * 128:(g + 1) * 128], uT)

            def scores(body, b, s):
                g, t = s // T, s % T
                if t == 0:
                    turn = 2 * b + g + 1
                    pe.wait_ge(q_placed, 16 * HQ * len(PARTS) * turn)
                    pe.wait_ge(k_placed, 16 * HQ * len(PARTS) * turn)
                for h in range(HQ):
                    j = job(body, f"s{s}.{h}", b)
                    for r in range(2):
                        for a, z in pieces(NU):
                            ins = pe.matmul(j.tile[0:P, a:z], qs[g][:, h, r, t * P:(t + 1) * P], ks[g][:, h, r, a:z],
                                            start=(r == 0), stop=(r == 1))
                    j.fill(ins)

            def attend(b, s):
                t, r = s % T, s % 2
                pe.wait_ge(vs_ready, b * STEPS + s + 1)
                if t == 0:
                    wait(pe, o_drained, 2 * b + s // T)
                for a, z in pieces(NU):
                    for h in range(HQ):
                        ins = pe.matmul(o_acc[DH * h:DH * h + DH, a:z], vs[:, r, h, :],
                                        e[:, r, h, :, :].rearrange("p t q -> p (t q)")[:, a:z],
                                        start=(t == 0), stop=(t == T - 1))
                ins.then_inc(av_done, 1)

            def output_projection(body, c, b):
                pe.wait_ge(o_drained, 2 * (b + 1))
                token_major(job(body, "F", c), P, [(og[g][:, :], wfinal[:, g, :]) for g in range(2)])

            def w_transposes(body, c, b):
                pe.wait_ge(w_ready, b + 1)
                transposes(job(body, "C1", c), lambda t: w[:, t, :], P, D)

            def routing(body, c):
                Job(body, "C1", c).wait_drained(pe)
                project(job(body, "C2", c), P, wroute[:, :], wT)

            def hidden(body, c, g):
                project(job(body, f"C{3 + g}", c), 128, wh[:, g * 128:(g + 1) * 128], wT)

            def route_transposes(body, c):
                Job(body, "C2", c).wait_drained(pe)
                j = job(body, "C2b", c)
                settle(pe)
                for t in range(T):
                    ins = pe.transpose(j.tile[0:P, t:t + 1], route[0:1, t * P:(t + 1) * P], ident[0:1, 0:1])
                j.fill(ins)

            def ffn_out(body, c, b):
                pe.wait_ge(gelu_ready, 2 * (b + 1))
                token_major(job(body, "C5", c), P, [(hT[g][:, :], wy[:, g, :]) for g in range(2)])

            def count_ties(body, c, b):
                pe.wait_ge(tied_ready, b + 1)
                j = job(body, "C6", c)
                pe.matmul(j.tile[0:P, 0:1], before[0:P, :], tied_sum[:, :], start=True, stop=True)
                j.fill(pe.matmul(j.tile[0:P, 1:2], images[0:P, :], tied_sum[:, :], start=True, stop=True))

            def prologue():
                weight_jobs()
                patch_transposes("prologue", 0, 0)
                embed("prologue", 0)
                x2_transposes("prologue", 0)
                pool_in("prologue", 0)
                y2_transposes("prologue", 0)
                pool_out("prologue", 0, 0)
                token_transposes("prologue", 0, 0)
                queries_keys("prologue", 0, 0)
                values_gates("prologue", 0, 0)

            def iteration(body, b, nxt, prev):
                for s in range(STEPS):
                    scores(body, b, s)
                    if s == 0:
                        queries_keys(body, b, 1)
                    if s == 2:
                        if prev:
                            output_projection(body, b, b - 1)
                        values_gates(body, b, 1)
                    if prev:
                        if s == 4:
                            w_transposes(body, b, b - 1)
                        if s == 5:
                            routing(body, b)
                        if s == 6:
                            hidden(body, b, 0)
                            route_transposes(body, b)
                        if s == 7:
                            hidden(body, b, 1)
                        if s == 10:
                            ffn_out(body, b, b - 1)
                        if s == 11:
                            count_ties(body, b, b - 1)
                    if nxt:
                        if s == 2:
                            patch_transposes(body, b, b + 1)
                        if s == 3:
                            embed(body, b)
                        if s == 4:
                            x2_transposes(body, b)
                        if s == 5:
                            pool_in(body, b)
                        if s == 6:
                            y2_transposes(body, b)
                        if s == 7:
                            pool_out(body, b, b + 1)
                        if s == 9:
                            token_transposes(body, b, b + 1)
                        if s == 10:
                            queries_keys(body, b, 0)
                        if s == 11:
                            values_gates(body, b, 0)
                    if s:
                        attend(b, s - 1)
                    elif prev:
                        attend(b - 1, STEPS - 1)

            def epilogue(body, b):
                attend(b, STEPS - 1)
                output_projection(body, b, b)
                w_transposes(body, b, b)
                routing(body, b)
                hidden(body, b, 0)
                route_transposes(body, b)
                hidden(body, b, 1)
                ffn_out(body, b, b)
                count_ties(body, b, b)

            run(pe, iteration, prologue, epilogue)


PARAMETERS = [
    "L0_tok_ln1_g", "L0_tok_ln1_b", "L0_tok_W1", "L0_tok_b1", "L0_tok_ln2_g", "L0_tok_ln2_b", "L0_tok_Wp1",
    "L0_tok_bp1", "L0_tok_lnp_g", "L0_tok_lnp_b", "L0_tok_Wp2", "L0_tok_bp2", "L0_txt_tables", "L0_attn_ln_gamma",
    "L0_attn_ln_beta", "L0_attn_W_qkv", "L0_attn_W_gate", "L0_attn_b_gate", "L0_attn_W_final", "L0_attn_b_final",
    "L0_ffn_wr", "L0_ffn_br", "L0_ffn_w1", "L0_ffn_b1", "L0_ffn_w2", "L0_ffn_b2",
]


def kernel(**inputs):
    import concourse.bacc as bacc
    from concourse.bass_utils import run_bass_kernel_spmd

    nc = bacc.Bacc("TRN2", target_bir_lowering=False, num_devices=1)
    arrays, args = {}, {}
    for name in ["x", "x_txt", *PARAMETERS]:
        a = np.ascontiguousarray(inputs[name])
        arrays[f"in_{name}"] = a
        args[name] = nc.dram_tensor(f"in_{name}", a.shape, mybir.dt.from_np(a.dtype), kind="ExternalInput").ap()
    out = nc.dram_tensor("out", (B, SEQ, D), F32, kind="ExternalOutput").ap()
    build(nc, args["x"], args["x_txt"], args, out)
    result = run_bass_kernel_spmd(nc, [arrays], core_ids=[0])
    return result.results[0]["out"]
```

```python
from contextlib import ExitStack

import numpy as np

import concourse.bass as bass
from concourse import mybir
from concourse.alu_op_type import AluOpType as ALU

F32 = mybir.dt.float32
BF16 = mybir.dt.bfloat16
I32 = mybir.dt.int32
ACT = mybir.ActivationFunctionType
AX = mybir.AxisListType
RMAX = bass.bass_isa.ReduceOp.max

B = 8
C, HW, PS = 3, 224, 8
GR = HW // PS
NI = GR * GR
L = 77
NU = NI + L
SEQ = 3 * NI + L
T = 7
PI, PT = NI // T, L // T
P = PI + PT
QW = GR // T
D = 64
FD = C * PS * PS
FC = FD // 2
H, DH = 8, 32
HQ = 4
INNER = H * DH
HID = 4 * D
EPS = 1e-5
SIZES = range(3, 21)
NS = len(SIZES)
TBL = 1024
PRIME = 31
SEL = int(0.5 * SEQ) - 1
KP = 96
BANK = 512
W4 = 4 * P
SLOTS = 3
STEPS = 2 * T
PARTS = [((0, 0), (0, 2)), ((0, 1), (1, 2)), ((1, 0), (2, 0)), ((1, 1), (2, 1))]


NEXT_JOBS = {(2, 0): ["A4"], (2, 3): ["A5"], (4, 3): ["A6"], (6, 0): ["A7"], (8, 0): ["A8"], (8, 2): ["A9"],
             (9, 1): ["q0"], (9, 3): ["k0"], (10, 2): ["v0"], (12, 0): ["A1"], (12, 1): ["A2"], (13, 0): ["A3"]}
OWN_JOBS = {(0, 1): ["q1"], (1, 0): ["k1"], (3, 1): ["v1"], (5, 1): ["g1"], (6, 2): ["g0"]}
FFN_JOBS = {(1, 2): ["F"], (3, 3): ["C1"], (4, 1): ["C2"], (4, 2): ["C3"], (5, 0): ["C2b"], (5, 2): ["C4"],
            (8, 3): ["C7"], (9, 2): ["C5"], (10, 0): ["C8"], (11, 2): ["C6"]}


def body_jobs(nxt, prev):
    names = []
    for s in range(STEPS):
        for h in range(HQ):
            at = (s, h)
            names += [f"s{s}.{h}"]
            names += (FFN_JOBS.get(at, []) if prev else []) + OWN_JOBS.get(at, []) + (NEXT_JOBS.get(at, []) if nxt else [])
    return names


BODIES = {
    "prologue": ["W1", "W2", "W3", "W4", "W5", "W6", "W7", "P1", "P2", "P3", "A4", "A5", "A6", "A7",
                 "A8", "A9", "q0", "k0", "v0", "A1", "A2", "A3"],
    "first": body_jobs(True, False),
    "steady": body_jobs(True, True),
    "last": body_jobs(False, True),
    "epilogue": [j for s in sorted(FFN_JOBS) for j in FFN_JOBS[s]],
}


def slots_of(body):
    at = [(n - len(BODIES[body])) % SLOTS for n in range(len(BODIES[body]))]
    return {name: (at[n], at[:n].count(at[n])) for n, name in enumerate(BODIES[body])}


def in_slot(body, slot):
    return sum(k == slot for k, _ in slots_of(body).values())


def uses_before(body, slot, b):
    n = 0
    if body == "prologue":
        return n
    n += in_slot("prologue", slot)
    if body == "first":
        return n
    n += in_slot("first", slot)
    if body == "steady":
        return (b - 1) * in_slot("steady", slot) + n
    n += (B - 2) * in_slot("steady", slot)
    if body == "last":
        return n
    return n + in_slot("last", slot)


def build(nc, x, x_txt, p, out):
    ctx = ExitStack()
    with ctx:
        def sb(name, shape, dt=F32):
            return ctx.enter_context(nc.sbuf_tensor(name, shape, dt))

        def sem(name):
            return ctx.enter_context(nc.semaphore(name))

        slot = [ctx.enter_context(nc.psum_tensor(f"slot{k}", [128, 2 * BANK], F32)) for k in range(SLOTS)]
        o_acc = ctx.enter_context(nc.psum_tensor("o_acc", [128, 2 * BANK], F32))

        ident = sb("ident", [128, 128])
        neg_half = sb("neg_half", [128, T])
        before = sb("before", [128, P])
        images = sb("images", [128, P])
        v_weight = sb("v_weight", [128, 1])
        copies = sb("copies", [128, 1], BF16)
        zeros7 = sb("zeros7", [128, T])
        ln1_gb = sb("ln1_gb", [FC, 2, 2])
        w1_raw = sb("w1_raw", [FC, 2, D])
        w1 = sb("w1", [FC + 1, 2, D])
        col = sb("col", [128, 12])
        wp1_raw = sb("wp1_raw", [D, D])
        wp1 = sb("wp1", [KP, D])
        wp2 = sb("wp2", [KP, D])
        wqkv = sb("wqkv", [KP, 3 * INNER])
        wgate = sb("wgate", [KP, INNER])
        wfinal = sb("wfinal", [128, 2, D])
        wroute = sb("wroute", [KP, P])
        wh = sb("wh", [KP, HID])
        wy = sb("wy", [128, 2, D])
        bf_rep = sb("bf_rep", [128, D])
        b2_rep = sb("b2_rep", [128, D])
        row = sb("row", [1, 2 * D])
        tok_raw = sb("tok_raw", [B, L], I32)
        tokf = sb("tokf", [B, L])
        ok = sb("ok", [B, L])
        ok2 = sb("ok2", [B, L])
        safe = sb("safe", [B, L])
        bad1 = sb("bad1", [B, L])
        hash_f = sb("hash_f", [B, 2, L])
        hash_i = sb("hash_i", [B, 2, L], I32)
        bad = sb("bad", [B, 2, L])
        ids = sb("ids", [L, NS, B + 1], I32)
        ids_now = sb("ids_now", [L, NS], I32)
        rows_flat = sb("rows_flat", [128, NS * D])
        rows = rows_flat[0:L, :].rearrange("p (n d) -> p n d", n=NS)
        text = sb("text", [L, D])
        patches = sb("patches", [PI, C, PS, T * PS])
        pn_flat = sb("pn_flat", [128, T * FD])
        pn = pn_flat[0:PI, :].rearrange("p (t f) -> p t f", t=T)
        st = {k: sb(f"st_{k}", [128, T, 6]) for k in ("p", "x", "y", "u", "n", "w")}
        mv = {k: sb(f"mv_{k}", [128, T, 2]) for k in ("p", "x", "y", "u", "n", "w")}
        ve = {k: sb(f"ve_{k}", [128, T]) for k in ("p", "x", "y", "u", "n", "w")}
        rstd = {k: sb(f"rstd_{k}", [128, T]) for k in ("p", "x", "y", "u", "n", "w")}
        pnT = sb("pnT", [FC + 1, 2, NI])
        x2 = sb("x2", [P, T, D])
        x2T = sb("x2T", [KP, NI])
        y2 = x2
        zT = sb("zT", [D, NI])
        x3T = x2T
        h_all = sb("h_all", [P, B, T, D])
        u = sb("u", [P, T, D])
        n2 = x2
        uT = sb("uT", [KP, NU])
        nT = sb("nT", [KP, NU])
        qparts = sb("qparts", [128, 3, NU], BF16)
        kparts = sb("kparts", [128, 3, NU], BF16)
        rest = {k: sb(f"rest_{k}", [128, NU]) for k in "qk"}
        qs = [sb(f"qs{g}", [128, HQ, 2, NU], BF16) for g in range(2)]
        ks = [sb(f"ks{g}", [128, HQ, 2, NU], BF16) for g in range(2)]
        v = [sb(f"v{g}", [P, T, HQ * DH]) for g in range(2)]
        gate = [sb(f"gate{g}", [128, NU]) for g in range(2)]
        e_flat = sb("e_flat", [128, 2 * HQ * NU])
        e = e_flat[0:P, :].rearrange("p (r h t q) -> p r h t q", r=2, h=HQ, t=T)
        raw_qkv = e_flat[:, 0:6 * D].rearrange("p (k n) -> p k n", k=6)
        raw_gate = e_flat[:, 6 * D:8 * D].rearrange("p (k n) -> p k n", k=2)
        raw_final = e_flat[0:D, 8 * D:8 * D + INNER]
        qkv_t = e_flat[0:D, 1024:1024 + 3 * INNER]
        ids_f = e_flat[0:B, 2048:2048 + NS * L].rearrange("p (n l) -> p n l", n=NS)
        negmax = sb("negmax", [P, 2, HQ])
        s_all = sb("s_all", [P, 2, HQ])
        s_txt = sb("s_txt", [P, 2, HQ])
        den = sb("den", [P, 2, HQ])
        rden = sb("rden", [P, 2, HQ])
        vs = sb("vs", [P, 2, HQ, DH])
        og = [sb("og0", [128, NU]), gate[1]]
        h2 = sb("h2", [P, T, D])
        w = sb("w", [P, T, D])
        wT = sb("wT", [KP, NU])
        base = sb("base", [P, T, D])
        route = sb("route", [P, NU])
        w_tok = sb("w_tok", [P, T])
        less = [(qparts, kparts)[t // 3][0:P, t % 3, :] for t in range(T - 1)] + [sb("less_last", [P, NU], BF16)[:, :]]
        above_cnt = sb("above_cnt", [P, T])
        cand = sb("cand", [P, T])
        edge = sb("edge", [P, 2])
        above = sb("above", [P, T])
        tied = sb("tied", [P, T])
        tied_sum = sb("tied_sum", [P, 1])
        tie_no = sb("tie_no", [P, T])
        ties = sb("ties", [P, 2])
        limit = sb("limit", [P, 3])
        take = sb("take", [P, 3, T])
        hz = [rest[k] for k in "qk"]
        hT = [pn_flat[:, 0:NU], rows_flat[:, 0:NU]]
        ys = sb("ys", [P, T, D])
        o_c = [sb(f"o_c{c}", [P, T, D]) for c in range(3)]

        filled = [sem(f"slot{k}_filled") for k in range(SLOTS)]
        drained = [sem(f"slot{k}_drained") for k in range(SLOTS)]
        weights_in = sem("weights_in")
        text_in = sem("text_in")
        consts_ready = sem("consts_ready")
        settled = sem("settled")
        ids_f_ready = sem("ids_f_ready")
        ids_now_ready = sem("ids_now_ready")
        rows_in = sem("rows_in")
        text_ready = sem("text_ready")
        text_placed = sem("text_placed")
        patches_in = sem("patches_in")
        patches_normed = sem("patches_normed")
        embedded = {n: sem(f"embedded_{n}") for n in "35"}
        x_normed = sem("x_normed")
        y_normed = sem("y_normed")
        var_ready = {k: sem(f"var_ready_{k}") for k in mv}
        centered = {k: sem(f"centered_{k}") for k in mv if k != "p"}
        rstd_ready = sem("rstd_ready")
        silu_in_ready = sem("silu_in_ready")
        silu_ready = sem("silu_ready")
        u_ready = sem("u_ready")
        n_ready = sem("n_ready")
        hub_ready = sem("hub_ready")
        q_top_ready = sem("q_top_ready")
        k_top_ready = sem("k_top_ready")
        q_rest_ready = sem("q_rest_ready")
        k_rest_ready = sem("k_rest_ready")
        q_mid_ready = sem("q_mid_ready")
        k_mid_ready = sem("k_mid_ready")
        q_parts_ready = sem("q_parts_ready")
        k_parts_ready = sem("k_parts_ready")
        q_placed = sem("q_placed")
        k_placed = sem("k_placed")
        negmax_ready = sem("negmax_ready")
        vs_ready = sem("vs_ready")
        av_done = sem("av_done")
        o_drained = sem("o_drained")
        w_ready = sem("w_ready")
        base_ready = sem("base_ready")
        gelu_arg_ready = sem("gelu_arg_ready")
        gelu_tanh_ready = sem("gelu_tanh_ready")
        gelu_ready = sem("gelu_ready")
        own_route_ready = sem("own_route_ready")
        less_ready = sem("less_ready")
        cand_ready = sem("cand_ready")
        edge_ready = sem("edge_ready")
        tied_ready = sem("tied_ready")
        take_ready = sem("take_ready")
        out_ready = sem("out_ready")
        stored = sem("stored")

        def wait(eng, s, value):
            if not (isinstance(value, int) and value <= 0):
                eng.wait_ge(s, value)

        def settle(eng):
            eng.sem_inc(settled)

        class Job:

            def __init__(self, body, name, b):
                self.k, turn = slots_of(body)[name]
                self.n = uses_before(body, self.k, b) + turn
                self.tile = slot[self.k]

            def wait_free(self, pe):
                wait(pe, drained[self.k], self.n)

            def wait_filled(self, eng):
                eng.wait_ge(filled[self.k], self.n + 1)

            def wait_drained(self, eng):
                eng.wait_ge(drained[self.k], self.n + 1)

            def fill(self, ins):
                ins.then_inc(filled[self.k], 1)

            def drain(self, ins):
                ins.then_inc(drained[self.k], 1)

        class Chain:

            def __init__(self, eng, name):
                self.eng, self.sem, self.n = eng, sem(name), 0

            def __call__(self, ins):
                ins.then_inc(self.sem, 1)
                self.n += 1

            def sync(self):
                if self.n:
                    self.eng.wait_ge(self.sem, self.n)

            def restart(self):
                if self.n:
                    self.eng.wait_ge(self.sem, self.n)
                    self.eng.sem_clear(self.sem)
                    self.n = 0

        def run(eng, iteration, prologue, epilogue):
            prologue()
            iteration("first", 0, True, False)
            with eng.Fori(1, B - 1) as b:
                iteration("steady", b, True, True)
            iteration("last", B - 1, False, True)
            epilogue("epilogue", B - 1)

        def pieces(n):
            return [(a, min(n, a + BANK)) for a in range(0, n, BANK)]

        def tile_col(t, parts):
            return (t // 4) * BANK + (t % 4) * parts

        def fold(eng_do, dst, tile, rows_, parts):
            eng_do(dst[:, 0:4 * parts], tile[0:rows_, 0:4 * parts])
            return eng_do(dst[:, 4 * parts:T * parts], tile[0:rows_, BANK:BANK + (T - 4) * parts])

        NW = 27
        block = ctx.enter_context(nc.Block())

        @block.sync
        def _(sp):
            def load(dst, src, s, elements=False):
                sp.dma_start(dst, src, allow_slow_non_contiguous=elements).then_inc(s, 16)

            def load_patches(b):
                for q in range(QW):
                    for c in range(C):
                        load(patches[q:PI:QW, c, :, :],
                             x[b, c].rearrange("(r y) (q w) -> q r y w", y=PS, q=QW)[q], patches_in)

            load(tok_raw[:, :], x_txt, text_in)
            load_patches(0)
            count = [0]

            def load_w(dst, src, elements=False):
                count[0] += 1
                load(dst, src, weights_in, elements)

            one = lambda a: a.rearrange("(a n) -> a n", a=1)
            column = lambda a: a.rearrange("(n a) -> n a", a=1)
            w1_d = p["L0_tok_W1"].rearrange("(f c) n -> c f n", c=C)
            for src, dst in ((w1_d, lambda a, b_, k: w1_raw[a:b_, k, :]),
                             (p["L0_tok_ln1_g"].rearrange("(f c o) -> c f o", c=C, o=1), lambda a, b_, k: ln1_gb[a:b_, k, 0:1]),
                             (p["L0_tok_ln1_b"].rearrange("(f c o) -> c f o", c=C, o=1), lambda a, b_, k: ln1_gb[a:b_, k, 1:2])):
                half = PS * PS // 2
                few = src is not w1_d
                load_w(dst(0, 2 * half, 0), src[0], few)
                load_w(dst(2 * half, 3 * half, 0), src[1, 0:half], few)
                load_w(dst(0, half, 1), src[1, half:2 * half], few)
                load_w(dst(half, 3 * half, 1), src[2], few)
            load_w(raw_qkv[:, :, :], p["L0_attn_W_qkv"].rearrange("(k r) n -> r k n", r=128))
            load_w(raw_gate[:, :, :], p["L0_attn_W_gate"].rearrange("(k r) n -> r k n", r=128))
            load_w(raw_final[:, :], p["L0_attn_W_final"])
            load_w(wp1_raw[:, :], p["L0_tok_Wp1"])
            for n, name in enumerate(("L0_tok_ln2_g", "L0_tok_ln2_b", "L0_tok_lnp_g", "L0_tok_lnp_b",
                                      "L0_attn_ln_gamma", "L0_attn_ln_beta")):
                load_w(col[0:D, n:n + 1], column(p[name]), True)
            load_w(row[0:1, 0:D], one(p["L0_tok_b1"]))
            load_w(row[0:1, D:2 * D], one(p["L0_tok_bp1"]))
            load_w(wy[:, :, :], p["L0_ffn_w2"].rearrange("(k r) n -> r k n", r=128))
            load_w(bf_rep[0:P, :], one(p["L0_attn_b_final"]).to_broadcast([P, D]))
            load_w(b2_rep[0:P, :], one(p["L0_ffn_b2"]).to_broadcast([P, D]))
            assert count[0] == NW, count
            sp.wait_ge(consts_ready, 1)
            load_w(wp2[0:D, :], p["L0_tok_Wp2"])
            load_w(wp2[D:D + 1, :], one(p["L0_tok_bp2"]))
            load_w(wgate[D:D + 1, :], one(p["L0_attn_b_gate"]))
            load_w(col[0:D, 7:8], p["L0_ffn_wr"], True)
            load_w(col[D:D + 1, 7:8], one(p["L0_ffn_br"]), True)
            load_w(wh[0:D, :], p["L0_ffn_w1"])
            load_w(wh[D:D + 1, :], one(p["L0_ffn_b1"]))
            assert count[0] == NW + 7

            def place(parts, dst, side, blocks, s):
                for h in range(HQ):
                    for r in blocks:
                        i, j = PARTS[r][0][side], PARTS[r][1][side]
                        src = parts[DH * h:DH * h + DH, i:j + 1:max(j - i, 1), :] if j > i else \
                            parts[DH * h:DH * h + DH, i:i + 1, :].to_broadcast([DH, 2, NU])
                        load(dst[DH * r:DH * r + DH, h, :, :], src, s)

            def place_quad(b, g, turn):
                sp.wait_ge(q_mid_ready, turn + 1)
                place(qparts, qs[g], 0, (0, 1), q_placed)
                sp.wait_ge(k_mid_ready, turn + 1)
                place(kparts, ks[g], 1, (2, 3), k_placed)
                sp.wait_ge(q_parts_ready, turn + 1)
                place(qparts, qs[g], 0, (2, 3), q_placed)
                sp.wait_ge(k_parts_ready, turn + 1)
                place(kparts, ks[g], 1, (0, 1), k_placed)

            def place_text(b):
                sp.wait_ge(text_ready, b + 1)
                for t in range(T):
                    load(h_all[PI:P, b, t, :], text[t:L:T, :], text_placed)

            def store(b):
                for c in range(3):
                    sp.wait_ge(out_ready, 3 * b + c + 1)
                    n = P if c == 2 else PI
                    load(out[b, c * NI:c * NI + n * T, :].rearrange("(p t) d -> p t d", t=T), o_c[c][0:n, :, :], stored)

            def prologue():
                for b in range(2):
                    sp.wait_ge(patches_normed, b + 1)
                    load_patches(b + 1)
                    if b == 0:
                        place_text(0)
                        place_quad(0, 0, 0)

            def iteration(body, b, nxt, prev):
                place_quad(b, 1, 2 * b + 1)
                if nxt:
                    place_text(b + 1)
                    place_quad(b + 1, 0, 2 * b + 2)
                    sp.wait_ge(patches_normed, b + 3)
                    load_patches((b + 3) % B)
                if prev:
                    store(b - 1)

            def epilogue(body, b):
                store(b)
                sp.wait_ge(stored, 16 * 3 * B)
                sp.wait_ge(patches_in, 16 * QW * C * (B + 2))

            run(sp, iteration, prologue, epilogue)

        @block.gpsimd
        def _(pool):
            chain = Chain(pool, "pool_chain")

            def step(ins):
                chain(ins)
                chain.sync()

            for tile in (wp1, wp2, wqkv, wgate, wroute, wh, x2T, uT, nT, wT):
                step(pool.memset(tile[D:KP, :], 0.0))
            step(pool.memset(ident[:, :], 0.0))
            step(pool.memset(before[:, :], 1.0))
            step(pool.memset(images[:, :], 1.0))
            step(pool.memset(v_weight[:, :], 1.5))
            step(pool.memset(copies[:, :], 3.0))
            step(pool.memset(neg_half[:, :], -0.5))
            step(pool.memset(pnT[FC:FC + 1, 1, :], 1.0))
            step(pool.memset(zeros7[:, :], 0.0))
            step(pool.memset(bad[:, :, :], 1.0))
            step(pool.memset(hash_f[:, :, :], 0.0))
            step(pool.memset(hash_i[:, :, :], 0))
            for tile in (x2T, uT, nT, wT):
                step(pool.memset(tile[D:D + 1, :], 1.0))
            step(pool.affine_select(out=ident[:, :], in_=ident[:, :], compare_op=ALU.not_equal, fill=1.0,
                                     base=0, pattern=[[-1, 128]], channel_multiplier=1))
            step(pool.affine_select(out=before[:, :], in_=before[:, :], compare_op=ALU.is_gt, fill=0.0,
                                     base=0, pattern=[[1, P]], channel_multiplier=-1))
            step(pool.affine_select(out=images[:, :], in_=images[:, :], compare_op=ALU.is_gt, fill=0.0,
                                     base=PI, pattern=[[0, P]], channel_multiplier=-1))
            step(pool.affine_select(out=v_weight[:, :], in_=v_weight[:, :], compare_op=ALU.is_gt, fill=0.5,
                                     base=PI, pattern=[[0, 1]], channel_multiplier=-1))
            step(pool.affine_select(out=copies[:, :], in_=copies[:, :], compare_op=ALU.is_gt, fill=1.0,
                                     base=PI, pattern=[[0, 1]], channel_multiplier=-1))
            pool.memset(ys[:, :, :], 0.0).then_inc(consts_ready, 1)
            pool.wait_ge(consts_ready, 1)

            def gather(b, sizes):
                pool.wait_ge(ids_now_ready, b + 1)
                settle(pool)
                for n in sizes:
                    pool.indirect_dma_start(
                        out=rows[:, n, :], out_offset=None,
                        in_=p["L0_txt_tables"].rearrange("n r d -> (n r) d"),
                        in_offset=bass.IndirectOffsetOnAxis(ap=ids_now[:, n:n + 1], axis=0)).then_inc(rows_in, 16)

            def find_rstd(k, b, parts):
                pool.wait_ge(var_ready[k], b + 1)
                settle(pool)
                chain(pool.tensor_scalar(ve[k][0:parts, :], mv[k][0:parts, :, 1], EPS, None, ALU.add))
                chain.sync()
                return pool.tensor_tensor(rstd[k][0:parts, :], ve[k][0:parts, :], neg_half[0:parts, :], ALU.pow)

            def finish_norm(k, b, dst, parts, normed):
                chain(find_rstd(k, b, parts))
                chain.sync()
                pool.wait_ge(centered[k], b + 1)
                pool.tensor_tensor(dst[0:parts, :, :], dst[0:parts, :, :],
                                   rstd[k][0:parts, :].unsqueeze(2).to_broadcast([parts, T, D]), ALU.mult)\
                    .then_inc(normed, 1)

            def make_hub(b):
                pool.wait_ge(u_ready, b + 1)
                chain(pool.tensor_tensor(h_all[:, b, :, :], h_all[:, b, :, :], u[:, :, :], ALU.add))
                chain.sync()
                pool.tensor_tensor(h_all[:, b, :, :], h_all[:, b, :, :],
                                   bf_rep[0:P, :].unsqueeze(1).to_broadcast([P, T, D]), ALU.add).then_inc(hub_ready, 1)

            def low_part(parts, k, mid_ready, parts_ready, turn):
                pool.wait_ge(mid_ready, turn + 1)
                pool.tensor_tensor(parts[:, 2, :], rest[k][:, :], parts[:, 1, :], ALU.subtract).then_inc(parts_ready, 1)

            def low_parts(turn):
                low_part(qparts, "q", q_mid_ready, q_parts_ready, turn)
                low_part(kparts, "k", k_mid_ready, k_parts_ready, turn)

            def make_base(b):
                pool.wait_ge(w_ready, b + 1)
                wait(pool, out_ready, 3 * b)
                pool.tensor_tensor(base[:, :, :], h2[:, :, :], w[:, :, :], ALU.add).then_inc(base_ready, 1)

            def gelu_arg(body, c, g):
                Job(body, f"C{3 + g}", c).wait_drained(pool)
                chain(pool.tensor_tensor(hT[g][:, :], hz[g][:, :], hz[g][:, :], ALU.mult))
                chain.sync()
                chain(pool.tensor_scalar(hT[g][:, :], hT[g][:, :], 0.044715, 1.0, ALU.mult, ALU.add))
                chain.sync()
                pool.tensor_tensor(hT[g][:, :], hT[g][:, :], hz[g][:, :], ALU.mult).then_inc(gelu_arg_ready, 1)

            def find_edge(b):
                pool.wait_ge(cand_ready, b + 1)
                settle(pool)
                pool.partition_all_reduce(edge[:, 1:2], edge[:, 0:1], P, RMAX).then_inc(edge_ready, 1)

            def finish(body, c, b):
                pool.wait_ge(take_ready, b + 1)
                Job(body, "C5", c).wait_drained(pool)
                wait(pool, stored, 48 * b)
                for k in range(3):
                    if k:
                        pool.wait_ge(out_ready, 3 * b + k)
                    else:
                        wait(pool, out_ready, 3 * b)
                    chain(pool.tensor_tensor(o_c[k][:, :, :], ys[:, :, :],
                                             take[:, k, :].unsqueeze(2).to_broadcast([P, T, D]), ALU.mult))
                    chain.sync()
                    pool.tensor_tensor(o_c[k][:, :, :], o_c[k][:, :, :], base[:, :, :], ALU.add).then_inc(out_ready, 1)

            def prologue():
                find_rstd("p", 0, PI).then_inc(rstd_ready, 1)
                gather(0, range(NS))
                finish_norm("x", 0, x2, PI, x_normed)
                finish_norm("y", 0, y2, PI, y_normed)
                finish_norm("u", 0, u, P, u_ready)
                finish_norm("n", 0, n2, P, n_ready)
                make_hub(0)
                low_parts(0)
                find_rstd("p", 1, PI).then_inc(rstd_ready, 1)
                gather(1, range(0, NS // 2))

            def iteration(body, b, nxt, prev):
                chain.restart()
                if nxt:
                    finish_norm("x", b + 1, x2, PI, x_normed)
                    gather(b + 1, range(NS // 2, NS))
                else:
                    pool.wait_ge(rows_in, 16 * (NS * B + NS // 2))
                if prev:
                    finish_norm("w", b - 1, w, P, w_ready)
                low_parts(2 * b + 1)
                if nxt:
                    finish_norm("y", b + 1, y2, PI, y_normed)
                if prev:
                    make_base(b - 1)
                if nxt:
                    find_rstd("p", b + 2, PI).then_inc(rstd_ready, 1)
                if prev:
                    gelu_arg(body, b, 0)
                    gelu_arg(body, b, 1)
                if nxt:
                    finish_norm("u", b + 1, u, P, u_ready)
                    finish_norm("n", b + 1, n2, P, n_ready)
                    make_hub(b + 1)
                if prev:
                    find_edge(b - 1)
                if nxt:
                    low_parts(2 * b + 2)
                    gather(b + 2, range(0, NS // 2))
                if prev:
                    finish(body, b, b - 1)
                chain.restart()

            def epilogue(body, b):
                finish_norm("w", b, w, P, w_ready)
                make_base(b)
                gelu_arg(body, b, 0)
                gelu_arg(body, b, 1)
                find_edge(b)
                finish(body, b, b)

            run(pool, iteration, prologue, epilogue)

        @block.scalar
        def _(act):
            chain = Chain(act, "act_chain")

            def copy(dst, src, **kw):
                return act.activation(dst, src, ACT.Copy, **kw)

            def evict(body, name, b, dst, rows_, parts):
                j = Job(body, name, b)
                j.wait_filled(act)
                j.drain(fold(copy, dst, j.tile, rows_, parts))

            def prepare_weights():
                act.wait_ge(consts_ready, 1)
                act.wait_ge(weights_in, 16 * (NW + 7))
                for k in range(2):
                    chain(act.activation(w1[0:FC, k, :], w1_raw[:, k, :], ACT.Copy, scale=ln1_gb[:, k, 0:1]))
                chain(act.activation(wp1[0:D, :], wp1_raw[:, :], ACT.Copy, scale=col[0:D, 0:1]))
                chain(act.activation(wp2[0:D, :], wp2[0:D, :], ACT.Copy, scale=0.5))
                chain(act.activation(wy[:, :, :], wy[:, :, :], ACT.Copy, scale=0.5))
                chain(copy(wroute[0:D + 1, :], col[0:D + 1, 7:8].to_broadcast([D + 1, P])))
                j = Job("prologue", "W1", 0)
                j.wait_filled(act)
                chain(copy(qkv_t[:, :], j.tile[0:D, 0:3 * INNER]))
                chain.sync()
                chain(act.activation(col[0:D, 6:7], col[0:D, 4:5], ACT.Copy, scale=float(DH) ** -0.5))
                chain.sync()
                chain(act.activation(wqkv[0:D, 0:INNER], qkv_t[:, 0:INNER], ACT.Copy, scale=col[0:D, 6:7]))
                j.drain(act.activation(wqkv[0:D, INNER:3 * INNER], qkv_t[:, INNER:3 * INNER], ACT.Copy,
                                       scale=col[0:D, 4:5]))
                j = Job("prologue", "W2", 0)
                j.wait_filled(act)
                j.drain(copy(wgate[0:D, :], j.tile[0:D, 0:INNER]))
                j = Job("prologue", "W3", 0)
                j.wait_filled(act)
                j.drain(act.activation(wfinal[:, :, :], j.tile[:, 0:2 * D].rearrange("p (k n) -> p k n", k=2),
                                       ACT.Copy, scale=0.5))
                j = Job("prologue", "W4", 0)
                j.wait_filled(act)
                chain(act.activation(wqkv[D:D + 1, 0:INNER], j.tile[0:1, 0:INNER], ACT.Copy,
                                     scale=float(DH) ** -0.5))
                j.drain(copy(wqkv[D:D + 1, INNER:3 * INNER], j.tile[0:1, INNER:3 * INNER]))
                j = Job("prologue", "W7", 0)
                j.wait_filled(act)
                found = j.tile[0:L, 0:NS * B].rearrange("p (n b) -> p n b", n=NS)
                chain(copy(ids[:, :, B:B + 1], found[:, :, 0:1]))
                chain.sync()
                j.drain(copy(ids[:, :, 0:B], found))

            def evict_patches(body, name, b, k):
                evict(body, name, b, pnT[0:FC, k, :], FC, PI)

            def silu_in(body, b):
                j = Job(body, "A6", b)
                j.wait_filled(act)
                j.drain(fold(lambda o, i: act.activation(o, i, ACT.Identity, scale=col[0:D, 2:3], bias=col[0:D, 3:4]),
                             zT[:, :], j.tile, D, PI))

            def silu_tanh(body, b):
                Job(body, "A6", b).wait_drained(act)
                act.activation(x3T[0:D, :], zT[:, :], ACT.Tanh, scale=0.5).then_inc(silu_in_ready, 1)

            def evict_tokens(body, b, dst_b):
                j = Job(body, "A7", b)
                j.wait_filled(act)
                j.drain(copy(h_all[0:PI, dst_b, :, :], j.tile[0:PI, 0:T * D].rearrange("p (t d) -> p t d", t=T)))

            def evict_embedded(body, name, c):
                j = Job(body, name, c)
                j.wait_filled(act)
                j.drain(copy(x2[0:PI, :, :], j.tile[0:PI, 0:T * D].rearrange("p (t d) -> p t d", t=T)))
                j.wait_drained(act)
                act.sem_inc(embedded[name[1]])

            def evict_query_key(body, b, k, g, turn):
                j = Job(body, f"{k}{g}", b)
                j.wait_filled(act)
                wait(act, {"q": q_placed, "k": k_placed}[k], 16 * HQ * len(PARTS) * turn)
                if g == 0:
                    wait(act, gelu_ready, 2 * b)
                j.drain(copy(rest[k][:, :], j.tile[:, 0:NU]))

            def top_part(body, b, k, g):
                Job(body, f"{k}{g}", b).wait_drained(act)
                parts, ready = {"q": (qparts, q_top_ready), "k": (kparts, k_top_ready)}[k]
                copy(parts[:, 0, :], rest[k][:, :]).then_inc(ready, 1)

            def mid_part(k, turn):
                parts, rest_ready, ready = {"q": (qparts, q_rest_ready, q_mid_ready),
                                            "k": (kparts, k_rest_ready, k_mid_ready)}[k]
                act.wait_ge(rest_ready, turn + 1)
                copy(parts[:, 1, :], rest[k][:, :]).then_inc(ready, 1)

            def evict_values(body, b, g):
                j = Job(body, f"v{g}", b)
                j.wait_filled(act)
                j.drain(act.activation(v[g][:, :, :], j.tile[0:P, 0:T * HQ * DH].rearrange("p (t n) -> p t n", t=T),
                                       ACT.Copy, scale=v_weight[0:P, :]))

            def gates(body, b, g):
                j = Job(body, f"g{g}", b)
                j.wait_filled(act)
                j.drain(act.activation(gate[g][:, :], j.tile[:, 0:NU], ACT.Tanh, scale=0.5))

            def exp_scores(body, b, s, h):
                j = Job(body, f"s{s}.{h}", b)
                act.wait_ge(negmax_ready, (b * STEPS + s) * HQ + h + 1)
                j.drain(act.activation(e[:, s % 2, h, :, :], j.tile[0:P, 0:NU].rearrange("p (t q) -> p t q", t=T),
                                       ACT.Exp, bias=negmax[:, s % 2, h:h + 1], accum_out=s_all[:, s % 2, h:h + 1]))

            def gelu_z(body, c, g, turn):
                j = Job(body, f"C{3 + g}", c)
                j.wait_filled(act)
                act.wait_ge((q_parts_ready, k_parts_ready)[g], turn)
                j.drain(copy(hz[g][:, :], j.tile[:, 0:NU]))

            def gelu_tanh(b, g):
                act.wait_ge(gelu_arg_ready, 2 * b + g + 1)
                act.activation(hT[g][:, :], hT[g][:, :], ACT.Tanh, scale=0.7978845608028654).then_inc(gelu_tanh_ready, 1)

            def evict_route(body, c, b):
                j = Job(body, "C2", c)
                j.wait_filled(act)
                wait(act, cand_ready, b)
                j.drain(copy(route[:, :], j.tile[0:P, 0:NU]))

            def evict_counts(body, c):
                j = Job(body, "C7", c)
                j.wait_filled(act)
                j.drain(copy(route[0:1, :], j.tile[0:1, 0:NU]))

            def prologue():
                prepare_weights()
                evict_patches("prologue", "P1", 0, 0)
                evict_patches("prologue", "P2", 0, 1)
                evict_embedded("prologue", "P3", 0)
                evict("prologue", "A4", 0, x2T[0:D, :], D, PI)
                evict_embedded("prologue", "A5", 0)
                silu_in("prologue", 0)
                silu_tanh("prologue", 0)
                evict_tokens("prologue", 0, 0)
                evict("prologue", "A8", 0, uT[0:D, :], D, P)
                evict("prologue", "A9", 0, nT[0:D, :], D, P)
                evict_query_key("prologue", 0, "q", 0, 0)
                evict_query_key("prologue", 0, "k", 0, 0)
                top_part("prologue", 0, "q", 0)
                top_part("prologue", 0, "k", 0)
                evict_values("prologue", 0, 0)
                mid_part("q", 0)
                mid_part("k", 0)
                evict_patches("prologue", "A1", 0, 0)
                evict_patches("prologue", "A2", 0, 1)
                evict_embedded("prologue", "A3", 0)

            def iteration(body, b, nxt, prev):
                chain.restart()
                for s in range(STEPS):
                    for h in range(HQ):
                        at = (s, h)
                        exp_scores(body, b, s, h)
                        if at == (0, 1):
                            evict_query_key(body, b, "q", 1, 2 * b + 1)
                        if at == (0, 3):
                            top_part(body, b, "q", 1)
                        if at == (1, 0):
                            evict_query_key(body, b, "k", 1, 2 * b + 1)
                        if at == (1, 1):
                            top_part(body, b, "k", 1)
                        if at == (2, 1):
                            mid_part("q", 2 * b + 1)
                        if at == (2, 2):
                            mid_part("k", 2 * b + 1)
                        if at == (3, 1):
                            evict_values(body, b, 1)
                        if at == (5, 1):
                            gates(body, b, 1)
                        if at == (6, 2):
                            gates(body, b, 0)
                        if prev:
                            if at == (3, 3):
                                evict(body, "C1", b, wT[0:D, :], D, P)
                            if at == (4, 1):
                                evict_route(body, b, b - 1)
                            if at == (4, 2):
                                gelu_z(body, b, 0, 2 * b + 2)
                            if at == (5, 2):
                                gelu_z(body, b, 1, 2 * b + 2)
                            if at == (7, 1):
                                gelu_tanh(b - 1, 0)
                            if at == (8, 1):
                                gelu_tanh(b - 1, 1)
                            if at == (8, 3):
                                evict_counts(body, b)
                        if nxt:
                            if at == (2, 0):
                                evict(body, "A4", b, x2T[0:D, :], D, PI)
                            if at == (2, 3):
                                evict_embedded(body, "A5", b)
                            if at == (4, 3):
                                silu_in(body, b)
                            if at == (5, 0):
                                silu_tanh(body, b)
                            if at == (6, 0):
                                evict_tokens(body, b, b + 1)
                            if at == (8, 0):
                                evict(body, "A8", b, uT[0:D, :], D, P)
                            if at == (8, 2):
                                evict(body, "A9", b, nT[0:D, :], D, P)
                            if at == (9, 1):
                                evict_query_key(body, b, "q", 0, 2 * b + 2)
                            if at == (9, 2):
                                top_part(body, b, "q", 0)
                            if at == (9, 3):
                                evict_query_key(body, b, "k", 0, 2 * b + 2)
                            if at == (10, 0):
                                top_part(body, b, "k", 0)
                            if at == (10, 1):
                                mid_part("q", 2 * b + 2)
                            if at == (10, 2):
                                evict_values(body, b, 0)
                            if at == (10, 3):
                                mid_part("k", 2 * b + 2)
                            if at == (12, 0):
                                evict_patches(body, "A1", b, 0)
                            if at == (12, 1):
                                evict_patches(body, "A2", b, 1)
                            if at == (13, 0):
                                evict_embedded(body, "A3", b)
                chain.restart()

            def epilogue(body, b):
                evict(body, "C1", b, wT[0:D, :], D, P)
                evict_route(body, b, b)
                gelu_z(body, b, 0, 2 * b + 2)
                gelu_z(body, b, 1, 2 * b + 2)
                gelu_tanh(b, 0)
                gelu_tanh(b, 1)
                evict_counts(body, b)

            run(act, iteration, prologue, epilogue)

        @block.vector
        def _(dve):
            chain = Chain(dve, "dve_chain")

            def stats(k, src, parts, tiles=range(T)):
                for t in tiles:
                    chain(dve.bn_stats(st[k][0:parts, t, :], src(t)))

            def moments(k, b, parts):
                chain.sync()
                for t in range(T):
                    ins = dve.bn_aggr(mv[k][0:parts, t, :], st[k][0:parts, t, :])
                    if t < T - 1:
                        chain(ins)
                ins.then_inc(var_ready[k], 1)

            def center(k, b, dst, src, parts):
                moments(k, b, parts)
                chain.sync()
                dve.wait_ge(var_ready[k], b + 1)
                dve.tensor_tensor(dst[0:parts, :, :], src, mv[k][0:parts, :, 0:1].to_broadcast([parts, T, D]),
                                  ALU.subtract).then_inc(centered[k], 1)

            patch_tile = lambda t: patches[:, :, :, PS * t:PS * t + PS].rearrange("p c y x -> p (c y) x")

            def patch_stats(b, tiles):
                dve.wait_ge(patches_in, 16 * QW * C * (b + 1))
                stats("p", patch_tile, PI, tiles)

            def patch_norm(b, tiles):
                dve.wait_ge(rstd_ready, b + 1)
                for t in tiles:
                    ins = dve.tensor_scalar(pn[:, t, :].rearrange("p (f x) -> p f x", x=PS), patch_tile(t),
                                            mv["p"][0:PI, t, 0:1], rstd["p"][0:PI, t:t + 1], ALU.subtract, ALU.mult)
                    if t < T - 1:
                        chain(ins)
                    else:
                        ins.then_inc(patches_normed, 1)

            def embedded_stats(k, name, b):
                dve.wait_ge(embedded[name[1]], b + 1)
                stats(k, lambda t: x2[0:PI, t, :], PI)

            def embedded_center(k, b):
                center(k, b, x2, x2[0:PI, :, :], PI)

            def silu_product(b):
                dve.wait_ge(silu_in_ready, b + 1)
                dve.scalar_tensor_tensor(out=x3T[0:D, :], in0=x3T[0:D, :], scalar=1.0, in1=zT[:, :],
                                         op0=ALU.add, op1=ALU.mult).then_inc(silu_ready, 1)

            def pick_ids(b):
                wait(dve, rows_in, 16 * NS * b)
                dve.tensor_copy(ids_now[:, :], ids[:, :, b]).then_inc(ids_now_ready, 1)

            def sum_text(b):
                dve.wait_ge(rows_in, 16 * NS * (b + 1))
                wait(dve, text_placed, 16 * T * b)
                chain(dve.tensor_reduce(out=text[:, :], in_=rows[:, :, :].rearrange("p n d -> p d n"), axis=AX.X, op=ALU.add))
                chain.sync()
                dve.tensor_scalar(text[:, :], text[:, :], 1.0 / (NS + 1), None, ALU.mult).then_inc(text_ready, 1)

            def u_stats(body, c, b):
                Job(body, "A7", c).wait_drained(dve)
                dve.wait_ge(text_placed, 16 * T * (b + 1))
                wait(dve, hub_ready, b)
                stats("u", lambda t: h_all[:, b, t, :], P)

            def u_center(b):
                center("u", b, u, h_all[:, b, :, :], P)

            def n_stats(b):
                dve.wait_ge(u_ready, b + 1)
                stats("n", lambda t: u[:, t, :], P)

            def n_center(b):
                center("n", b, n2, u[:, :, :], P)

            def rests(k, turn):
                parts, top_ready, rest_ready = {"q": (qparts, q_top_ready, q_rest_ready),
                                                "k": (kparts, k_top_ready, k_rest_ready)}[k]
                dve.wait_ge(top_ready, turn + 1)
                dve.tensor_tensor(rest[k][:, :], rest[k][:, :], parts[:, 0, :], ALU.subtract).then_inc(rest_ready, 1)

            def maximum(body, b, s, h):
                j = Job(body, f"s{s}.{h}", b)
                j.wait_filled(dve)
                dve.tensor_reduce(out=negmax[:, s % 2, h:h + 1], in_=j.tile[0:P, 0:NU], axis=AX.X, op=ALU.max,
                                  negate=True).then_inc(negmax_ready, 1)

            def text_sums(body, b, s):
                if s == STEPS - 1:
                    dve.wait_ge(drained[SLOTS - 1], uses_before(body, SLOTS - 1, b))
                else:
                    Job(body, f"s{s}.{HQ - 1}", b).wait_drained(dve)
                chain(dve.tensor_reduce(out=s_txt[:, s % 2, :], in_=e[:, s % 2, :, :, PI:P], axis=AX.XY, op=ALU.add))

            def denominators(s):
                r = s % 2
                chain.sync()
                chain(dve.scalar_tensor_tensor(out=den[:, r, :], in0=s_all[:, r, :], scalar=1.5, in1=s_txt[:, r, :],
                                               op0=ALU.mult, op1=ALU.subtract))

            def reciprocals(s):
                chain.sync()
                chain(dve.reciprocal(rden[:, s % 2, :], den[:, s % 2, :]))

            def scale_values(s):
                g, t, r = s // T, s % T, s % 2
                chain.sync()
                dve.tensor_tensor(vs[:, r, :, :], v[g][:, t, :].rearrange("p (h d) -> p h d", h=HQ),
                                  rden[:, r, :].unsqueeze(2).to_broadcast([P, HQ, DH]), ALU.mult).then_inc(vs_ready, 1)

            def gate_output(b, g):
                dve.wait_ge(av_done, b * STEPS + T * (g + 1))
                dve.scalar_tensor_tensor(out=og[g][:, :], in0=gate[g][:, :], scalar=1.0, in1=o_acc[:, 0:NU],
                                         op0=ALU.add, op1=ALU.mult).then_inc(o_drained, 1)

            def add_residual(body, c, b):
                j = Job(body, "F", c)
                j.wait_filled(dve)
                dve.wait_ge(hub_ready, b + 1)
                wait(dve, base_ready, b)
                j.drain(dve.tensor_tensor(h2[:, :, :], j.tile[0:P, 0:T * D].rearrange("p (t d) -> p t d", t=T),
                                          h_all[:, b, :, :], ALU.add))

            def w_stats(body, c):
                Job(body, "F", c).wait_drained(dve)
                stats("w", lambda t: h2[:, t, :], P)

            def w_center(b):
                center("w", b, w, h2[:, :, :], P)

            def own_route(body, c, b):
                j = Job(body, "C2b", c)
                j.wait_filled(dve)
                wait(dve, take_ready, b)
                j.drain(dve.tensor_copy(w_tok[:, :], j.tile[0:P, 0:T]))
                j.wait_drained(dve)
                dve.sem_inc(own_route_ready)

            def compare(b, tiles, quads):
                dve.wait_ge(own_route_ready, b + 1)
                for t in tiles:
                    if t < T - 1:
                        dve.wait_ge((q_placed, k_placed)[t // 3], 16 * HQ * len(PARTS) * quads)
                    dve.tensor_scalar(less[t], route[:, :], w_tok[:, t:t + 1], None, ALU.is_lt).then_inc(less_ready, 1)

            def candidates(body, c, b):
                j = Job(body, "C8", c)
                j.wait_filled(dve)
                j.drain(dve.tensor_scalar(above_cnt[:, :], j.tile[0:P, 0:T], 1.0, None, ALU.add))
                j.wait_drained(dve)
                chain(dve.scalar_tensor_tensor(out=cand[:, :], in0=above_cnt[:, :], scalar=float(SEL), in1=above_cnt[:, :],
                                               op0=ALU.is_le, op1=ALU.mult))
                chain.sync()
                dve.tensor_reduce(out=edge[:, 0:1], in_=cand[:, :], axis=AX.X, op=ALU.max).then_inc(cand_ready, 1)

            def tied_tokens(b):
                dve.wait_ge(edge_ready, b + 1)
                chain(dve.tensor_scalar(above[:, :], above_cnt[:, :], edge[:, 1:2], None, ALU.is_lt))
                chain(dve.tensor_scalar(tied[:, :], above_cnt[:, :], edge[:, 1:2], None, ALU.is_equal))
                chain.sync()
                dve.tensor_reduce(out=tied_sum[:, :], in_=tied[:, :], axis=AX.X, op=ALU.add).then_inc(tied_ready, 1)

            def selection(body, c, b):
                j = Job(body, "C6", c)
                j.wait_filled(dve)
                j.drain(dve.tensor_copy(ties[:, :], j.tile[0:P, 0:2]))
                j.wait_drained(dve)
                chain(dve.tensor_tensor_scan(out=tie_no[:, :], data0=tied[:, :], data1=zeros7[0:P, :],
                                             initial=ties[:, 0:1], op0=ALU.add, op1=ALU.add))
                chain(dve.tensor_scalar(limit[:, 0:1], edge[:, 1:2], -1.0, float(SEL + 1), ALU.mult, ALU.add))
                chain.sync()
                chain(dve.tensor_tensor(limit[:, 1:2], limit[:, 0:1], ties[:, 1:2], ALU.subtract))
                chain(dve.tensor_tensor(tie_no[:, :], tie_no[:, :], tied[:, :], ALU.subtract))
                chain.sync()
                chain(dve.tensor_tensor(limit[:, 2:3], limit[:, 1:2], ties[:, 1:2], ALU.subtract))
                chain.sync()
                for k in range(3):
                    chain(dve.scalar_tensor_tensor(out=take[:, k, :], in0=tie_no[:, :], scalar=limit[:, k:k + 1],
                                                   in1=tied[:, :], op0=ALU.is_lt, op1=ALU.mult))
                chain.sync()
                chain(dve.tensor_tensor(take[:, :, :], take[:, :, :], above[:, :].unsqueeze(1).to_broadcast([P, 3, T]), ALU.add))
                chain.sync()
                dve.tensor_tensor(take[:, :, :], take[:, :, :], w_tok[:, :].unsqueeze(1).to_broadcast([P, 3, T]), ALU.mult)\
                    .then_inc(take_ready, 1)

            def gelu_product(b, g):
                dve.wait_ge(gelu_tanh_ready, 2 * b + g + 1)
                dve.scalar_tensor_tensor(out=hT[g][:, :], in0=hT[g][:, :], scalar=1.0, in1=hz[g][:, :],
                                         op0=ALU.add, op1=ALU.mult).then_inc(gelu_ready, 1)

            def ffn_output(body, c, b):
                j = Job(body, "C5", c)
                j.wait_filled(dve)
                wait(dve, out_ready, 3 * b)
                j.drain(dve.tensor_tensor(ys[:, :, :], j.tile[0:P, 0:T * D].rearrange("p (t d) -> p t d", t=T),
                                          b2_rep[0:P, :].unsqueeze(1).to_broadcast([P, T, D]), ALU.add))

            def hash_text():
                dve.wait_ge(text_in, 16)
                dve.wait_ge(consts_ready, 1)
                chain(dve.tensor_copy(tokf[:, :], tok_raw[:, :]))
                chain.sync()
                chain(dve.tensor_scalar(ok[:, :], tokf[:, :], 1.0, None, ALU.is_ge))
                chain(dve.tensor_scalar(ok2[:, :], tokf[:, :], 4.0, None, ALU.is_le))
                chain.sync()
                chain(dve.tensor_tensor(ok[:, :], ok[:, :], ok2[:, :], ALU.mult))
                chain.sync()
                chain(dve.scalar_tensor_tensor(out=safe[:, :], in0=tokf[:, :], scalar=-1.0, in1=ok[:, :],
                                               op0=ALU.add, op1=ALU.mult))
                chain(dve.tensor_scalar(bad1[:, :], ok[:, :], -1.0, 1.0, ALU.mult, ALU.add))
                chain.sync()
                chain(dve.tensor_copy(hash_i[:, 1, :], safe[:, :]))
                chain(dve.tensor_copy(bad[:, 1, :], bad1[:, :]))
                chain.sync()
                for k in range(2, SIZES[-1] + 1):
                    now, last = k % 2, (k + 1) % 2
                    chain(dve.scalar_tensor_tensor(out=hash_i[:, now, 1:L], in0=hash_i[:, last, 0:L - 1],
                                                   scalar=float(PRIME), in1=safe[:, 1:L], op0=ALU.mult, op1=ALU.add))
                    chain(dve.tensor_copy(hash_i[:, now, 0:1], safe[:, 0:1]))
                    chain(dve.tensor_tensor(bad[:, now, 1:L], bad[:, last, 0:L - 1], bad1[:, 1:L], ALU.max))
                    chain(dve.memset(bad[:, now, 0:1], 1.0))
                    chain.sync()
                    chain(dve.tensor_scalar(hash_i[:, now, :], hash_i[:, now, :], TBL - 1, None, ALU.bitwise_and))
                    chain.sync()
                    if k in SIZES:
                        n = k - SIZES[0]
                        chain(dve.scalar_tensor_tensor(out=ids_f[:, n, :], in0=bad[:, now, :], scalar=float(TBL),
                                                       in1=hash_i[:, now, :], op0=ALU.mult, op1=ALU.max))
                        chain.sync()
                        ins = dve.tensor_scalar(ids_f[:, n, :], ids_f[:, n, :], float(n * (TBL + 1)), None, ALU.add)
                        if n == NS - 1:
                            ins.then_inc(ids_f_ready, 1)
                        else:
                            chain(ins)

            def bias_rows():
                dve.wait_ge(weights_in, 16 * (NW + 7))
                j = Job("prologue", "W5", 0)
                j.wait_filled(dve)
                j.drain(dve.tensor_tensor(w1[FC:FC + 1, 1, :], j.tile[0:1, 0:D], row[0:1, 0:D], ALU.add))
                j = Job("prologue", "W6", 0)
                j.wait_filled(dve)
                j.drain(dve.tensor_tensor(wp1[D:D + 1, :], j.tile[0:1, 0:D], row[0:1, D:2 * D], ALU.add))

            def prologue():
                patch_stats(0, range(T))
                moments("p", 0, PI)
                hash_text()
                patch_norm(0, range(T))
                bias_rows()
                Job("prologue", "W7", 0).wait_drained(dve)
                pick_ids(0)
                embedded_stats("x", "P3", 0)
                embedded_center("x", 0)
                embedded_stats("y", "A5", 0)
                embedded_center("y", 0)
                silu_product(0)
                sum_text(0)
                u_stats("prologue", 0, 0)
                u_center(0)
                n_stats(0)
                n_center(0)
                rests("q", 0)
                rests("k", 0)
                patch_stats(1, range(T))
                moments("p", 1, PI)
                pick_ids(1)
                patch_norm(1, range(T))

            def iteration(body, b, nxt, prev):
                chain.restart()
                for s in range(STEPS):
                    last = s - 1 if s else STEPS - 1 if prev else None
                    for h in range(HQ):
                        at = (s, h)
                        maximum(body, b, s, h)
                        if last is not None:
                            if h == 0:
                                text_sums(body, b, last)
                                denominators(last)
                            if h == 1:
                                reciprocals(last)
                                scale_values(last)
                        if nxt:
                            if at == (0, 2):
                                embedded_stats("x", "A3", b + 1)
                            if at == (0, 3):
                                embedded_center("x", b + 1)
                            if at == (3, 2):
                                embedded_stats("y", "A5", b + 1)
                            if at == (3, 3):
                                embedded_center("y", b + 1)
                            if at == (4, 0):
                                sum_text(b + 1)
                            if at == (4, 2):
                                patch_stats(b + 2, range(0, T // 2))
                            if at == (4, 3):
                                patch_stats(b + 2, range(T // 2, T))
                            if at == (5, 0):
                                moments("p", b + 2, PI)
                            if at == (5, 2):
                                silu_product(b + 1)
                            if at == (6, 2):
                                u_stats(body, b, b + 1)
                            if at == (6, 3):
                                u_center(b + 1)
                            if at == (7, 2):
                                n_stats(b + 1)
                            if at == (7, 3):
                                n_center(b + 1)
                            if at == (9, 3):
                                rests("q", 2 * b + 2)
                            if at == (10, 2):
                                rests("k", 2 * b + 2)
                            if at == (10, 3):
                                pick_ids(b + 2)
                            if at == (11, 1):
                                patch_norm(b + 2, range(0, T // 2))
                            if at == (11, 2):
                                patch_norm(b + 2, range(T // 2, T))
                        if at == (1, 2):
                            rests("q", 2 * b + 1)
                        if at == (2, 1):
                            rests("k", 2 * b + 1)
                        if at == (8, 0):
                            gate_output(b, 0)
                        if prev:
                            if at == (1, 0):
                                gate_output(b - 1, 1)
                            if at == (1, 3):
                                add_residual(body, b, b - 1)
                            if at == (2, 2):
                                w_stats(body, b)
                            if at == (2, 3):
                                w_center(b - 1)
                            if at == (5, 1):
                                own_route(body, b, b - 1)
                            if at == (5, 3):
                                compare(b - 1, range(0, 1), 2 * b + 2)
                            if at == (6, 1):
                                compare(b - 1, range(1, 3), 2 * b + 2)
                            if at == (7, 0):
                                compare(b - 1, range(3, 4), 2 * b + 2)
                            if at == (7, 1):
                                compare(b - 1, range(4, 6), 2 * b + 2)
                            if at == (8, 1):
                                compare(b - 1, range(6, 7), 2 * b + 2)
                            if at == (8, 2):
                                gelu_product(b - 1, 0)
                            if at == (8, 3):
                                gelu_product(b - 1, 1)
                            if at == (9, 2):
                                ffn_output(body, b, b - 1)
                            if at == (10, 0):
                                candidates(body, b, b - 1)
                            if at == (11, 0):
                                tied_tokens(b - 1)
                            if at == (11, 3):
                                selection(body, b, b - 1)
                chain.restart()

            def epilogue(body, b):
                text_sums(body, b, STEPS - 1)
                denominators(STEPS - 1)
                reciprocals(STEPS - 1)
                scale_values(STEPS - 1)
                gate_output(b, 1)
                add_residual(body, b, b)
                w_stats(body, b)
                w_center(b)
                own_route(body, b, b)
                compare(b, range(T), 2 * b + 2)
                gelu_product(b, 0)
                gelu_product(b, 1)
                ffn_output(body, b, b)
                candidates(body, b, b)
                tied_tokens(b)
                selection(body, b, b)

            run(dve, iteration, prologue, epilogue)

        @block.tensor
        def _(pe):
            def job(body, name, c):
                j = Job(body, name, c)
                j.wait_free(pe)
                return j

            def transposes(j, src, parts, cols):
                settle(pe)
                for t in range(T):
                    a = tile_col(t, parts)
                    ins = pe.transpose(j.tile[0:cols, a:a + parts], src(t), ident[0:parts, 0:parts])
                j.fill(ins)

            def project(j, rows_, weights, xT):
                for a, z in pieces(NU):
                    ins = pe.matmul(j.tile[0:rows_, a:z], weights, xT[:, a:z], start=True, stop=True)
                j.fill(ins)

            def token_major(j, parts, pairs):
                for t in range(T):
                    for i, (xT, weights) in enumerate(pairs):
                        ins = pe.matmul(j.tile[0:parts, t * D:t * D + D], xT[:, t * parts:(t + 1) * parts], weights,
                                        start=(i == 0), stop=(i == len(pairs) - 1))
                j.fill(ins)

            def weight_jobs():
                pe.wait_ge(consts_ready, 1)
                pe.wait_ge(weights_in, 16 * (NW + 7))
                j = job("prologue", "W1", 0)
                for k in range(6):
                    ins = pe.transpose(j.tile[0:D, k * 128:(k + 1) * 128], raw_qkv[:, k, :], ident[:, :])
                j.fill(ins)
                j = job("prologue", "W2", 0)
                for k in range(2):
                    ins = pe.transpose(j.tile[0:D, k * 128:(k + 1) * 128], raw_gate[:, k, :], ident[:, :])
                j.fill(ins)
                j = job("prologue", "W3", 0)
                for k in range(2):
                    ins = pe.transpose(j.tile[:, k * D:(k + 1) * D], raw_final[:, k * 128:(k + 1) * 128], ident[0:D, 0:D])
                j.fill(ins)
                Job("prologue", "W1", 0).wait_drained(pe)
                j = job("prologue", "W4", 0)
                for a, z in pieces(3 * INNER):
                    ins = pe.matmul(j.tile[0:1, a:z], col[0:D, 5:6], qkv_t[:, a:z], start=True, stop=True)
                j.fill(ins)
                j = job("prologue", "W5", 0)
                for k in range(2):
                    ins = pe.matmul(j.tile[0:1, 0:D], ln1_gb[:, k, 1:2], w1_raw[:, k, :], start=(k == 0), stop=(k == 1))
                j.fill(ins)
                j = job("prologue", "W6", 0)
                j.fill(pe.matmul(j.tile[0:1, 0:D], col[0:D, 1:2], wp1_raw[:, :], start=True, stop=True))
                pe.wait_ge(ids_f_ready, 1)
                j = job("prologue", "W7", 0)
                for n in range(NS):
                    ins = pe.transpose(j.tile[0:L, n * B:(n + 1) * B], ids_f[:, n, :], ident[0:B, 0:B])
                j.fill(ins)
                for name in ("W4", "W5", "W6"):
                    Job("prologue", name, 0).wait_drained(pe)

            def patch_transposes(body, names, c, b):
                pe.wait_ge(patches_normed, b + 1)
                for name in names:
                    k = int(name[1]) - 1
                    transposes(job(body, name, c), lambda t: pn[:, t, k * FC:(k + 1) * FC], PI, FC)

            def embed(body, names, c):
                Job(body, names[0], c).wait_drained(pe)
                token_major(job(body, names[1], c), PI, [(pnT[0:FC, 0, :], w1[0:FC, 0, :]), (pnT[:, 1, :], w1[:, 1, :])])

            def x2_transposes(body, c, b):
                pe.wait_ge(x_normed, b + 1)
                transposes(job(body, "A4", c), lambda t: x2[0:PI, t, :], PI, D)

            def pool_in(body, c):
                Job(body, "A4", c).wait_drained(pe)
                token_major(job(body, "A5", c), PI, [(x2T[:, :], wp1[:, :])])

            def y2_transposes(body, c, b):
                pe.wait_ge(y_normed, b + 1)
                transposes(job(body, "A6", c), lambda t: y2[0:PI, t, :], PI, D)

            def pool_out(body, c, b):
                pe.wait_ge(silu_ready, b + 1)
                token_major(job(body, "A7", c), PI, [(x3T[:, :], wp2[:, :])])

            def u_transposes(body, c, b):
                pe.wait_ge(u_ready, b + 1)
                transposes(job(body, "A8", c), lambda t: u[:, t, :], P, D)

            def n_transposes(body, c, b):
                pe.wait_ge(n_ready, b + 1)
                transposes(job(body, "A9", c), lambda t: n2[:, t, :], P, D)

            def query_key(body, c, k, g):
                if g == 0:
                    Job(body, "A9", c).wait_drained(pe)
                a = "qk".index(k) * INNER + g * 128
                project(job(body, f"{k}{g}", c), 128, wqkv[:, a:a + 128], nT)

            def values(body, c, g):
                j = job(body, f"v{g}", c)
                a = 2 * INNER + g * 128
                for t in range(T):
                    ins = pe.matmul(j.tile[0:P, t * 128:(t + 1) * 128], nT[:, t * P:(t + 1) * P], wqkv[:, a:a + 128],
                                    start=True, stop=True)
                j.fill(ins)

            def gates(body, c, g):
                project(job(body, f"g{g}", c), 128, wgate[:, g * 128:(g + 1) * 128], uT)

            def scores(body, b, s, h):
                g, t = s // T, s % T
                if t == 0 and h == 0:
                    turn = 2 * b + g + 1
                    pe.wait_ge(q_placed, 16 * HQ * len(PARTS) * turn)
                    pe.wait_ge(k_placed, 16 * HQ * len(PARTS) * turn)
                j = job(body, f"s{s}.{h}", b)
                for r in range(2):
                    for a, z in pieces(NU):
                        ins = pe.matmul(j.tile[0:P, a:z], qs[g][:, h, r, t * P:(t + 1) * P], ks[g][:, h, r, a:z],
                                        start=(r == 0), stop=(r == 1))
                j.fill(ins)

            def attend(b, s):
                t, r = s % T, s % 2
                pe.wait_ge(vs_ready, b * STEPS + s + 1)
                if t == 0:
                    wait(pe, o_drained, 2 * b + s // T)
                for a, z in pieces(NU):
                    for h in range(HQ):
                        ins = pe.matmul(o_acc[DH * h:DH * h + DH, a:z], vs[:, r, h, :],
                                        e[:, r, h, :, :].rearrange("p t q -> p (t q)")[:, a:z],
                                        start=(t == 0), stop=(t == T - 1))
                ins.then_inc(av_done, 1)

            def output_projection(body, c, b):
                pe.wait_ge(o_drained, 2 * (b + 1))
                token_major(job(body, "F", c), P, [(og[g][:, :], wfinal[:, g, :]) for g in range(2)])

            def w_transposes(body, c, b):
                pe.wait_ge(w_ready, b + 1)
                transposes(job(body, "C1", c), lambda t: w[:, t, :], P, D)

            def routing(body, c):
                Job(body, "C1", c).wait_drained(pe)
                project(job(body, "C2", c), P, wroute[:, :], wT)

            def hidden(body, c, g):
                project(job(body, f"C{3 + g}", c), 128, wh[:, g * 128:(g + 1) * 128], wT)

            def route_transposes(body, c):
                Job(body, "C2", c).wait_drained(pe)
                j = job(body, "C2b", c)
                settle(pe)
                for t in range(T):
                    ins = pe.transpose(j.tile[0:P, t:t + 1], route[0:1, t * P:(t + 1) * P], ident[0:1, 0:1])
                j.fill(ins)

            def count_heavier(body, c, b):
                pe.wait_ge(less_ready, T * (b + 1))
                j = job(body, "C7", c)
                for a, z in pieces(NU):
                    for t in range(T):
                        ins = pe.matmul(j.tile[0:1, a:z], copies[0:P, :], less[t][:, a:z], start=(t == 0), stop=(t == T - 1))
                j.fill(ins)

            def count_transposes(body, c):
                Job(body, "C7", c).wait_drained(pe)
                j = job(body, "C8", c)
                settle(pe)
                for t in range(T):
                    ins = pe.transpose(j.tile[0:P, t:t + 1], route[0:1, t * P:(t + 1) * P], ident[0:1, 0:1])
                j.fill(ins)

            def ffn_out(body, c, b):
                pe.wait_ge(gelu_ready, 2 * (b + 1))
                token_major(job(body, "C5", c), P, [(hT[g][:, :], wy[:, g, :]) for g in range(2)])

            def count_ties(body, c, b):
                pe.wait_ge(tied_ready, b + 1)
                j = job(body, "C6", c)
                pe.matmul(j.tile[0:P, 0:1], before[0:P, :], tied_sum[:, :], start=True, stop=True)
                j.fill(pe.matmul(j.tile[0:P, 1:2], images[0:P, :], tied_sum[:, :], start=True, stop=True))

            def prologue():
                weight_jobs()
                patch_transposes("prologue", ("P1", "P2"), 0, 0)
                embed("prologue", ("P2", "P3"), 0)
                x2_transposes("prologue", 0, 0)
                pool_in("prologue", 0)
                y2_transposes("prologue", 0, 0)
                pool_out("prologue", 0, 0)
                u_transposes("prologue", 0, 0)
                n_transposes("prologue", 0, 0)
                query_key("prologue", 0, "q", 0)
                query_key("prologue", 0, "k", 0)
                values("prologue", 0, 0)
                patch_transposes("prologue", ("A1", "A2"), 0, 1)
                embed("prologue", ("A2", "A3"), 0)

            def iteration(body, b, nxt, prev):
                for s in range(STEPS):
                    for h in range(HQ):
                        at = (s, h)
                        scores(body, b, s, h)
                        if prev:
                            if at == (1, 2):
                                output_projection(body, b, b - 1)
                            if at == (3, 3):
                                w_transposes(body, b, b - 1)
                            if at == (4, 1):
                                routing(body, b)
                            if at == (4, 2):
                                hidden(body, b, 0)
                            if at == (5, 0):
                                route_transposes(body, b)
                            if at == (5, 2):
                                hidden(body, b, 1)
                            if at == (8, 3):
                                count_heavier(body, b, b - 1)
                            if at == (9, 2):
                                ffn_out(body, b, b - 1)
                            if at == (10, 0):
                                count_transposes(body, b)
                            if at == (11, 2):
                                count_ties(body, b, b - 1)
                        if at == (0, 1):
                            query_key(body, b, "q", 1)
                        if at == (1, 0):
                            query_key(body, b, "k", 1)
                        if at == (3, 1):
                            values(body, b, 1)
                        if at == (5, 1):
                            gates(body, b, 1)
                        if at == (6, 2):
                            gates(body, b, 0)
                        if nxt:
                            if at == (2, 0):
                                x2_transposes(body, b, b + 1)
                            if at == (2, 3):
                                pool_in(body, b)
                            if at == (4, 3):
                                y2_transposes(body, b, b + 1)
                            if at == (6, 0):
                                pool_out(body, b, b + 1)
                            if at == (8, 0):
                                u_transposes(body, b, b + 1)
                            if at == (8, 2):
                                n_transposes(body, b, b + 1)
                            if at == (9, 1):
                                query_key(body, b, "q", 0)
                            if at == (9, 3):
                                query_key(body, b, "k", 0)
                            if at == (10, 2):
                                values(body, b, 0)
                            if at == (12, 0):
                                patch_transposes(body, ("A1",), b, b + 2)
                            if at == (12, 1):
                                patch_transposes(body, ("A2",), b, b + 2)
                            if at == (13, 0):
                                embed(body, ("A2", "A3"), b)
                    if s:
                        attend(b, s - 1)
                    elif prev:
                        attend(b - 1, STEPS - 1)

            def epilogue(body, b):
                attend(b, STEPS - 1)
                output_projection(body, b, b)
                w_transposes(body, b, b)
                routing(body, b)
                hidden(body, b, 0)
                route_transposes(body, b)
                hidden(body, b, 1)
                count_heavier(body, b, b)
                ffn_out(body, b, b)
                count_transposes(body, b)
                count_ties(body, b, b)

            run(pe, iteration, prologue, epilogue)


PARAMETERS = [
    "L0_tok_ln1_g", "L0_tok_ln1_b", "L0_tok_W1", "L0_tok_b1", "L0_tok_ln2_g", "L0_tok_ln2_b", "L0_tok_Wp1",
    "L0_tok_bp1", "L0_tok_lnp_g", "L0_tok_lnp_b", "L0_tok_Wp2", "L0_tok_bp2", "L0_txt_tables", "L0_attn_ln_gamma",
    "L0_attn_ln_beta", "L0_attn_W_qkv", "L0_attn_W_gate", "L0_attn_b_gate", "L0_attn_W_final", "L0_attn_b_final",
    "L0_ffn_wr", "L0_ffn_br", "L0_ffn_w1", "L0_ffn_b1", "L0_ffn_w2", "L0_ffn_b2",
]


def kernel(**inputs):
    import concourse.bacc as bacc
    from concourse.bass_utils import run_bass_kernel_spmd

    nc = bacc.Bacc("TRN2", target_bir_lowering=False, num_devices=1)
    arrays, args = {}, {}
    for name in ["x", "x_txt", *PARAMETERS]:
        a = np.ascontiguousarray(inputs[name])
        arrays[f"in_{name}"] = a
        args[name] = nc.dram_tensor(f"in_{name}", a.shape, mybir.dt.from_np(a.dtype), kind="ExternalInput").ap()
    out = nc.dram_tensor("out", (B, SEQ, D), F32, kind="ExternalOutput").ap()
    build(nc, args["x"], args["x_txt"], args, out)
    result = run_bass_kernel_spmd(nc, [arrays], core_ids=[0])
    return result.results[0]["out"]
```

```python
from contextlib import ExitStack

import numpy as np

import concourse.bass as bass
from concourse import mybir
from concourse.alu_op_type import AluOpType as ALU

F32 = mybir.dt.float32
BF16 = mybir.dt.bfloat16
I32 = mybir.dt.int32
ACT = mybir.ActivationFunctionType
AX = mybir.AxisListType
RMAX = bass.bass_isa.ReduceOp.max

B = 8
C, HW, PS = 3, 224, 8
GR = HW // PS
NI = GR * GR
L = 77
NU = NI + L
SEQ = 3 * NI + L
T = 7
PI, PT = NI // T, L // T
P = PI + PT
QW = GR // T
D = 64
FD = C * PS * PS
FC = FD // 2
H, DH = 8, 32
HQ = 4
INNER = H * DH
HID = 4 * D
EPS = 1e-5
SIZES = range(3, 21)
NS = len(SIZES)
TBL = 1024
PRIME = 31
SEL = int(0.5 * SEQ) - 1
KP = 96
BANK = 512
W4 = 4 * P
SLOTS = 3
STEPS = 2 * T
PARTS = [((0, 0), (0, 2)), ((0, 1), (1, 2)), ((1, 0), (2, 0)), ((1, 1), (2, 1))]


NEXT_JOBS = {(2, 0): ["A4"], (3, 1): ["A5"], (4, 3): ["A6"], (6, 0): ["A7"], (8, 0): ["A8"], (8, 2): ["A9"],
             (9, 0): ["q0"], (9, 2): ["k0"], (11, 0): ["v0"], (11, 2): ["A1"], (12, 0): ["A2"], (13, 1): ["A3"]}
OWN_JOBS = {(0, 2): ["q1"], (1, 0): ["k1"], (6, 2): ["g0"], (7, 0): ["g1"], (7, 2): ["v1"]}
FFN_JOBS = {(1, 2): ["F"], (3, 2): ["C1"], (4, 0): ["C2"], (4, 2): ["C3"], (4, 3): ["C2b"], (5, 2): ["C4"],
            (8, 2): ["C7"], (9, 2): ["C5"], (10, 0): ["C8"], (13, 0): ["C6"]}


def body_jobs(nxt, prev):
    names = []
    for s in range(STEPS):
        for h in range(HQ):
            at = (s, h)
            names += [f"s{s}.{h}"]
            names += (FFN_JOBS.get(at, []) if prev else []) + OWN_JOBS.get(at, []) + (NEXT_JOBS.get(at, []) if nxt else [])
    return names


BODIES = {
    "prologue": ["W5", "W6", "P1", "P2", "W7", "P3", "A4", "W1", "W2", "A5", "W3", "W4", "A6", "A7",
                 "A1", "A2", "A8", "A9", "q0", "k0", "v0", "A3"],
    "first": body_jobs(True, False),
    "steady": body_jobs(True, True),
    "last": body_jobs(False, True),
    "epilogue": ["F", "C1", "C2", "C3", "C4", "C2b", "C7", "C8", "C5", "C6"],
}


def slots_of(body):
    at = [(n - len(BODIES[body])) % SLOTS for n in range(len(BODIES[body]))]
    return {name: (at[n], at[:n].count(at[n])) for n, name in enumerate(BODIES[body])}


def in_slot(body, slot):
    return sum(k == slot for k, _ in slots_of(body).values())


def uses_before(body, slot, b):
    n = 0
    if body == "prologue":
        return n
    n += in_slot("prologue", slot)
    if body == "first":
        return n
    n += in_slot("first", slot)
    if body == "steady":
        return (b - 1) * in_slot("steady", slot) + n
    n += (B - 2) * in_slot("steady", slot)
    if body == "last":
        return n
    return n + in_slot("last", slot)


def build(nc, x, x_txt, p, out):
    ctx = ExitStack()
    with ctx:
        def sb(name, shape, dt=F32):
            return ctx.enter_context(nc.sbuf_tensor(name, shape, dt))

        def sem(name):
            return ctx.enter_context(nc.semaphore(name))

        slot = [ctx.enter_context(nc.psum_tensor(f"slot{k}", [128, 2 * BANK], F32)) for k in range(SLOTS)]
        o_acc = ctx.enter_context(nc.psum_tensor("o_acc", [128, 2 * BANK], F32))

        ident = sb("ident", [128, 128])
        neg_half = sb("neg_half", [128, T])
        before = sb("before", [128, P])
        images = sb("images", [128, P])
        v_weight = sb("v_weight", [128, 1])
        copies = sb("copies", [128, 1], BF16)
        zeros7 = sb("zeros7", [128, T])
        ln1_gb = sb("ln1_gb", [FC, 2, 2])
        w1_raw = sb("w1_raw", [FC, 2, D])
        w1 = sb("w1", [FC + 1, 2, D])
        col = sb("col", [128, 12])
        wp1_raw = sb("wp1_raw", [D, D])
        wp1 = sb("wp1", [KP, D])
        wp2 = sb("wp2", [KP, D])
        wqkv = sb("wqkv", [KP, 3 * INNER])
        wgate = sb("wgate", [KP, INNER])
        wfinal = sb("wfinal", [128, 2, D])
        wroute = sb("wroute", [KP, P])
        wh = sb("wh", [KP, HID])
        wy = sb("wy", [128, 2, D])
        bf_rep = sb("bf_rep", [128, D])
        b2_rep = sb("b2_rep", [128, D])
        row = sb("row", [1, 2 * D])
        tok_raw = sb("tok_raw", [B, L], I32)
        tokf = sb("tokf", [B, L])
        ok = sb("ok", [B, L])
        ok2 = sb("ok2", [B, L])
        safe = sb("safe", [B, L])
        good_run = sb("good_run", [B, L])
        table_start = sb("table_start", [L, NS, B])
        ids = sb("ids", [L, NS, B + 1], I32)
        ids_now = sb("ids_now", [L, NS], I32)
        rows_flat = sb("rows_flat", [128, NS * D])
        rows = rows_flat[0:L, :].rearrange("p (n d) -> p n d", n=NS)
        text = sb("text", [L, D])
        patches = sb("patches", [PI, C, PS, T * PS])
        pn_flat = sb("pn_flat", [128, T * FD])
        pn = pn_flat[0:PI, :].rearrange("p (t f) -> p t f", t=T)
        st = {k: sb(f"st_{k}", [128, T, 6]) for k in ("p", "x", "y", "u", "n", "w")}
        mv = {k: sb(f"mv_{k}", [128, T, 2]) for k in ("p", "x", "y", "u", "n", "w")}
        ve = {k: sb(f"ve_{k}", [128, T]) for k in ("p", "x", "y", "u", "n", "w")}
        rstd = {k: sb(f"rstd_{k}", [128, T]) for k in ("p", "x", "y", "u", "n", "w")}
        neg_mean_rstd = sb("neg_mean_rstd", [128, T])
        pnT = sb("pnT", [FC + 1, 2, NI])
        x2 = sb("x2", [P, T, D])
        x2T = sb("x2T", [KP, NI])
        y2 = x2
        zT = sb("zT", [D, NI])
        x3T = x2T
        h_all = sb("h_all", [P, B, T, D])
        u = sb("u", [P, T, D])
        n2 = x2
        uT = sb("uT", [KP, NU])
        nT = sb("nT", [KP, NU])
        qparts = sb("qparts", [128, 3, NU], BF16)
        kparts = sb("kparts", [128, 3, NU], BF16)
        rest = {k: sb(f"rest_{k}", [128, NU]) for k in "qk"}
        qs = [sb(f"qs{g}", [128, HQ, 2, NU], BF16) for g in range(2)]
        ks = [sb(f"ks{g}", [128, HQ, 2, NU], BF16) for g in range(2)]
        v = [sb(f"v{g}", [P, T, HQ * DH]) for g in range(2)]
        gate = [sb(f"gate{g}", [128, NU]) for g in range(2)]
        e_flat = sb("e_flat", [128, 2 * HQ * NU])
        e = e_flat[0:P, :].rearrange("p (r h t q) -> p r h t q", r=2, h=HQ, t=T)
        raw_qkv = e_flat[:, 0:6 * D].rearrange("p (k n) -> p k n", k=6)
        raw_gate = e_flat[:, 6 * D:8 * D].rearrange("p (k n) -> p k n", k=2)
        raw_final = e_flat[0:D, 8 * D:8 * D + INNER]
        qkv_t = e_flat[0:D, 1024:1024 + 3 * INNER]
        ids_f = e_flat[0:B, 2048:2048 + NS * L].rearrange("p (n l) -> p n l", n=NS)
        NG, LC = SIZES[-1], L + 1
        hashes = e_flat[0:B, 3600:3600 + NG * LC].bitcast(I32).rearrange("p (n l) -> p n l", n=NG)
        negmax = sb("negmax", [P, 2, HQ])
        s_all = sb("s_all", [P, 2, HQ])
        s_txt = sb("s_txt", [P, 2, HQ])
        den = sb("den", [P, 2, HQ])
        rden = sb("rden", [P, 2, HQ])
        vs = sb("vs", [P, 2, HQ, DH])
        og = [sb("og0", [128, NU]), gate[1]]
        h2 = sb("h2", [P, T, D])
        w = sb("w", [P, T, D])
        wT = sb("wT", [KP, NU])
        base = sb("base", [P, T, D])
        route = sb("route", [P, NU])
        w_tok = sb("w_tok", [P, T])
        less = [(qparts, kparts)[t // 3][0:P, t % 3, :] for t in range(T - 1)] + [sb("less_last", [P, NU], BF16)[:, :]]
        above_cnt = sb("above_cnt", [P, T])
        cand = sb("cand", [P, T])
        edge = sb("edge", [P, 2])
        above = sb("above", [P, T])
        tied = sb("tied", [P, T])
        tied_sum = sb("tied_sum", [P, 1])
        tie_no = sb("tie_no", [P, T])
        ties = sb("ties", [P, 2])
        limit = sb("limit", [P, 3])
        take = sb("take", [P, 3, T])
        hz = [rest[k] for k in "qk"]
        hT = [pn_flat[:, 0:NU], rows_flat[:, 0:NU]]
        ys = sb("ys", [P, T, D])
        o_c = [sb(f"o_c{c}", [P, T, D]) for c in range(3)]

        filled = [sem(f"slot{k}_filled") for k in range(SLOTS)]
        drained = [sem(f"slot{k}_drained") for k in range(SLOTS)]
        token_weights_in = sem("token_weights_in")
        weights_in = sem("weights_in")
        text_in = sem("text_in")
        consts_ready = sem("consts_ready")
        rows_ready = sem("rows_ready")
        settled = sem("settled")
        ids_f_ready = sem("ids_f_ready")
        ids_now_ready = sem("ids_now_ready")
        rows_in = sem("rows_in")
        text_ready = sem("text_ready")
        text_placed = sem("text_placed")
        patches_in = sem("patches_in")
        patches_normed = sem("patches_normed")
        embedded = {n: sem(f"embedded_{n}") for n in "35"}
        x_normed = sem("x_normed")
        y_normed = sem("y_normed")
        var_ready = {k: sem(f"var_ready_{k}") for k in mv}
        centered = {k: sem(f"centered_{k}") for k in mv if k != "p"}
        rstd_ready = sem("rstd_ready")
        silu_in_ready = sem("silu_in_ready")
        silu_ready = sem("silu_ready")
        u_ready = sem("u_ready")
        n_ready = sem("n_ready")
        hub_ready = sem("hub_ready")
        q_top_ready = sem("q_top_ready")
        k_top_ready = sem("k_top_ready")
        q_rest_ready = sem("q_rest_ready")
        k_rest_ready = sem("k_rest_ready")
        q_mid_ready = sem("q_mid_ready")
        k_mid_ready = sem("k_mid_ready")
        q_parts_ready = sem("q_parts_ready")
        k_parts_ready = sem("k_parts_ready")
        placed = [sem(f"head{h}_placed") for h in range(HQ)]
        negmax_ready = sem("negmax_ready")
        vs_ready = sem("vs_ready")
        av_done = sem("av_done")
        o_drained = sem("o_drained")
        w_ready = sem("w_ready")
        base_ready = sem("base_ready")
        gelu_arg_ready = sem("gelu_arg_ready")
        gelu_tanh_ready = sem("gelu_tanh_ready")
        gelu_ready = sem("gelu_ready")
        own_route_ready = sem("own_route_ready")
        less_ready = sem("less_ready")
        cand_ready = sem("cand_ready")
        edge_ready = sem("edge_ready")
        tied_ready = sem("tied_ready")
        take_ready = sem("take_ready")
        out_ready = sem("out_ready")
        stored = sem("stored")

        START = 1

        def wait(eng, s, value):
            if not (isinstance(value, int) and value <= 0):
                eng.wait_ge(s, value)

        PLACED = 16 * 2 * len(PARTS)

        def wait_placed(eng, quads):
            for h in range(HQ):
                wait(eng, placed[h], PLACED * quads)

        def settle(eng):
            eng.sem_inc(settled)

        class Job:

            def __init__(self, body, name, b):
                self.k, turn = slots_of(body)[name]
                self.n = uses_before(body, self.k, b) + turn
                self.tile = slot[self.k]

            def wait_free(self, pe):
                wait(pe, drained[self.k], self.n)

            def wait_filled(self, eng):
                eng.wait_ge(filled[self.k], self.n + 1)

            def wait_drained(self, eng):
                eng.wait_ge(drained[self.k], self.n + 1)

            def fill(self, ins):
                ins.then_inc(filled[self.k], 1)

            def drain(self, ins):
                ins.then_inc(drained[self.k], 1)

        class Chain:

            def __init__(self, eng, name):
                self.eng, self.sem, self.n = eng, sem(name), 0

            def __call__(self, ins):
                ins.then_inc(self.sem, 1)
                self.n += 1

            def sync(self):
                if self.n:
                    self.eng.wait_ge(self.sem, self.n)

            def restart(self):
                if self.n:
                    self.eng.wait_ge(self.sem, self.n)
                    self.eng.sem_clear(self.sem)
                    self.n = 0

        def rests(eng, k, turn):
            parts, top_ready, rest_ready = {"q": (qparts, q_top_ready, q_rest_ready),
                                            "k": (kparts, k_top_ready, k_rest_ready)}[k]
            eng.wait_ge(top_ready, turn + 1)
            eng.tensor_tensor(rest[k][:, :], rest[k][:, :], parts[:, 0, :], ALU.subtract).then_inc(rest_ready, 1)

        def run(eng, iteration, prologue, epilogue):
            prologue()
            iteration("first", 0, True, False)
            with eng.Fori(1, B - 1) as b:
                iteration("steady", b, True, True)
            iteration("last", B - 1, False, True)
            epilogue("epilogue", B - 1)

        def pieces(n):
            return [(a, min(n, a + BANK)) for a in range(0, n, BANK)]

        def tile_col(t, parts):
            return (t // 4) * BANK + (t % 4) * parts

        def fold(eng_do, dst, tile, rows_, parts):
            eng_do(dst[:, 0:4 * parts], tile[0:rows_, 0:4 * parts])
            return eng_do(dst[:, 4 * parts:T * parts], tile[0:rows_, BANK:BANK + (T - 4) * parts])

        patch_tile = lambda t: patches[:, :, :, PS * t:PS * t + PS].rearrange("p c y x -> p (c y) x")
        NTW, NW = 19, 15
        block = ctx.enter_context(nc.Block())

        @block.sync
        def _(sp):
            def load(dst, src, s, elements=False):
                sp.dma_start(dst, src, allow_slow_non_contiguous=elements).then_inc(s, 16)

            def load_patches(b):
                for q in range(QW):
                    for c in range(C):
                        load(patches[q:PI:QW, c, :, :],
                             x[b, c].rearrange("(r y) (q w) -> q r y w", y=PS, q=QW)[q], patches_in)

            load(tok_raw[:, :], x_txt, text_in)
            load_patches(0)
            count = [0, 0]

            def load_w(dst, src, elements=False, later=1):
                count[later] += 1
                load(dst, src, (token_weights_in, weights_in)[later], elements)

            one = lambda a: a.rearrange("(a n) -> a n", a=1)
            column = lambda a: a.rearrange("(n a) -> n a", a=1)
            w1_d = p["L0_tok_W1"].rearrange("(f c) n -> c f n", c=C)
            for src, dst in ((w1_d, lambda a, b_, k: w1_raw[a:b_, k, :]),
                             (p["L0_tok_ln1_g"].rearrange("(f c o) -> c f o", c=C, o=1), lambda a, b_, k: ln1_gb[a:b_, k, 0:1]),
                             (p["L0_tok_ln1_b"].rearrange("(f c o) -> c f o", c=C, o=1), lambda a, b_, k: ln1_gb[a:b_, k, 1:2])):
                half = PS * PS // 2
                few = src is not w1_d
                load_w(dst(0, 2 * half, 0), src[0], few, 0)
                load_w(dst(2 * half, 3 * half, 0), src[1, 0:half], few, 0)
                load_w(dst(0, half, 1), src[1, half:2 * half], few, 0)
                load_w(dst(half, 3 * half, 1), src[2], few, 0)
            load_w(wp1_raw[:, :], p["L0_tok_Wp1"], False, 0)
            for n, name in enumerate(("L0_tok_ln2_g", "L0_tok_ln2_b", "L0_tok_lnp_g", "L0_tok_lnp_b")):
                load_w(col[0:D, n:n + 1], column(p[name]), True, 0)
            load_w(row[0:1, 0:D], one(p["L0_tok_b1"]), False, 0)
            load_w(row[0:1, D:2 * D], one(p["L0_tok_bp1"]), False, 0)
            load_w(raw_qkv[:, :, :], p["L0_attn_W_qkv"].rearrange("(k r) n -> r k n", r=128))
            load_w(raw_gate[:, :, :], p["L0_attn_W_gate"].rearrange("(k r) n -> r k n", r=128))
            load_w(raw_final[:, :], p["L0_attn_W_final"])
            for n, name in enumerate(("L0_attn_ln_gamma", "L0_attn_ln_beta"), 4):
                load_w(col[0:D, n:n + 1], column(p[name]), True)
            load_w(wy[:, :, :], p["L0_ffn_w2"].rearrange("(k r) n -> r k n", r=128))
            load_w(bf_rep[0:P, :], one(p["L0_attn_b_final"]).to_broadcast([P, D]))
            load_w(b2_rep[0:P, :], one(p["L0_ffn_b2"]).to_broadcast([P, D]))
            sp.wait_ge(consts_ready, 1)
            load_w(wp2[0:D, :], p["L0_tok_Wp2"])
            load_w(wp2[D:D + 1, :], one(p["L0_tok_bp2"]))
            load_w(wgate[D:D + 1, :], one(p["L0_attn_b_gate"]))
            load_w(col[0:D, 7:8], p["L0_ffn_wr"], True)
            load_w(col[D:D + 1, 7:8], one(p["L0_ffn_br"]), True)
            load_w(wh[0:D, :], p["L0_ffn_w1"])
            load_w(wh[D:D + 1, :], one(p["L0_ffn_b1"]))
            assert count == [NTW, NW], count

            def place(g, side, h, r):
                parts, dst = ((qparts, qs[g]), (kparts, ks[g]))[side]
                i, j = PARTS[r][0][side], PARTS[r][1][side]
                src = parts[DH * h:DH * h + DH, i:j + 1:max(j - i, 1), :] if j > i else \
                    parts[DH * h:DH * h + DH, i:i + 1, :].to_broadcast([DH, 2, NU])
                load(dst[DH * r:DH * r + DH, h, :, :], src, placed[h])

            def place_quad(g, turn):
                for ready, side, r in ((q_top_ready, 0, 0), (k_top_ready, 1, 2), (q_mid_ready, 0, 1), (k_mid_ready, 1, 3)):
                    sp.wait_ge(ready, turn + 1)
                    for h in range(HQ):
                        place(g, side, h, r)
                sp.wait_ge(q_parts_ready, turn + 1)
                sp.wait_ge(k_parts_ready, turn + 1)
                for h in range(HQ):
                    for side, r in ((0, 2), (0, 3), (1, 0), (1, 1)):
                        place(g, side, h, r)

            def place_text(b):
                sp.wait_ge(text_ready, b + 1)
                load(h_all[PI:P, b, :, :], text[:, :], text_placed)

            def store(b):
                for c in range(3):
                    sp.wait_ge(out_ready, START + 3 * b + c + 1)
                    n = P if c == 2 else PI
                    load(out[b, c * NI:c * NI + n * T, :].rearrange("(p t) d -> p t d", t=T), o_c[c][0:n, :, :], stored)

            def prologue():
                for b in range(2):
                    sp.wait_ge(patches_normed, b + 1)
                    load_patches(b + 1)
                    if b == 0:
                        place_text(0)
                        place_quad(0, 0)

            def iteration(body, b, nxt, prev):
                place_quad(1, 2 * b + 1)
                if nxt:
                    place_text(b + 1)
                    place_quad(0, 2 * b + 2)
                    sp.wait_ge(patches_normed, b + 3)
                    load_patches((b + 3) % B)
                if prev:
                    store(b - 1)

            def epilogue(body, b):
                store(b)
                sp.wait_ge(stored, START + 16 * 3 * B)
                sp.wait_ge(patches_in, 16 * QW * C * (B + 2))

            run(sp, iteration, prologue, epilogue)

        @block.gpsimd
        def _(pool):
            chain = Chain(pool, "pool_chain")

            def step(ins):
                chain(ins)
                chain.sync()

            for count in (base_ready, cand_ready, out_ready, stored, take_ready):
                pool.sem_inc(count)
            for tile in (wp1, wp2, wqkv, wgate, wroute, wh):
                step(pool.memset(tile[D:KP, :], 0.0))
            step(pool.memset(ident[:, :], 0.0))
            step(pool.memset(before[:, :], 1.0))
            step(pool.memset(images[:, :], 1.0))
            step(pool.memset(v_weight[:, :], 1.5))
            step(pool.memset(copies[:, :], 3.0))
            step(pool.memset(neg_half[:, :], -0.5))
            step(pool.memset(zeros7[:, :], 0.0))
            step(pool.affine_select(out=ident[:, :], in_=ident[:, :], compare_op=ALU.not_equal, fill=1.0,
                                     base=0, pattern=[[-1, 128]], channel_multiplier=1))
            step(pool.affine_select(out=before[:, :], in_=before[:, :], compare_op=ALU.is_gt, fill=0.0,
                                     base=0, pattern=[[1, P]], channel_multiplier=-1))
            step(pool.affine_select(out=images[:, :], in_=images[:, :], compare_op=ALU.is_gt, fill=0.0,
                                     base=PI, pattern=[[0, P]], channel_multiplier=-1))
            step(pool.affine_select(out=v_weight[:, :], in_=v_weight[:, :], compare_op=ALU.is_gt, fill=0.5,
                                     base=PI, pattern=[[0, 1]], channel_multiplier=-1))
            step(pool.affine_select(out=copies[:, :], in_=copies[:, :], compare_op=ALU.is_gt, fill=1.0,
                                     base=PI, pattern=[[0, 1]], channel_multiplier=-1))
            for n in range(NS):
                chain(pool.memset(table_start[:, n, :], float(n * (TBL + 1))))
            chain.sync()
            pool.memset(ys[:, :, :], 0.0).then_inc(consts_ready, 1)
            pool.wait_ge(consts_ready, 1)

            def gather(b, sizes):
                pool.wait_ge(ids_now_ready, b + 1)
                settle(pool)
                for n in sizes:
                    pool.indirect_dma_start(
                        out=rows[:, n, :], out_offset=None,
                        in_=p["L0_txt_tables"].rearrange("n r d -> (n r) d"),
                        in_offset=bass.IndirectOffsetOnAxis(ap=ids_now[:, n:n + 1], axis=0)).then_inc(rows_in, 16)

            def sum_text(b):
                pool.wait_ge(rows_in, 16 * NS * (b + 1))
                n = NS
                while n > 1:
                    half = n // 2
                    chain(pool.tensor_tensor(rows[:, 0:half, :], rows[:, 0:half, :], rows[:, n - half:n, :], ALU.add))
                    chain.sync()
                    n -= half
                wait(pool, text_placed, 16 * b)
                settle(pool)
                pool.tensor_scalar(text[:, :], rows[:, 0, :], 1.0 / (NS + 1), None, ALU.mult).then_inc(text_ready, 1)

            def find_rstd(k, b, parts):
                pool.wait_ge(var_ready[k], b + 1)
                settle(pool)
                chain(pool.tensor_scalar(ve[k][0:parts, :], mv[k][0:parts, :, 1], EPS, None, ALU.add))
                chain.sync()
                return pool.tensor_tensor(rstd[k][0:parts, :], ve[k][0:parts, :], neg_half[0:parts, :], ALU.pow)

            def patch_scales(b):
                chain(find_rstd("p", b, PI))
                chain.sync()
                chain(pool.tensor_tensor(ve["p"][0:PI, :], mv["p"][0:PI, :, 0], rstd["p"][0:PI, :], ALU.mult))
                chain.sync()
                pool.tensor_scalar(neg_mean_rstd[0:PI, :], ve["p"][0:PI, :], -1.0, None, ALU.mult).then_inc(rstd_ready, 1)

            def finish_norm(k, b, dst, parts, normed):
                chain(find_rstd(k, b, parts))
                chain.sync()
                pool.wait_ge(centered[k], b + 1)
                pool.tensor_tensor(dst[0:parts, :, :], dst[0:parts, :, :],
                                   rstd[k][0:parts, :].unsqueeze(2).to_broadcast([parts, T, D]), ALU.mult)\
                    .then_inc(normed, 1)

            def make_hub(b):
                pool.wait_ge(u_ready, b + 1)
                chain(pool.tensor_tensor(h_all[:, b, :, :], h_all[:, b, :, :], u[:, :, :], ALU.add))
                chain.sync()
                pool.tensor_tensor(h_all[:, b, :, :], h_all[:, b, :, :],
                                   bf_rep[0:P, :].unsqueeze(1).to_broadcast([P, T, D]), ALU.add).then_inc(hub_ready, 1)

            def low_part(parts, k, mid_ready, parts_ready, turn):
                pool.wait_ge(mid_ready, turn + 1)
                pool.tensor_tensor(parts[:, 2, :], rest[k][:, :], parts[:, 1, :], ALU.subtract).then_inc(parts_ready, 1)

            def low_parts(turn):
                low_part(qparts, "q", q_mid_ready, q_parts_ready, turn)
                low_part(kparts, "k", k_mid_ready, k_parts_ready, turn)

            def make_base(b):
                pool.wait_ge(w_ready, b + 1)
                wait(pool, out_ready, START + 3 * b)
                pool.tensor_tensor(base[:, :, :], h2[:, :, :], w[:, :, :], ALU.add).then_inc(base_ready, 1)

            def gelu_arg(body, c, g):
                Job(body, f"C{3 + g}", c).wait_drained(pool)
                chain(pool.tensor_tensor(hT[g][:, :], hz[g][:, :], hz[g][:, :], ALU.mult))
                chain.sync()
                chain(pool.tensor_scalar(hT[g][:, :], hT[g][:, :], 0.044715, 1.0, ALU.mult, ALU.add))
                chain.sync()
                pool.tensor_tensor(hT[g][:, :], hT[g][:, :], hz[g][:, :], ALU.mult).then_inc(gelu_arg_ready, 1)

            def find_edge(b):
                pool.wait_ge(cand_ready, START + b + 1)
                settle(pool)
                pool.partition_all_reduce(edge[:, 1:2], edge[:, 0:1], P, RMAX).then_inc(edge_ready, 1)

            def finish(body, c, b, k):
                if k:
                    pool.wait_ge(out_ready, START + 3 * b + k)
                else:
                    pool.wait_ge(take_ready, START + b + 1)
                    Job(body, "C5", c).wait_drained(pool)
                    wait(pool, stored, START + 48 * b)
                    wait(pool, out_ready, START + 3 * b)
                chain(pool.tensor_tensor(o_c[k][:, :, :], ys[:, :, :],
                                         take[:, k, :].unsqueeze(2).to_broadcast([P, T, D]), ALU.mult))
                chain.sync()
                pool.tensor_tensor(o_c[k][:, :, :], o_c[k][:, :, :], base[:, :, :], ALU.add).then_inc(out_ready, 1)

            def prologue():
                patch_scales(0)
                gather(0, range(0, 8))
                finish_norm("x", 0, x2, PI, x_normed)
                gather(0, range(8, NS - 2))
                finish_norm("y", 0, y2, PI, y_normed)
                gather(0, range(NS - 2, NS))
                sum_text(0)
                patch_scales(1)
                finish_norm("u", 0, u, P, u_ready)
                finish_norm("n", 0, n2, P, n_ready)
                low_parts(0)
                make_hub(0)
                gather(1, range(0, NS // 2))

            def iteration(body, b, nxt, prev):
                chain.restart()
                if not nxt:
                    pool.wait_ge(rows_in, 16 * (NS * B + NS // 2))
                if nxt:
                    finish_norm("x", b + 1, x2, PI, x_normed)
                    gather(b + 1, range(NS // 2, NS))
                if prev:
                    finish_norm("w", b - 1, w, P, w_ready)
                    make_base(b - 1)
                if nxt:
                    sum_text(b + 1)
                low_part(qparts, "q", q_mid_ready, q_parts_ready, 2 * b + 1)
                low_part(kparts, "k", k_mid_ready, k_parts_ready, 2 * b + 1)
                if nxt:
                    finish_norm("y", b + 1, y2, PI, y_normed)
                    patch_scales(b + 2)
                if prev:
                    gelu_arg(body, b, 0)
                    gelu_arg(body, b, 1)
                if nxt:
                    finish_norm("u", b + 1, u, P, u_ready)
                    finish_norm("n", b + 1, n2, P, n_ready)
                if prev:
                    find_edge(b - 1)
                if nxt:
                    make_hub(b + 1)
                    low_part(qparts, "q", q_mid_ready, q_parts_ready, 2 * b + 2)
                    rests(pool, "k", 2 * b + 2)
                    low_part(kparts, "k", k_mid_ready, k_parts_ready, 2 * b + 2)
                    gather(b + 2, range(0, NS // 2))
                if prev:
                    finish(body, b, b - 1, 0)
                    finish(body, b, b - 1, 1)
                    finish(body, b, b - 1, 2)
                chain.restart()

            def epilogue(body, b):
                finish_norm("w", b, w, P, w_ready)
                make_base(b)
                gelu_arg(body, b, 0)
                find_edge(b)

            run(pool, iteration, prologue, epilogue)

        @block.scalar
        def _(act):
            chain = Chain(act, "act_chain")

            def copy(dst, src, **kw):
                return act.activation(dst, src, ACT.Copy, **kw)

            def evict(body, name, b, dst, rows_, parts):
                j = Job(body, name, b)
                j.wait_filled(act)
                j.drain(fold(copy, dst, j.tile, rows_, parts))

            def fill_rows():
                act.wait_ge(consts_ready, 1)
                for tile, n in ((x2T, NI), (uT, NU), (nT, NU), (wT, NU)):
                    chain(copy(tile[D:KP, :], zeros7[D:KP, 0:1].to_broadcast([KP - D, n])))
                chain(copy(pnT[FC:FC + 1, 1, :], images[FC:FC + 1, 0:1].to_broadcast([1, NI])))
                chain.sync()
                for tile, n in ((x2T, NI), (uT, NU), (nT, NU), (wT, NU)):
                    chain(copy(tile[D:D + 1, :], images[D:D + 1, 0:1].to_broadcast([1, n])))
                chain.sync()
                act.sem_inc(rows_ready)

            def token_weights():
                act.wait_ge(token_weights_in, 16 * NTW)
                for k in range(2):
                    chain(act.activation(w1[0:FC, k, :], w1_raw[:, k, :], ACT.Copy, scale=ln1_gb[:, k, 0:1]))
                chain(act.activation(wp1[0:D, :], wp1_raw[:, :], ACT.Copy, scale=col[0:D, 0:1]))

            def qkv_gate_weights():
                act.wait_ge(weights_in, 16 * NW)
                chain(act.activation(wp2[0:D, :], wp2[0:D, :], ACT.Copy, scale=0.5))
                chain(act.activation(wy[:, :, :], wy[:, :, :], ACT.Copy, scale=0.5))
                chain(copy(wroute[0:D + 1, :], col[0:D + 1, 7:8].to_broadcast([D + 1, P])))
                j = Job("prologue", "W1", 0)
                j.wait_filled(act)
                chain(copy(qkv_t[:, :], j.tile[0:D, 0:3 * INNER]))
                chain.sync()
                chain(act.activation(col[0:D, 6:7], col[0:D, 4:5], ACT.Copy, scale=float(DH) ** -0.5))
                chain.sync()
                chain(act.activation(wqkv[0:D, 0:INNER], qkv_t[:, 0:INNER], ACT.Copy, scale=col[0:D, 6:7]))
                j.drain(act.activation(wqkv[0:D, INNER:3 * INNER], qkv_t[:, INNER:3 * INNER], ACT.Copy,
                                       scale=col[0:D, 4:5]))
                j = Job("prologue", "W2", 0)
                j.wait_filled(act)
                j.drain(copy(wgate[0:D, :], j.tile[0:D, 0:INNER]))

            def final_weights_and_biases():
                j = Job("prologue", "W3", 0)
                j.wait_filled(act)
                j.drain(act.activation(wfinal[:, :, :], j.tile[:, 0:2 * D].rearrange("p (k n) -> p k n", k=2),
                                       ACT.Copy, scale=0.5))
                j = Job("prologue", "W4", 0)
                j.wait_filled(act)
                chain(act.activation(wqkv[D:D + 1, 0:INNER], j.tile[0:1, 0:INNER], ACT.Copy,
                                     scale=float(DH) ** -0.5))
                j.drain(copy(wqkv[D:D + 1, INNER:3 * INNER], j.tile[0:1, INNER:3 * INNER]))

            def evict_patches(body, name, b, k):
                evict(body, name, b, pnT[0:FC, k, :], FC, PI)

            def patch_norm(body, c, b, tiles):
                act.wait_ge(rstd_ready, b + 1)
                if body in ("steady", "last"):
                    Job(body, "C5", c).wait_drained(act)
                for t in tiles:
                    ins = act.activation(pn[:, t, :].rearrange("p (f x) -> p f x", x=PS), patch_tile(t), ACT.Identity,
                                         scale=rstd["p"][0:PI, t:t + 1], bias=neg_mean_rstd[0:PI, t:t + 1])
                    if t < T - 1:
                        chain(ins)
                    else:
                        ins.then_inc(patches_normed, 1)

            def silu_in(body, b):
                j = Job(body, "A6", b)
                j.wait_filled(act)
                j.drain(fold(lambda o, i: act.activation(o, i, ACT.Identity, scale=col[0:D, 2:3], bias=col[0:D, 3:4]),
                             zT[:, :], j.tile, D, PI))

            def silu_tanh(body, b):
                Job(body, "A6", b).wait_drained(act)
                act.activation(x3T[0:D, :], zT[:, :], ACT.Tanh, scale=0.5).then_inc(silu_in_ready, 1)

            def evict_tokens(body, b, dst_b):
                j = Job(body, "A7", b)
                j.wait_filled(act)
                j.drain(copy(h_all[0:PI, dst_b, :, :], j.tile[0:PI, 0:T * D].rearrange("p (t d) -> p t d", t=T)))

            def evict_embedded(body, name, c):
                j = Job(body, name, c)
                j.wait_filled(act)
                j.drain(copy(x2[0:PI, :, :], j.tile[0:PI, 0:T * D].rearrange("p (t d) -> p t d", t=T)))
                j.wait_drained(act)
                act.sem_inc(embedded[name[1]])

            def evict_query_key(body, b, k, g, turn):
                j = Job(body, f"{k}{g}", b)
                j.wait_filled(act)
                wait_placed(act, turn)
                if g == 0:
                    wait(act, gelu_ready, 2 * b)
                j.drain(copy(rest[k][:, :], j.tile[:, 0:NU]))

            def top_part(body, b, k, g):
                Job(body, f"{k}{g}", b).wait_drained(act)
                parts, ready = {"q": (qparts, q_top_ready), "k": (kparts, k_top_ready)}[k]
                copy(parts[:, 0, :], rest[k][:, :]).then_inc(ready, 1)

            def mid_part(k, turn):
                parts, rest_ready, ready = {"q": (qparts, q_rest_ready, q_mid_ready),
                                            "k": (kparts, k_rest_ready, k_mid_ready)}[k]
                act.wait_ge(rest_ready, turn + 1)
                copy(parts[:, 1, :], rest[k][:, :]).then_inc(ready, 1)

            def evict_values(body, b, g):
                j = Job(body, f"v{g}", b)
                j.wait_filled(act)
                j.drain(act.activation(v[g][:, :, :], j.tile[0:P, 0:T * HQ * DH].rearrange("p (t n) -> p t n", t=T),
                                       ACT.Copy, scale=v_weight[0:P, :]))

            def gates(body, b, g):
                j = Job(body, f"g{g}", b)
                j.wait_filled(act)
                j.drain(act.activation(gate[g][:, :], j.tile[:, 0:NU], ACT.Tanh, scale=0.5))

            def exp_scores(body, b, s, h):
                j = Job(body, f"s{s}.{h}", b)
                act.wait_ge(negmax_ready, (b * STEPS + s) * HQ + h + 1)
                j.drain(act.activation(e[:, s % 2, h, :, :], j.tile[0:P, 0:NU].rearrange("p (t q) -> p t q", t=T),
                                       ACT.Exp, bias=negmax[:, s % 2, h:h + 1], accum_out=s_all[:, s % 2, h:h + 1]))

            def gelu_z(body, c, g, turn):
                j = Job(body, f"C{3 + g}", c)
                j.wait_filled(act)
                act.wait_ge((q_parts_ready, k_parts_ready)[g], turn)
                j.drain(copy(hz[g][:, :], j.tile[:, 0:NU]))

            def gelu_tanh(b, g):
                act.wait_ge(gelu_arg_ready, 2 * b + g + 1)
                act.activation(hT[g][:, :], hT[g][:, :], ACT.Tanh, scale=0.7978845608028654).then_inc(gelu_tanh_ready, 1)

            def evict_route(body, c, b):
                j = Job(body, "C2", c)
                j.wait_filled(act)
                wait(act, cand_ready, START + b)
                j.drain(copy(route[:, :], j.tile[0:P, 0:NU]))

            def evict_counts(body, c):
                j = Job(body, "C7", c)
                j.wait_filled(act)
                j.drain(copy(route[0:1, :], j.tile[0:1, 0:NU]))

            def prologue():
                fill_rows()
                patch_norm("prologue", 0, 0, range(T))
                token_weights()
                evict_patches("prologue", "P1", 0, 0)
                evict_patches("prologue", "P2", 0, 1)
                evict_embedded("prologue", "P3", 0)
                evict("prologue", "A4", 0, x2T[0:D, :], D, PI)
                qkv_gate_weights()
                evict_embedded("prologue", "A5", 0)
                final_weights_and_biases()
                silu_in("prologue", 0)
                silu_tanh("prologue", 0)
                evict_tokens("prologue", 0, 0)
                patch_norm("prologue", 0, 1, range(T))
                evict_patches("prologue", "A1", 0, 0)
                evict_patches("prologue", "A2", 0, 1)
                evict("prologue", "A8", 0, uT[0:D, :], D, P)
                evict("prologue", "A9", 0, nT[0:D, :], D, P)
                evict_query_key("prologue", 0, "q", 0, 0)
                top_part("prologue", 0, "q", 0)
                evict_query_key("prologue", 0, "k", 0, 0)
                mid_part("q", 0)
                top_part("prologue", 0, "k", 0)
                mid_part("k", 0)
                evict_values("prologue", 0, 0)
                evict_embedded("prologue", "A3", 0)

            def iteration(body, b, nxt, prev):
                chain.restart()
                for s in range(STEPS):
                    for h in range(HQ):
                        at = (s, h)
                        exp_scores(body, b, s, h)
                        if prev:
                            if at == (3, 2):
                                evict(body, "C1", b, wT[0:D, :], D, P)
                            if at == (4, 0):
                                evict_route(body, b, b - 1)
                            if at == (4, 2):
                                gelu_z(body, b, 0, 2 * b + 2)
                            if at == (5, 2):
                                gelu_z(body, b, 1, 2 * b + 2)
                            if at == (7, 3):
                                gelu_tanh(b - 1, 0)
                            if at == (8, 1):
                                gelu_tanh(b - 1, 1)
                            if at == (8, 2):
                                evict_counts(body, b)
                        if at == (0, 2):
                            evict_query_key(body, b, "q", 1, 2 * b + 1)
                        if at == (0, 3):
                            top_part(body, b, "q", 1)
                        if at == (1, 0):
                            evict_query_key(body, b, "k", 1, 2 * b + 1)
                            top_part(body, b, "k", 1)
                        if at == (2, 1):
                            mid_part("q", 2 * b + 1)
                        if at == (2, 2):
                            mid_part("k", 2 * b + 1)
                        if at == (6, 2):
                            gates(body, b, 0)
                        if at == (7, 0):
                            gates(body, b, 1)
                        if at == (7, 2):
                            evict_values(body, b, 1)
                        if nxt:
                            if at == (2, 0):
                                evict(body, "A4", b, x2T[0:D, :], D, PI)
                            if at == (3, 1):
                                evict_embedded(body, "A5", b)
                            if at == (4, 3):
                                silu_in(body, b)
                                silu_tanh(body, b)
                            if at == (6, 0):
                                evict_tokens(body, b, b + 1)
                            if at == (8, 0):
                                evict(body, "A8", b, uT[0:D, :], D, P)
                            if at == (8, 2):
                                evict(body, "A9", b, nT[0:D, :], D, P)
                            if at == (9, 0):
                                evict_query_key(body, b, "q", 0, 2 * b + 2)
                            if at == (9, 2):
                                evict_query_key(body, b, "k", 0, 2 * b + 2)
                                top_part(body, b, "q", 0)
                                top_part(body, b, "k", 0)
                            if at == (10, 0):
                                patch_norm(body, b, b + 2, range(0, 2))
                            if at == (10, 1):
                                patch_norm(body, b, b + 2, range(2, 4))
                            if at == (10, 3):
                                mid_part("q", 2 * b + 2)
                                patch_norm(body, b, b + 2, range(4, 6))
                            if at == (11, 0):
                                evict_values(body, b, 0)
                                patch_norm(body, b, b + 2, range(6, T))
                            if at == (11, 1):
                                mid_part("k", 2 * b + 2)
                            if at == (11, 2):
                                evict_patches(body, "A1", b, 0)
                            if at == (12, 0):
                                evict_patches(body, "A2", b, 1)
                            if at == (13, 1):
                                evict_embedded(body, "A3", b)
                chain.restart()

            def epilogue(body, b):
                evict(body, "C1", b, wT[0:D, :], D, P)
                evict_route(body, b, b)
                gelu_z(body, b, 0, 2 * b + 2)
                gelu_z(body, b, 1, 2 * b + 2)
                gelu_tanh(b, 0)
                gelu_tanh(b, 1)
                evict_counts(body, b)

            run(act, iteration, prologue, epilogue)

        @block.vector
        def _(dve):
            chain = Chain(dve, "dve_chain")

            def stats(k, src, parts, tiles=range(T)):
                for t in tiles:
                    chain(dve.bn_stats(st[k][0:parts, t, :], src(t)))

            def moments(k, b, parts):
                chain.sync()
                for t in range(T):
                    ins = dve.bn_aggr(mv[k][0:parts, t, :], st[k][0:parts, t, :])
                    if t < T - 1:
                        chain(ins)
                ins.then_inc(var_ready[k], 1)

            def center(k, b, dst, src, parts):
                moments(k, b, parts)
                chain.sync()
                dve.wait_ge(var_ready[k], b + 1)
                dve.tensor_tensor(dst[0:parts, :, :], src, mv[k][0:parts, :, 0:1].to_broadcast([parts, T, D]),
                                  ALU.subtract).then_inc(centered[k], 1)


            def patch_stats(b, tiles):
                dve.wait_ge(patches_in, 16 * QW * C * (b + 1))
                stats("p", patch_tile, PI, tiles)

            def embedded_stats(k, name, b):
                dve.wait_ge(embedded[name[1]], b + 1)
                stats(k, lambda t: x2[0:PI, t, :], PI)

            def embedded_center(k, b):
                center(k, b, x2, x2[0:PI, :, :], PI)

            def silu_product(b):
                dve.wait_ge(silu_in_ready, b + 1)
                dve.scalar_tensor_tensor(out=x3T[0:D, :], in0=x3T[0:D, :], scalar=1.0, in1=zT[:, :],
                                         op0=ALU.add, op1=ALU.mult).then_inc(silu_ready, 1)

            def pick_ids(b):
                wait(dve, rows_in, 16 * NS * b)
                dve.tensor_copy(ids_now[:, :], ids[:, :, b]).then_inc(ids_now_ready, 1)

            def u_stats(body, c, b):
                Job(body, "A7", c).wait_drained(dve)
                dve.wait_ge(text_placed, 16 * (b + 1))
                wait(dve, hub_ready, b)
                stats("u", lambda t: h_all[:, b, t, :], P)

            def u_center(b):
                center("u", b, u, h_all[:, b, :, :], P)

            def n_stats(b):
                dve.wait_ge(u_ready, b + 1)
                stats("n", lambda t: u[:, t, :], P)

            def n_center(b):
                center("n", b, n2, u[:, :, :], P)

            def maximum(body, b, s, h):
                j = Job(body, f"s{s}.{h}", b)
                j.wait_filled(dve)
                dve.tensor_reduce(out=negmax[:, s % 2, h:h + 1], in_=j.tile[0:P, 0:NU], axis=AX.X, op=ALU.max,
                                  negate=True).then_inc(negmax_ready, 1)

            def text_sums(body, b, s, heads):
                if s == STEPS - 1 and heads.stop == HQ:
                    dve.wait_ge(drained[SLOTS - 1], uses_before(body, SLOTS - 1, b))
                else:
                    Job(body, f"s{s}.{heads.stop - 1}", b).wait_drained(dve)
                a, z = heads.start, heads.stop
                chain(dve.tensor_reduce(out=s_txt[:, s % 2, a:z], in_=e[:, s % 2, a:z, :, PI:P], axis=AX.XY, op=ALU.add))

            def denominators(s):
                r = s % 2
                chain.sync()
                chain(dve.scalar_tensor_tensor(out=den[:, r, :], in0=s_all[:, r, :], scalar=1.5, in1=s_txt[:, r, :],
                                               op0=ALU.mult, op1=ALU.subtract))

            def reciprocals(s):
                chain.sync()
                chain(dve.reciprocal(rden[:, s % 2, :], den[:, s % 2, :]))

            def scale_values(s):
                g, t, r = s // T, s % T, s % 2
                chain.sync()
                dve.tensor_tensor(vs[:, r, :, :], v[g][:, t, :].rearrange("p (h d) -> p h d", h=HQ),
                                  rden[:, r, :].unsqueeze(2).to_broadcast([P, HQ, DH]), ALU.mult).then_inc(vs_ready, 1)

            def gate_output(b, g):
                dve.wait_ge(av_done, b * STEPS + T * (g + 1))
                dve.scalar_tensor_tensor(out=og[g][:, :], in0=gate[g][:, :], scalar=1.0, in1=o_acc[:, 0:NU],
                                         op0=ALU.add, op1=ALU.mult).then_inc(o_drained, 1)

            def add_residual(body, c, b):
                j = Job(body, "F", c)
                j.wait_filled(dve)
                dve.wait_ge(hub_ready, b + 1)
                wait(dve, base_ready, START + b)
                j.drain(dve.tensor_tensor(h2[:, :, :], j.tile[0:P, 0:T * D].rearrange("p (t d) -> p t d", t=T),
                                          h_all[:, b, :, :], ALU.add))

            def w_stats(body, c):
                Job(body, "F", c).wait_drained(dve)
                stats("w", lambda t: h2[:, t, :], P)

            def w_center(b):
                center("w", b, w, h2[:, :, :], P)

            def own_route(body, c, b):
                j = Job(body, "C2b", c)
                j.wait_filled(dve)
                wait(dve, take_ready, START + b)
                j.drain(dve.tensor_copy(w_tok[:, :], j.tile[0:P, 0:T]))
                j.wait_drained(dve)
                dve.sem_inc(own_route_ready)

            def compare(b, tiles, quads):
                dve.wait_ge(own_route_ready, b + 1)
                wait_placed(dve, quads)
                for t in tiles:
                    dve.tensor_scalar(less[t], route[:, :], w_tok[:, t:t + 1], None, ALU.is_lt).then_inc(less_ready, 1)

            def candidates(body, c, b):
                j = Job(body, "C8", c)
                j.wait_filled(dve)
                j.drain(dve.tensor_scalar(above_cnt[:, :], j.tile[0:P, 0:T], 1.0, None, ALU.add))
                j.wait_drained(dve)
                chain(dve.scalar_tensor_tensor(out=cand[:, :], in0=above_cnt[:, :], scalar=float(SEL), in1=above_cnt[:, :],
                                               op0=ALU.is_le, op1=ALU.mult))
                chain.sync()
                dve.tensor_reduce(out=edge[:, 0:1], in_=cand[:, :], axis=AX.X, op=ALU.max).then_inc(cand_ready, 1)

            def tied_tokens(b):
                dve.wait_ge(edge_ready, b + 1)
                chain(dve.tensor_scalar(above[:, :], above_cnt[:, :], edge[:, 1:2], None, ALU.is_lt))
                chain(dve.tensor_scalar(tied[:, :], above_cnt[:, :], edge[:, 1:2], None, ALU.is_equal))
                chain.sync()
                dve.tensor_reduce(out=tied_sum[:, :], in_=tied[:, :], axis=AX.X, op=ALU.add).then_inc(tied_ready, 1)

            def selection(body, c, b):
                j = Job(body, "C6", c)
                j.wait_filled(dve)
                j.drain(dve.tensor_copy(ties[:, :], j.tile[0:P, 0:2]))
                j.wait_drained(dve)
                chain(dve.tensor_tensor_scan(out=tie_no[:, :], data0=tied[:, :], data1=zeros7[0:P, :],
                                             initial=ties[:, 0:1], op0=ALU.add, op1=ALU.add))
                chain(dve.tensor_scalar(limit[:, 0:1], edge[:, 1:2], -1.0, float(SEL + 1), ALU.mult, ALU.add))
                chain.sync()
                chain(dve.tensor_tensor(limit[:, 1:2], limit[:, 0:1], ties[:, 1:2], ALU.subtract))
                chain(dve.tensor_tensor(tie_no[:, :], tie_no[:, :], tied[:, :], ALU.subtract))
                chain.sync()
                chain(dve.tensor_tensor(limit[:, 2:3], limit[:, 1:2], ties[:, 1:2], ALU.subtract))
                chain.sync()
                for k in range(3):
                    chain(dve.scalar_tensor_tensor(out=take[:, k, :], in0=tie_no[:, :], scalar=limit[:, k:k + 1],
                                                   in1=tied[:, :], op0=ALU.is_lt, op1=ALU.mult))
                chain.sync()
                chain(dve.tensor_tensor(take[:, :, :], take[:, :, :], above[:, :].unsqueeze(1).to_broadcast([P, 3, T]), ALU.add))
                chain.sync()
                dve.tensor_tensor(take[:, :, :], take[:, :, :], w_tok[:, :].unsqueeze(1).to_broadcast([P, 3, T]), ALU.mult)\
                    .then_inc(take_ready, 1)

            def gelu_product(b, g):
                dve.wait_ge(gelu_tanh_ready, 2 * b + g + 1)
                dve.scalar_tensor_tensor(out=hT[g][:, :], in0=hT[g][:, :], scalar=1.0, in1=hz[g][:, :],
                                         op0=ALU.add, op1=ALU.mult).then_inc(gelu_ready, 1)

            def gelu_arg_1(body, c):
                Job(body, "C4", c).wait_drained(dve)
                chain(dve.tensor_tensor(hT[1][:, :], hz[1][:, :], hz[1][:, :], ALU.mult))
                chain.sync()
                chain(dve.tensor_scalar(hT[1][:, :], hT[1][:, :], 0.044715, 1.0, ALU.mult, ALU.add))
                chain.sync()
                dve.wait_ge(gelu_arg_ready, 2 * (B - 1) + 1)
                dve.tensor_tensor(hT[1][:, :], hT[1][:, :], hz[1][:, :], ALU.mult).then_inc(gelu_arg_ready, 1)

            def finish(b):
                dve.wait_ge(take_ready, START + b + 1)
                dve.wait_ge(base_ready, START + b + 1)
                dve.wait_ge(stored, START + 48 * b)
                for k in range(3):
                    chain(dve.tensor_tensor(o_c[k][:, :, :], ys[:, :, :],
                                            take[:, k, :].unsqueeze(2).to_broadcast([P, T, D]), ALU.mult))
                chain.sync()
                for k in range(3):
                    dve.tensor_tensor(o_c[k][:, :, :], o_c[k][:, :, :], base[:, :, :], ALU.add).then_inc(out_ready, 1)

            def ffn_output(body, c, b):
                j = Job(body, "C5", c)
                j.wait_filled(dve)
                wait(dve, out_ready, START + 3 * b)
                j.drain(dve.tensor_tensor(ys[:, :, :], j.tile[0:P, 0:T * D].rearrange("p (t d) -> p t d", t=T),
                                          b2_rep[0:P, :].unsqueeze(1).to_broadcast([P, T, D]), ALU.add))

            def hash_text():
                chain(dve.memset(hashes[:, :, :], 0))
                dve.wait_ge(text_in, 16)
                chain(dve.tensor_copy(tokf[:, :], tok_raw[:, :]))
                chain.sync()
                chain(dve.tensor_scalar(ok[:, :], tokf[:, :], 1.0, None, ALU.is_ge))
                chain(dve.tensor_scalar(ok2[:, :], tokf[:, :], 4.0, None, ALU.is_le))
                chain.sync()
                chain(dve.tensor_tensor(ok[:, :], ok[:, :], ok2[:, :], ALU.mult))
                chain.sync()
                chain(dve.scalar_tensor_tensor(out=safe[:, :], in0=tokf[:, :], scalar=-1.0, in1=ok[:, :],
                                               op0=ALU.add, op1=ALU.mult))
                chain(dve.tensor_tensor_scan(out=good_run[:, :], data0=ok[:, :], data1=ok[:, :], initial=0.0,
                                             op0=ALU.mult, op1=ALU.add))
                chain.sync()
                chain(dve.tensor_copy(hashes[:, 0, 1:LC], safe[:, :]))
                for n in range(1, NG):
                    if n == NG // 2:
                        patch_stats(0, range(T))
                        moments("p", 0, PI)
                    chain.sync()
                    chain(dve.scalar_tensor_tensor(out=hashes[:, n, 1:LC], in0=hashes[:, n - 1, 0:L],
                                                   scalar=float(PRIME), in1=safe[:, :], op0=ALU.mult, op1=ALU.add))
                    if n + 1 in SIZES:
                        chain(dve.tensor_scalar(ids_f[:, n + 1 - SIZES[0], :], good_run[:, :], float(n + 1), float(TBL),
                                                ALU.is_lt, ALU.mult))
                    if n % 2:
                        chain.sync()
                        chain(dve.tensor_scalar(hashes[:, n, 1:LC], hashes[:, n, 1:LC], TBL - 1, None, ALU.bitwise_and))
                chain.sync()
                found = hashes[:, SIZES[0] - 1:NG, 1:LC]
                chain(dve.tensor_scalar(found, found, TBL - 1, None, ALU.bitwise_and))
                chain.sync()
                dve.tensor_tensor(ids_f[:, :, :], ids_f[:, :, :], found, ALU.max).then_inc(ids_f_ready, 1)

            def text_ids():
                j = Job("prologue", "W7", 0)
                j.wait_filled(dve)
                found = j.tile[0:L, 0:NS * B].rearrange("p (n b) -> p n b", n=NS)
                chain(dve.tensor_tensor(ids[:, :, B:B + 1], found[:, :, 0:1], table_start[:, :, 0:1], ALU.add))
                chain.sync()
                j.drain(dve.tensor_tensor(ids[:, :, 0:B], found, table_start[:, :, :], ALU.add))

            def bias_rows():
                dve.wait_ge(token_weights_in, 16 * NTW)
                j = Job("prologue", "W5", 0)
                j.wait_filled(dve)
                j.drain(dve.tensor_tensor(w1[FC:FC + 1, 1, :], j.tile[0:1, 0:D], row[0:1, 0:D], ALU.add))
                j = Job("prologue", "W6", 0)
                j.wait_filled(dve)
                j.drain(dve.tensor_tensor(wp1[D:D + 1, :], j.tile[0:1, 0:D], row[0:1, D:2 * D], ALU.add))

            def prologue():
                hash_text()
                bias_rows()
                text_ids()
                Job("prologue", "W7", 0).wait_drained(dve)
                pick_ids(0)
                embedded_stats("x", "P3", 0)
                embedded_center("x", 0)
                embedded_stats("y", "A5", 0)
                embedded_center("y", 0)
                patch_stats(1, range(T))
                moments("p", 1, PI)
                silu_product(0)
                u_stats("prologue", 0, 0)
                u_center(0)
                n_stats(0)
                n_center(0)
                rests(dve, "q", 0)
                rests(dve, "k", 0)
                pick_ids(1)

            def iteration(body, b, nxt, prev):
                chain.restart()
                for s in range(STEPS):
                    last = s - 1 if s else STEPS - 1 if prev else None
                    for h in range(HQ):
                        at = (s, h)
                        maximum(body, b, s, h)
                        if h == HQ - 1:
                            text_sums(body, b, s, range(0, 2))
                        if last is not None:
                            if h == 0:
                                text_sums(body, b, last, range(2, HQ))
                                denominators(last)
                            if h == 1:
                                reciprocals(last)
                                scale_values(last)
                        if nxt:
                            if at == (0, 1):
                                embedded_stats("x", "A3", b + 1)
                            if at == (0, 3):
                                embedded_center("x", b + 1)
                            if at == (3, 2):
                                embedded_stats("y", "A5", b + 1)
                                embedded_center("y", b + 1)
                            if at == (4, 3):
                                patch_stats(b + 2, range(0, T // 2))
                                patch_stats(b + 2, range(T // 2, T))
                                moments("p", b + 2, PI)
                            if at == (5, 2):
                                silu_product(b + 1)
                            if at == (6, 2):
                                u_stats(body, b, b + 1)
                                u_center(b + 1)
                            if at == (7, 2):
                                n_stats(b + 1)
                            if at == (7, 3):
                                n_center(b + 1)
                            if at == (8, 3):
                                pick_ids(b + 2)
                            if at == (9, 3):
                                rests(dve, "q", 2 * b + 2)
                        if at == (1, 1):
                            rests(dve, "q", 2 * b + 1)
                        if at == (1, 2):
                            rests(dve, "k", 2 * b + 1)
                        if at == (8, 2):
                            gate_output(b, 0)
                        if prev:
                            if at == (1, 0):
                                gate_output(b - 1, 1)
                            if at == (1, 3):
                                add_residual(body, b, b - 1)
                                w_stats(body, b)
                            if at == (2, 2):
                                w_center(b - 1)
                            if at == (4, 2):
                                own_route(body, b, b - 1)
                            if at == (5, 2):
                                compare(b - 1, range(0, 1), 2 * b + 2)
                                compare(b - 1, range(1, 2), 2 * b + 2)
                            if at == (6, 0):
                                compare(b - 1, range(2, 3), 2 * b + 2)
                            if at == (6, 2):
                                compare(b - 1, range(3, 4), 2 * b + 2)
                            if at == (7, 0):
                                compare(b - 1, range(4, 5), 2 * b + 2)
                            if at == (7, 2):
                                compare(b - 1, range(5, 6), 2 * b + 2)
                            if at == (8, 0):
                                compare(b - 1, range(6, 7), 2 * b + 2)
                            if at == (8, 2):
                                gelu_product(b - 1, 0)
                            if at == (8, 3):
                                gelu_product(b - 1, 1)
                            if at == (9, 2):
                                ffn_output(body, b, b - 1)
                            if at == (10, 1):
                                candidates(body, b, b - 1)
                            if at == (12, 3):
                                tied_tokens(b - 1)
                            if at == (13, 0):
                                selection(body, b, b - 1)
                chain.restart()

            def epilogue(body, b):
                text_sums(body, b, STEPS - 1, range(2, HQ))
                denominators(STEPS - 1)
                reciprocals(STEPS - 1)
                scale_values(STEPS - 1)
                gate_output(b, 1)
                add_residual(body, b, b)
                w_stats(body, b)
                w_center(b)
                own_route(body, b, b)
                compare(b, range(T), 2 * b + 2)
                gelu_arg_1(body, b)
                gelu_product(b, 0)
                gelu_product(b, 1)
                candidates(body, b, b)
                ffn_output(body, b, b)
                tied_tokens(b)
                selection(body, b, b)
                finish(b)

            run(dve, iteration, prologue, epilogue)

        @block.tensor
        def _(pe):
            def job(body, name, c):
                j = Job(body, name, c)
                j.wait_free(pe)
                return j

            def transposes(j, src, parts, cols):
                settle(pe)
                for t in range(T):
                    a = tile_col(t, parts)
                    ins = pe.transpose(j.tile[0:cols, a:a + parts], src(t), ident[0:parts, 0:parts])
                j.fill(ins)

            def project(j, rows_, weights, xT):
                for a, z in pieces(NU):
                    ins = pe.matmul(j.tile[0:rows_, a:z], weights, xT[:, a:z], start=True, stop=True)
                j.fill(ins)

            def token_major(j, parts, pairs):
                for t in range(T):
                    for i, (xT, weights) in enumerate(pairs):
                        ins = pe.matmul(j.tile[0:parts, t * D:t * D + D], xT[:, t * parts:(t + 1) * parts], weights,
                                        start=(i == 0), stop=(i == len(pairs) - 1))
                j.fill(ins)

            def beta_products():
                pe.wait_ge(token_weights_in, 16 * NTW)
                j = job("prologue", "W5", 0)
                for k in range(2):
                    ins = pe.matmul(j.tile[0:1, 0:D], ln1_gb[:, k, 1:2], w1_raw[:, k, :], start=(k == 0), stop=(k == 1))
                j.fill(ins)
                j = job("prologue", "W6", 0)
                j.fill(pe.matmul(j.tile[0:1, 0:D], col[0:D, 1:2], wp1_raw[:, :], start=True, stop=True))

            def id_transposes():
                pe.wait_ge(ids_f_ready, 1)
                j = job("prologue", "W7", 0)
                for n in range(NS):
                    ins = pe.transpose(j.tile[0:L, n * B:(n + 1) * B], ids_f[:, n, :], ident[0:B, 0:B])
                j.fill(ins)

            def qkv_gate_transposes():
                pe.wait_ge(weights_in, 16 * NW)
                j = job("prologue", "W1", 0)
                for k in range(6):
                    ins = pe.transpose(j.tile[0:D, k * 128:(k + 1) * 128], raw_qkv[:, k, :], ident[:, :])
                j.fill(ins)
                j = job("prologue", "W2", 0)
                for k in range(2):
                    ins = pe.transpose(j.tile[0:D, k * 128:(k + 1) * 128], raw_gate[:, k, :], ident[:, :])
                j.fill(ins)

            def final_transposes_and_betas():
                j = job("prologue", "W3", 0)
                for k in range(2):
                    ins = pe.transpose(j.tile[:, k * D:(k + 1) * D], raw_final[:, k * 128:(k + 1) * 128], ident[0:D, 0:D])
                j.fill(ins)
                Job("prologue", "W1", 0).wait_drained(pe)
                j = job("prologue", "W4", 0)
                for a, z in pieces(3 * INNER):
                    ins = pe.matmul(j.tile[0:1, a:z], col[0:D, 5:6], qkv_t[:, a:z], start=True, stop=True)
                j.fill(ins)

            def patch_transposes(body, names, c, b):
                pe.wait_ge(patches_normed, b + 1)
                for name in names:
                    k = int(name[1]) - 1
                    transposes(job(body, name, c), lambda t: pn[:, t, k * FC:(k + 1) * FC], PI, FC)

            def embed(body, names, c):
                Job(body, names[0], c).wait_drained(pe)
                token_major(job(body, names[1], c), PI, [(pnT[0:FC, 0, :], w1[0:FC, 0, :]), (pnT[:, 1, :], w1[:, 1, :])])

            def x2_transposes(body, c, b):
                pe.wait_ge(x_normed, b + 1)
                transposes(job(body, "A4", c), lambda t: x2[0:PI, t, :], PI, D)

            def pool_in(body, c):
                Job(body, "A4", c).wait_drained(pe)
                token_major(job(body, "A5", c), PI, [(x2T[:, :], wp1[:, :])])

            def y2_transposes(body, c, b):
                pe.wait_ge(y_normed, b + 1)
                transposes(job(body, "A6", c), lambda t: y2[0:PI, t, :], PI, D)

            def pool_out(body, c, b):
                pe.wait_ge(silu_ready, b + 1)
                token_major(job(body, "A7", c), PI, [(x3T[:, :], wp2[:, :])])

            def u_transposes(body, c, b):
                pe.wait_ge(u_ready, b + 1)
                transposes(job(body, "A8", c), lambda t: u[:, t, :], P, D)

            def n_transposes(body, c, b):
                pe.wait_ge(n_ready, b + 1)
                transposes(job(body, "A9", c), lambda t: n2[:, t, :], P, D)

            def query_key(body, c, k, g):
                if g == 0:
                    Job(body, "A9", c).wait_drained(pe)
                a = "qk".index(k) * INNER + g * 128
                project(job(body, f"{k}{g}", c), 128, wqkv[:, a:a + 128], nT)

            def values(body, c, g):
                j = job(body, f"v{g}", c)
                a = 2 * INNER + g * 128
                for t in range(T):
                    ins = pe.matmul(j.tile[0:P, t * 128:(t + 1) * 128], nT[:, t * P:(t + 1) * P], wqkv[:, a:a + 128],
                                    start=True, stop=True)
                j.fill(ins)

            def gates(body, c, g):
                project(job(body, f"g{g}", c), 128, wgate[:, g * 128:(g + 1) * 128], uT)

            def scores(body, b, s, h):
                g, t = s // T, s % T
                if t == 0:
                    pe.wait_ge(placed[h], PLACED * (2 * b + g + 1))
                j = job(body, f"s{s}.{h}", b)
                for r in range(2):
                    for a, z in pieces(NU):
                        ins = pe.matmul(j.tile[0:P, a:z], qs[g][:, h, r, t * P:(t + 1) * P], ks[g][:, h, r, a:z],
                                        start=(r == 0), stop=(r == 1))
                j.fill(ins)

            def attend(b, s):
                t, r = s % T, s % 2
                pe.wait_ge(vs_ready, b * STEPS + s + 1)
                if t == 0:
                    wait(pe, o_drained, 2 * b + s // T)
                for a, z in pieces(NU):
                    for h in range(HQ):
                        ins = pe.matmul(o_acc[DH * h:DH * h + DH, a:z], vs[:, r, h, :],
                                        e[:, r, h, :, :].rearrange("p t q -> p (t q)")[:, a:z],
                                        start=(t == 0), stop=(t == T - 1))
                ins.then_inc(av_done, 1)

            def output_projection(body, c, b):
                pe.wait_ge(o_drained, 2 * (b + 1))
                token_major(job(body, "F", c), P, [(og[g][:, :], wfinal[:, g, :]) for g in range(2)])

            def w_transposes(body, c, b):
                pe.wait_ge(w_ready, b + 1)
                transposes(job(body, "C1", c), lambda t: w[:, t, :], P, D)

            def routing(body, c):
                Job(body, "C1", c).wait_drained(pe)
                project(job(body, "C2", c), P, wroute[:, :], wT)

            def hidden(body, c, g):
                project(job(body, f"C{3 + g}", c), 128, wh[:, g * 128:(g + 1) * 128], wT)

            def route_transposes(body, c):
                Job(body, "C2", c).wait_drained(pe)
                j = job(body, "C2b", c)
                settle(pe)
                for t in range(T):
                    ins = pe.transpose(j.tile[0:P, t:t + 1], route[0:1, t * P:(t + 1) * P], ident[0:1, 0:1])
                j.fill(ins)

            def count_heavier(body, c, b):
                pe.wait_ge(less_ready, T * (b + 1))
                j = job(body, "C7", c)
                for a, z in pieces(NU):
                    for t in range(T):
                        ins = pe.matmul(j.tile[0:1, a:z], copies[0:P, :], less[t][:, a:z], start=(t == 0), stop=(t == T - 1))
                j.fill(ins)

            def count_transposes(body, c):
                Job(body, "C7", c).wait_drained(pe)
                j = job(body, "C8", c)
                settle(pe)
                for t in range(T):
                    ins = pe.transpose(j.tile[0:P, t:t + 1], route[0:1, t * P:(t + 1) * P], ident[0:1, 0:1])
                j.fill(ins)

            def ffn_out(body, c, b):
                pe.wait_ge(gelu_ready, 2 * (b + 1))
                token_major(job(body, "C5", c), P, [(hT[g][:, :], wy[:, g, :]) for g in range(2)])

            def count_ties(body, c, b):
                pe.wait_ge(tied_ready, b + 1)
                j = job(body, "C6", c)
                pe.matmul(j.tile[0:P, 0:1], before[0:P, :], tied_sum[:, :], start=True, stop=True)
                j.fill(pe.matmul(j.tile[0:P, 1:2], images[0:P, :], tied_sum[:, :], start=True, stop=True))

            def prologue():
                pe.wait_ge(consts_ready, 1)
                pe.wait_ge(rows_ready, 1)
                beta_products()
                patch_transposes("prologue", ("P1", "P2"), 0, 0)
                id_transposes()
                for name in ("W5", "W6"):
                    Job("prologue", name, 0).wait_drained(pe)
                embed("prologue", ("P2", "P3"), 0)
                x2_transposes("prologue", 0, 0)
                qkv_gate_transposes()
                pool_in("prologue", 0)
                final_transposes_and_betas()
                y2_transposes("prologue", 0, 0)
                pool_out("prologue", 0, 0)
                patch_transposes("prologue", ("A1", "A2"), 0, 1)
                u_transposes("prologue", 0, 0)
                n_transposes("prologue", 0, 0)
                Job("prologue", "W4", 0).wait_drained(pe)
                query_key("prologue", 0, "q", 0)
                query_key("prologue", 0, "k", 0)
                values("prologue", 0, 0)
                embed("prologue", ("A2", "A3"), 0)

            def iteration(body, b, nxt, prev):
                for s in range(STEPS):
                    for h in range(HQ):
                        at = (s, h)
                        scores(body, b, s, h)
                        if prev:
                            if at == (1, 2):
                                output_projection(body, b, b - 1)
                            if at == (3, 2):
                                w_transposes(body, b, b - 1)
                            if at == (4, 0):
                                routing(body, b)
                            if at == (4, 2):
                                hidden(body, b, 0)
                            if at == (4, 3):
                                route_transposes(body, b)
                            if at == (5, 2):
                                hidden(body, b, 1)
                            if at == (8, 2):
                                count_heavier(body, b, b - 1)
                            if at == (9, 2):
                                ffn_out(body, b, b - 1)
                            if at == (10, 0):
                                count_transposes(body, b)
                            if at == (13, 0):
                                count_ties(body, b, b - 1)
                        if at == (0, 2):
                            query_key(body, b, "q", 1)
                        if at == (1, 0):
                            query_key(body, b, "k", 1)
                        if at == (6, 2):
                            gates(body, b, 0)
                        if at == (7, 0):
                            gates(body, b, 1)
                        if at == (7, 2):
                            values(body, b, 1)
                        if nxt:
                            if at == (2, 0):
                                x2_transposes(body, b, b + 1)
                            if at == (3, 1):
                                pool_in(body, b)
                            if at == (4, 3):
                                y2_transposes(body, b, b + 1)
                            if at == (6, 0):
                                pool_out(body, b, b + 1)
                            if at == (8, 0):
                                u_transposes(body, b, b + 1)
                            if at == (8, 2):
                                n_transposes(body, b, b + 1)
                            if at == (9, 0):
                                query_key(body, b, "q", 0)
                            if at == (9, 2):
                                query_key(body, b, "k", 0)
                            if at == (11, 0):
                                values(body, b, 0)
                            if at == (11, 2):
                                patch_transposes(body, ("A1",), b, b + 2)
                            if at == (12, 0):
                                patch_transposes(body, ("A2",), b, b + 2)
                            if at == (13, 1):
                                embed(body, ("A2", "A3"), b)
                    if s:
                        attend(b, s - 1)
                    elif prev:
                        attend(b - 1, STEPS - 1)

            def epilogue(body, b):
                attend(b, STEPS - 1)
                output_projection(body, b, b)
                w_transposes(body, b, b)
                routing(body, b)
                hidden(body, b, 0)
                hidden(body, b, 1)
                route_transposes(body, b)
                count_heavier(body, b, b)
                count_transposes(body, b)
                ffn_out(body, b, b)
                count_ties(body, b, b)

            run(pe, iteration, prologue, epilogue)


PARAMETERS = [
    "L0_tok_ln1_g", "L0_tok_ln1_b", "L0_tok_W1", "L0_tok_b1", "L0_tok_ln2_g", "L0_tok_ln2_b", "L0_tok_Wp1",
    "L0_tok_bp1", "L0_tok_lnp_g", "L0_tok_lnp_b", "L0_tok_Wp2", "L0_tok_bp2", "L0_txt_tables", "L0_attn_ln_gamma",
    "L0_attn_ln_beta", "L0_attn_W_qkv", "L0_attn_W_gate", "L0_attn_b_gate", "L0_attn_W_final", "L0_attn_b_final",
    "L0_ffn_wr", "L0_ffn_br", "L0_ffn_w1", "L0_ffn_b1", "L0_ffn_w2", "L0_ffn_b2",
]


def kernel(**inputs):
    import concourse.bacc as bacc
    from concourse.bass_utils import run_bass_kernel_spmd

    nc = bacc.Bacc("TRN2", target_bir_lowering=False, num_devices=1)
    arrays, args = {}, {}
    for name in ["x", "x_txt", *PARAMETERS]:
        a = np.ascontiguousarray(inputs[name])
        arrays[f"in_{name}"] = a
        args[name] = nc.dram_tensor(f"in_{name}", a.shape, mybir.dt.from_np(a.dtype), kind="ExternalInput").ap()
    out = nc.dram_tensor("out", (B, SEQ, D), F32, kind="ExternalOutput").ap()
    build(nc, args["x"], args["x_txt"], args, out)
    result = run_bass_kernel_spmd(nc, [arrays], core_ids=[0])
    return result.results[0]["out"]
```
